# Optimizing a Trainium2 kernel written in Bass

```python
import numpy as np
import jax
import jax.numpy as jnp

def _softmax(x, axis=-1):
    return jax.nn.softmax(x, axis=axis)

def _gelu(x):
    return jax.nn.gelu(x, approximate=True)

def _silu(x):
    return jax.nn.silu(x)

def _sigmoid(x):
    return jax.nn.sigmoid(x)

def _layernorm(x, axis=-1, eps=1e-05):
    m = jnp.mean(x, axis=axis, keepdims=True)
    v = jnp.var(x, axis=axis, keepdims=True)
    return (x - m) / jnp.sqrt(v + eps)

def _scatter_add(tgt, idx, src, axis=0):
    return tgt.at[idx].add(src)

def _segment_sum(src, seg, n):
    return jax.ops.segment_sum(src, seg, n)
kernel_name = 'mk_seq_postln_d1_jaxref_r4_2c2746'

def setup_inputs(seed: int=0):
    np.random.seed(seed)
    _w = jnp.asarray

    def _L0_attn_setup():
        import jax, jax.numpy as jnp
        import numpy as np
        D_MODEL = 256
        NUM_HEADS = 16
        HEAD_DIM = D_MODEL // NUM_HEADS
        key = jax.random.key(seed)
        ks = jax.random.split(key, 5)
        B, S = (4, 512)
        x = jax.random.normal(ks[0], (B, S, D_MODEL), dtype=jnp.float32)
        scale = 1.0 / np.sqrt(D_MODEL)
        qkv_w = jax.random.normal(ks[1], (3 * D_MODEL, D_MODEL), dtype=jnp.float32) * scale
        qkv_b = jnp.zeros((3 * D_MODEL,), dtype=jnp.float32)
        out_w = jax.random.normal(ks[2], (D_MODEL, D_MODEL), dtype=jnp.float32) * scale
        out_b = jnp.zeros((D_MODEL,), dtype=jnp.float32)
        return {'x': x, 'qkv_w': qkv_w, 'qkv_b': qkv_b, 'out_w': out_w, 'out_b': out_b}
    _L0_attn_in = _L0_attn_setup()

    def _L0_ffn_setup():
        import jax, jax.numpy as jnp
        import numpy as np
        B, S, H = (2, 1024, 256)
        E, K, I = (8, 2, 352)
        key = jax.random.key(seed)
        ks = jax.random.split(key, 9)
        sc = 0.02
        return {'hidden_states': jax.random.normal(ks[0], (B, S, H), jnp.float32), 'gate_w': jax.random.normal(ks[1], (E, H), jnp.float32) * sc, 'w_gate': jax.random.normal(ks[2], (E, H, I), jnp.float32) * sc, 'w_up': jax.random.normal(ks[3], (E, H, I), jnp.float32) * sc, 'w_down': jax.random.normal(ks[4], (E, I, H), jnp.float32) * sc, 'sw_gate': jax.random.normal(ks[5], (H, I), jnp.float32) * sc, 'sw_up': jax.random.normal(ks[6], (H, I), jnp.float32) * sc, 'sw_down': jax.random.normal(ks[7], (I, H), jnp.float32) * sc, 'shared_gate_w': jax.random.normal(ks[8], (1, H), jnp.float32) * sc}
    _L0_ffn_in = _L0_ffn_setup()
    _d = {'L0_attn_x': _L0_attn_in['x'], 'L0_attn_qkv_w': _L0_attn_in['qkv_w'], 'L0_attn_qkv_b': _L0_attn_in['qkv_b'], 'L0_attn_out_w': _L0_attn_in['out_w'], 'L0_attn_out_b': _L0_attn_in['out_b'], 'L0_ffn_gate_w': _L0_ffn_in['gate_w'], 'L0_ffn_w_gate': _L0_ffn_in['w_gate'], 'L0_ffn_w_up': _L0_ffn_in['w_up'], 'L0_ffn_w_down': _L0_ffn_in['w_down'], 'L0_ffn_sw_gate': _L0_ffn_in['sw_gate'], 'L0_ffn_sw_up': _L0_ffn_in['sw_up'], 'L0_ffn_sw_down': _L0_ffn_in['sw_down'], 'L0_ffn_shared_gate_w': _L0_ffn_in['shared_gate_w']}
    _x0 = _d['L0_attn_x']
    _d['L0_attn_x'] = jax.random.normal(jax.random.fold_in(jax.random.key(seed), 1), (8, 1024, 256), dtype=_x0.dtype)
    del _x0
    return _d

def reference(L0_attn_x, L0_attn_qkv_w, L0_attn_qkv_b, L0_attn_out_w, L0_attn_out_b, L0_ffn_gate_w, L0_ffn_w_gate, L0_ffn_w_up, L0_ffn_w_down, L0_ffn_sw_gate, L0_ffn_sw_up, L0_ffn_sw_down, L0_ffn_shared_gate_w):

    def _L0_attn_ref(x, qkv_w, qkv_b, out_w, out_b):
        import jax, jax.numpy as jnp
        import numpy as np
        D_MODEL = 256
        NUM_HEADS = 16
        HEAD_DIM = D_MODEL // NUM_HEADS
        B, S, _ = x.shape
        qkv = x @ qkv_w.T + qkv_b
        q, k, v = jnp.split(qkv, 3, axis=-1)
        q = q.reshape(B, S, NUM_HEADS, HEAD_DIM).transpose(0, 2, 1, 3)
        k = k.reshape(B, S, NUM_HEADS, HEAD_DIM).transpose(0, 2, 1, 3)
        v = v.reshape(B, S, NUM_HEADS, HEAD_DIM).transpose(0, 2, 1, 3)
        scores = jnp.einsum('bhqd,bhkd->bhqk', q, k) / np.sqrt(HEAD_DIM).astype(np.float32)
        attn = jax.nn.softmax(scores, axis=-1)
        context = jnp.einsum('bhqk,bhkd->bhqd', attn, v)
        context = context.transpose(0, 2, 1, 3).reshape(B, S, D_MODEL)
        return context @ out_w.T + out_b

    def _L0_ffn_ref(hidden_states, gate_w, w_gate, w_up, w_down, sw_gate, sw_up, sw_down, shared_gate_w):
        import jax, jax.numpy as jnp
        import numpy as np
        B, S, H = (2, 1024, 256)
        E, K, I = (8, 2, 352)
        b, s, h = hidden_states.shape
        x = hidden_states.reshape(-1, h)
        logits = jnp.einsum('th,eh->te', x, gate_w)
        probs = jax.nn.softmax(logits.astype(jnp.float32), axis=-1)
        topk_w, topk_i = jax.lax.top_k(probs, K)
        topk_w = topk_w / jnp.sum(topk_w, axis=-1, keepdims=True)
        combine = jnp.sum(jax.nn.one_hot(topk_i, E, dtype=topk_w.dtype) * topk_w[..., None], axis=1)
        combine = combine.astype(x.dtype)
        g = jnp.einsum('th,ehi->eti', x, w_gate)
        u = jnp.einsum('th,ehi->eti', x, w_up)
        eo = jnp.einsum('eti,eih->eth', jax.nn.silu(g) * u, w_down)
        out = jnp.einsum('te,eth->th', combine, eo)
        sg = jax.nn.sigmoid(jnp.einsum('th,oh->to', x, shared_gate_w))
        so = jax.nn.silu(x @ sw_gate) * (x @ sw_up) @ sw_down
        out = out + sg * so
        return out.reshape(b, s, h)
    x = L0_attn_x
    x = _layernorm(x + _L0_attn_ref(x, L0_attn_qkv_w, L0_attn_qkv_b, L0_attn_out_w, L0_attn_out_b), axis=-1)
    x = _layernorm(x + _L0_ffn_ref(x, L0_ffn_gate_w, L0_ffn_w_gate, L0_ffn_w_up, L0_ffn_w_down, L0_ffn_sw_gate, L0_ffn_sw_up, L0_ffn_sw_down, L0_ffn_shared_gate_w), axis=-1)
    return x

_drawn_inputs = setup_inputs


def setup_inputs(seed=0):
    import zlib

    import numpy as np

    out = dict(_drawn_inputs(seed))
    spreads = {'L0_attn_qkv_b': (0.0, 0.1), 'L0_attn_out_b': (0.0, 0.1)}
    factors = {'L0_ffn_gate_w': 4.616,
     'L0_ffn_w_gate': 4.053,
     'L0_ffn_w_up': 4.014,
     'L0_ffn_w_down': 4.003,
     'L0_ffn_sw_gate': 5.509,
     'L0_ffn_sw_up': 5.466,
     'L0_ffn_sw_down': 5.456,
     'L0_ffn_shared_gate_w': 8.0}
    for name, (base, spread) in spreads.items():
        noise = np.random.default_rng([zlib.crc32(name.encode()), seed]).standard_normal(out[name].shape)
        drawn = base * np.exp(spread * noise) if base else spread * noise
        out[name] = jnp.asarray(drawn.astype(out[name].dtype))
    for name, factor in factors.items():
        out[name] = (out[name] * factor).astype(out[name].dtype)
    return out
```

```python
from contextlib import ExitStack

import concourse.bass as bass
from concourse import mybir

F32 = mybir.dt.float32
BF16 = mybir.dt.bfloat16
ALU = mybir.AluOpType
ACT = mybir.ActivationFunctionType
AX = mybir.AxisListType

P = 128
NH = 16
HD = 16
MM_N = 512
VW = 32

Q_PART = (0, 0, 0, 1, 1, 2)
K_PART = (0, 1, 2, 0, 1, 0)
KS = len(Q_PART) * HD
MROWS = 3


def hold(eng, passed, s, value):
    eng.wait_ge(s, value)
    eng.sem_inc(passed, 1)


def attention(nc, xT, wqkT, wvT, qk_b, v_b, ctx_out, qk_parts, blank, sem):
    B, D, S = xT.shape
    DK = D // P
    NT = S // P
    NHALF = S // MM_N
    NQK = 2 * D // P
    HT = P // HD
    RING = 8
    QC = S // 4
    SCALE = 1.0 / HD ** 0.5
    PAIRS = NH // 2
    NCH = NT + NQK * NHALF
    TILES = (0, 2, 1, 3)

    with ExitStack() as ctx:
        def sb(name, shape, dt=F32):
            return ctx.enter_context(nc.sbuf_tensor(name, shape, dt))

        def pb(name, shape, dt=F32):
            return ctx.enter_context(nc.psum_tensor(name, shape, dt))

        q_aug = sb("q_aug", [P, NH, S], BF16)
        k_aug = sb("k_aug", [P, NH, S], BF16)
        probs = sb("probs", [P, RING, S])
        qk_sb = sb("qk_sb", [P, NQK, S])
        parts = sb("parts", [P, 2, 3, S], BF16)
        x_v = sb("x_v", [P, DK, S])
        x_qk = sb("x_qk", [P, DK, S])
        wqk_sb = sb("wqk_sb", [P, DK, 2 * D])
        wv_sb = sb("wv_sb", [P, DK, D])
        qkb_sb = sb("qkb_sb", [P, NQK])
        vb_sb = sb("vb_sb", [P, D])
        v_sb = sb("v_sb", [P, NT, D])
        v_st = sb("v_st", [P, 2, NT, VW])
        ctx_sb = sb("ctx_sb", [P, NT, D])
        o_sb = sb("o_sb", [P, 2, QC])
        rden = sb("rden", [P, 2, 2, 4, 1])
        rmax = sb("rmax", [P, 2, NT])
        rres = sb("rres", [P, 2, NT])
        mparts = sb("mparts", [P, 2, MROWS, NT], BF16)
        m_rows = sb("m_rows", [MROWS * NT, 2, P], BF16)
        zeros = sb("zeros", [P, D])
        identf = sb("identf", [P, P])
        identb = sb("identb", [P, P], BF16)

        ps_rows = [pb(f"ps_rows{i}", [P, S]) for i in range(2)]
        ps_cols = [pb(f"ps_cols{i}", [P, MM_N]) for i in range(2)]
        ps_o = pb("ps_o", [P, QC])
        ps_misc = pb("ps_misc", [P, MM_N])
        ps_m = ps_misc[0:MROWS * NT, 256:256 + P // 2].bitcast(BF16)
        ps_ot = ps_misc[:, 0:256].rearrange("p (j n) -> p j n", j=2)

        w_in = sem("w_in")
        xv_in = sem("xv_in")
        xq_in = sem("xq_in")
        const = sem("const")
        chunk_done = sem("chunk_done")
        v_ev = sem("v_ev")
        qk_ev = sem("qk_ev")
        split_step = sem("split_step")
        parts_out = [sem(f"parts_out{i}") for i in range(2)]
        aug_in = [sem(f"aug_in{i}") for i in range(2)]
        rows_done = sem("rows_done")
        rows_free = sem("rows_free")
        cols_done = sem("cols_done")
        exp_done = sem("exp_done")
        pv_done = sem("pv_done")
        v_staged = sem("v_staged")
        o_ev = sem("o_ev")
        ot_done = sem("ot_done")
        norm_done = sem("norm_done")
        norm_step = sem("norm_step")
        dve_step = sem("dve_step")
        m_split = sem("m_split")
        mt_done = sem("mt_done")
        m_ev = sem("m_ev")
        m_in = [sem(f"m_in{i}") for i in range(2)]
        passed = sem("passed")
        ctx_st = sem("ctx_st")
        blanked = sem("blanked")

        half = [slice(0, NH // 2), slice(NH // 2, NH)]

        def split(ns, eng, nb, i, step):
            t = TILES[i]
            src = qk_sb[:, t, :]
            pt = parts[:, i % 2, :, :]
            zero = zeros[:, 0:1].broadcast_to([P, S])
            if step == 0:
                eng.wait_ge(qk_ev, nb * NQK * NHALF + 2 * t + 2)
                if i >= 2:
                    eng.wait_ge(parts_out[i % 2], nb * 32 + 16)
                else:
                    eng.wait_ge(parts_out[i % 2], nb * 32)
            for c in (0, 1) if step == 0 else (2, 3):
                if not (step == 0 and c == 0):
                    eng.wait_ge(split_step, nb * 16 + 4 * i + c)
                if c == 0:
                    op = ns.tensor_tensor(pt[:, 0, :], src, zero, ALU.add)
                elif c == 1:
                    op = ns.tensor_tensor(src, src, pt[:, 0, :], ALU.subtract)
                elif c == 2:
                    op = ns.tensor_tensor(pt[:, 1, :], src, zero, ALU.add)
                else:
                    op = ns.tensor_tensor(pt[:, 2, :], src, pt[:, 1, :], ALU.subtract)
                op.then_inc(split_step, 1)

        block = ctx.enter_context(nc.Block())

        @block.sync
        def _(sp):
            sp.dma_start(wqk_sb[:, :, :], wqkT.rearrange("(c p) n -> p c n", p=P)).then_inc(w_in, 16)
            sp.dma_start(x_qk[:, :, :], xT[0].rearrange("(c p) n -> p c n", p=P)).then_inc(xq_in, 16)
            sp.dma_start(qkb_sb[:, :], qk_b).then_inc(w_in, 16)
            sp.dma_start(wv_sb[:, :, :], wvT.rearrange("(c p) n -> p c n", p=P)).then_inc(w_in, 16)
            sp.dma_start(vb_sb[:, :], v_b.partition_broadcast(P)).then_inc(w_in, 16)
            sp.dma_start(x_v[:, :, :], xT[0].rearrange("(c p) n -> p c n", p=P)).then_inc(xv_in, 16)

            def store_parts(nb, i):
                t = TILES[i]
                side, hf = t // 2, t % 2
                hold(sp, passed, split_step, nb * 16 + 4 * i + 4)
                hold(sp, passed, aug_in[hf], nb * 192)
                dst = qk_parts[side, :, hf * P:(hf + 1) * P, :].rearrange("c p s -> p c s")
                sp.dma_start(dst, parts[:, i % 2, :, :]).then_inc(parts_out[i % 2], 16)

            def load_aug(nb, hf, first=False):
                for i in (2 * hf, 2 * hf + 1):
                    hold(sp, passed, parts_out[i % 2], nb * 32 + 16 * (i // 2) + 16)
                if not first:
                    sp.wait_ge(cols_done, (nb - 1) * 256 + (hf + 1) * 128)
                for side, (aug, part) in enumerate(((q_aug, Q_PART), (k_aug, K_PART))):
                    for j, c in enumerate(part):
                        src = qk_parts[side, c, hf * P:(hf + 1) * P, :].rearrange("(h d) s -> d h s", d=HD)
                        sp.dma_start(aug[HD * j:HD * j + HD, half[hf], :], src).then_inc(aug_in[hf], 16)

            sp.wait_ge(chunk_done, NQK * NHALF)
            sp.dma_start(x_qk[:, :, :], xT[1].rearrange("(c p) n -> p c n", p=P)).then_inc(xq_in, 16)
            for i in range(NQK):
                store_parts(0, i)
                if i % 2:
                    load_aug(0, i // 2, True)

            def batch(b, prep, xq):
                def rows(h, k):
                    sp.wait_ge(m_ev, b * NH + h + 1)
                    for r in range(MROWS):
                        sp.dma_start(q_aug[KS + r:KS + r + 1, bass.ds(h, 1), :].rearrange("r h s -> r (h s)"),
                                     m_rows[NT * r:NT * (r + 1), k, :]).then_inc(m_in[k], 16)

                rows(0, 0)
                if prep:
                    sp.wait_ge(chunk_done, b * NCH + NCH + NCH - NT)
                    sp.dma_start(x_v[:, :, :], xT[b + 1].rearrange("(c p) n -> p c n", p=P)).then_inc(xv_in, 16)
                if xq:
                    sp.dma_start(x_qk[:, :, :], xT[b + 2].rearrange("(c p) n -> p c n", p=P)).then_inc(xq_in, 16)
                for h in range(NH - 1):
                    rows(h + 1, (h + 1) % 2)
                    if prep and h in (2, 4, 6, 8):
                        store_parts(b + 1, h // 2 - 1)
                    if prep and h == 9:
                        load_aug(b + 1, 0)
                sp.wait_ge(norm_done, b * NH + NH + 2)
                sp.dma_start(ctx_out[b].rearrange("(t p) d -> p t d", p=P), ctx_sb[:, :, :]).then_inc(ctx_st, 16)
                if prep:
                    load_aug(b + 1, 1)
                rows_b = blank.shape[0] // B
                sp.dma_start(blank[bass.ds(b * rows_b, rows_b), :].rearrange("(p r) d -> p r d", p=P),
                             zeros[:, :].rearrange("p (o d) -> p o d", o=1).broadcast_to([P, rows_b // P, D])
                             ).then_inc(blanked, 16)

            with sp.Fori(0, B - 2) as b:
                batch(b, True, True)
            batch(B - 2, True, False)
            batch(B - 1, False, False)
            sp.wait_ge(ctx_st, 16 * B + 16)
            sp.wait_ge(blanked, 16 * B)

        @block.gpsimd
        def _(pool):
            for m in (identf, identb, zeros):
                nc.gpsimd.memset(m[:, :], 0.0).then_inc(const, 1)
            nc.gpsimd.memset(v_st[:, :, :, HD + 1:VW], 0.0).then_inc(const, 1)
            nc.gpsimd.memset(v_st[:, :, :, HD:HD + 1], 1.0).then_inc(const, 1)
            pool.wait_ge(const, 5)
            nc.gpsimd.memset(k_aug[KS:KS + MROWS, :, :], -1.0).then_inc(const, 1)
            pool.wait_ge(const, 6)
            for m in (identf, identb):
                nc.gpsimd.affine_select(out=m[:, :], in_=m[:, :], compare_op=ALU.not_equal, fill=1.0,
                                        base=0, pattern=[[-1, P]], channel_multiplier=1).then_inc(const, 1)

            pool.sem_inc(v_staged, 1)

            def stage_v(b, h, k):
                n = b * NH + h
                pool.wait_ge(pv_done, 8 * n + 1)
                nc.gpsimd.tensor_tensor(v_st[:, k, :, 0:HD], v_sb[:, :, h * HD:(h + 1) * HD],
                                        zeros[:, 0:NT * HD].rearrange("p (t d) -> p t d", d=HD),
                                        ALU.add).then_inc(v_staged, 1)

            def batch(b, prep):
                pool.wait_ge(v_ev, NT * b + NT)
                stage_v(b, 0, 0)
                if prep:
                    for i in range(NQK):
                        stage_v(b, 2 * i + 1, 1)
                        split(nc.gpsimd, pool, b + 1, i, 0)
                        stage_v(b, 2 * i + 2, 0)
                        split(nc.gpsimd, pool, b + 1, i, 1)
                for h in range(9 if prep else 1, NH):
                    stage_v(b, h, h % 2)

            with pool.Fori(0, B - 1) as b:
                batch(b, True)
            batch(B - 1, False)

        @block.scalar
        def _(act):
            def evac_qk(nb, c):
                t, j = c // NHALF, c % NHALF
                act.wait_ge(chunk_done, nb * NCH + c + 1)
                if c == 0:
                    act.wait_ge(split_step, nb * 16)
                nc.scalar.activation(qk_sb[:, t, j * MM_N:(j + 1) * MM_N], ps_cols[c % 2][:, :], ACT.Identity,
                                     bias=qkb_sb[:, t:t + 1]).then_inc(qk_ev, 1)

            def evac_o(b, h, k):
                n = b * NH + h
                act.wait_ge(pv_done, RING + 8 * n + 8)
                act.wait_ge(ot_done, n + 1)
                nc.scalar.activation(o_sb[:, k, :], ps_o[:, :], ACT.Copy).then_inc(o_ev, 1)

            def exps(b, h, k, first=False):
                for kt in range(NT):
                    n = (b * NH + h) * NT + kt
                    act.wait_ge(pv_done, n + 1)
                    for j in range(NHALF):
                        act.wait_ge(cols_done, 2 * n + j + 1)
                        nc.scalar.activation(probs[:, kt, j * MM_N:(j + 1) * MM_N], ps_cols[j][:, :],
                                             ACT.Exp, scale=SCALE).then_inc(exp_done, 1)
                    if kt == 0 and not first:
                        evac_o(b, h - 1, 1 - k)

            def batch(b, prep):
                if prep:
                    for c in range(NQK * NHALF):
                        evac_qk(b + 1, c)
                exps(b, 0, 0, True)
                exps(b, 1, 1)
                with act.Fori(1, PAIRS) as p:
                    exps(b, 2 * p, 0)
                    exps(b, 2 * p + 1, 1)
                evac_o(b, NH - 1, 1)

            act.wait_ge(w_in, 64)
            for c in range(NQK * NHALF):
                evac_qk(0, c)
            act.sem_inc(exp_done, 2)
            act.sem_inc(o_ev, 1)
            with act.Fori(0, B - 1) as b:
                batch(b, True)
            batch(B - 1, False)

        @block.vector
        def _(dve):
            dve.sem_inc(rows_free, 2)
            dve.sem_inc(norm_done, 2)
            dve.wait_ge(const, 8)
            for i in range(NQK):
                split(nc.vector, dve, 0, i, 0)
                split(nc.vector, dve, 0, i, 1)

            def row_max(b, h, k, qt):
                n = (b * NH + h) * NT + qt
                dve.wait_ge(rows_done, n + 1)
                nc.vector.tensor_reduce(rmax[:, k, qt:qt + 1], ps_rows[qt % 2][:, :], AX.X,
                                        ALU.max).then_inc(rows_free, 1)

            def split_max(b, h, k):
                n = b * NH + h
                dve.wait_ge(rows_free, 2 + 8 * n + 8)
                nc.vector.tensor_copy(mparts[:, k, 0, :], rmax[:, k, :]).then_inc(dve_step, 1)
                dve.wait_ge(dve_step, 3 * n + 1)
                nc.vector.tensor_tensor(rres[:, k, :], rmax[:, k, :], mparts[:, k, 0, :],
                                        ALU.subtract).then_inc(dve_step, 1)
                dve.wait_ge(dve_step, 3 * n + 2)
                nc.vector.tensor_copy(mparts[:, k, 1, :], rres[:, k, :]).then_inc(dve_step, 1)
                dve.wait_ge(dve_step, 3 * n + 3)
                nc.vector.tensor_tensor(mparts[:, k, 2, :], rres[:, k, :], mparts[:, k, 1, :],
                                        ALU.subtract).then_inc(m_split, 1)

            def evac_m(b, h, k, hh):
                n = b * NH + h
                dve.wait_ge(mt_done, n + 1)
                dve.wait_ge(m_in[k], 16 + 48 * (b * (NH // 2) + hh))
                nc.vector.tensor_copy(m_rows[:, k, :], ps_m).then_inc(m_ev, 1)

            def norm(b, h, k):
                n = b * NH + h
                dve.wait_ge(ot_done, n + 3)
                view = ps_ot.rearrange("p j (c w) -> p j c w", w=VW)
                nc.vector.reciprocal(rden[:, k, :, :, :], view[:, :, :, HD:HD + 1]).then_inc(norm_step, 1)
                dve.wait_ge(norm_step, n + 1)
                out = ctx_sb[:, :, bass.ds(h * HD, HD)].rearrange("p (c j) d -> p j c d", j=2)
                nc.vector.tensor_tensor(out, view[:, :, :, 0:HD],
                                        rden[:, k, :, :, :].broadcast_to([P, 2, 4, HD]),
                                        ALU.mult).then_inc(norm_done, 1)

            def evac_v(b, c):
                dve.wait_ge(chunk_done, (b + 1) * NCH - NT + c + 1)
                if c == 0:
                    dve.wait_ge(v_staged, b * NH + 1)
                nc.vector.tensor_tensor(v_sb[:, c, :], ps_cols[c % 2][:, 0:D], vb_sb[:, :], ALU.add).then_inc(v_ev, 1)

            def slot(b, h, k, hh, ahead, first):
                for qt in range(NT):
                    if ahead == 2:
                        row_max(b, h + 2, k, qt)
                    if qt == 2 and ahead >= 1:
                        evac_m(b, h + 1, 1 - k, hh)
                    if qt == 5 and not first:
                        norm(b, h - 1, 1 - k)
                if ahead == 2:
                    split_max(b, h + 2, k)

            def batch(b):
                for qt in range(NT):
                    row_max(b, 0, 0, qt)
                    evac_v(b, qt)
                split_max(b, 0, 0)
                for qt in range(NT):
                    row_max(b, 1, 1, qt)
                split_max(b, 1, 1)
                evac_m(b, 0, 0, 0)
                dve.wait_ge(ctx_st, 16 * b + 16)
                slot(b, 0, 0, 0, 2, True)
                slot(b, 1, 1, 1, 2, False)
                with dve.Fori(1, PAIRS - 1) as p:
                    slot(b, 2 * p, 0, p, 2, False)
                    slot(b, 2 * p + 1, 1, p + 1, 2, False)
                slot(b, NH - 2, 0, PAIRS - 1, 1, False)
                slot(b, NH - 1, 1, PAIRS, 0, False)
                norm(b, NH - 1, 1)

            with dve.Fori(0, B) as b:
                batch(b)

        @block.tensor
        def _(pe):
            def qk_chunk(nb, c):
                t, j = c // NHALF, c % NHALF
                if c >= 2:
                    pe.wait_ge(qk_ev, nb * NQK * NHALF + c - 1)
                for d in range(DK):
                    mm = pe.matmul(ps_cols[c % 2][:, :], wqk_sb[:, d, t * P:(t + 1) * P],
                                   x_qk[:, d, j * MM_N:(j + 1) * MM_N], start=(d == 0), stop=(d == DK - 1))
                mm.then_inc(chunk_done, 1)

            def v_chunk(b, c):
                if c >= 2:
                    pe.wait_ge(v_ev, b * NT + c - 1)
                for d in range(DK):
                    mm = pe.matmul(ps_cols[c % 2][:, 0:D], x_v[:, d, c * P:(c + 1) * P], wv_sb[:, d, :],
                                   start=(d == 0), stop=(d == DK - 1))
                mm.then_inc(chunk_done, 1)

            def rows(b, h, qt):
                n = (b * NH + h) * NT + qt
                pe.wait_ge(rows_free, n + 1)
                for j in range(NHALF):
                    mm = pe.matmul(ps_rows[qt % 2][:, j * MM_N:(j + 1) * MM_N],
                                   q_aug[0:KS, bass.ds(h, 1), qt * P:(qt + 1) * P].rearrange("p h s -> p (h s)"),
                                   k_aug[0:KS, bass.ds(h, 1), j * MM_N:(j + 1) * MM_N].rearrange("p h s -> p (h s)"),
                                   start=True, stop=True)
                mm.then_inc(rows_done, 1)

            def cols(b, h, kt):
                n = (b * NH + h) * NT + kt
                for j in range(NHALF):
                    pe.wait_ge(exp_done, 2 * n + j + 1)
                    pe.matmul(ps_cols[j][:, :],
                              k_aug[0:KS + MROWS, bass.ds(h, 1), kt * P:(kt + 1) * P].rearrange("p h s -> p (h s)"),
                              q_aug[0:KS + MROWS, bass.ds(h, 1), j * MM_N:(j + 1) * MM_N].rearrange("p h s -> p (h s)"),
                              start=True, stop=True).then_inc(cols_done, 1)

            def values(b, h, k, kt):
                n = b * NH + h
                if kt == 0:
                    pe.wait_ge(o_ev, n + 1)
                    pe.wait_ge(v_staged, n + 2)
                pe.wait_ge(exp_done, 2 * (n * NT + kt) + 4)
                for c in range(4):
                    mm = pe.matmul(ps_o[VW * c:VW * (c + 1), :], v_st[:, k, kt, :],
                                   probs[:, kt, c * QC:(c + 1) * QC], start=(kt == 0), stop=(kt == NT - 1),
                                   tile_position=(0, VW * c))
                mm.then_inc(pv_done, 1)

            def turn_max(b, h, k):
                n = b * NH + h
                pe.wait_ge(m_split, n + 1)
                pe.wait_ge(m_ev, n)
                pe.wait_ge(norm_done, n)
                pe.transpose(ps_m, mparts[:, k, :, :].rearrange("p c t -> p (c t)"), identb[:, :]).then_inc(mt_done, 1)

            def turn_o(b, h, k, m_evs):
                n = b * NH + h
                pe.wait_ge(o_ev, n + 2)
                pe.wait_ge(m_ev, b * NH + m_evs)
                pe.wait_ge(norm_done, n + 2)
                for j in range(2):
                    mm = pe.transpose(ps_ot[:, j, :], o_sb[:, k, j * P:(j + 1) * P], identf[:, :])
                mm.then_inc(ot_done, 1)

            def slot(b, h, k, hh, ahead, first):
                for kt in range(NT):
                    if kt < NT - 1:
                        cols(b, h, kt + 1)
                    elif ahead >= 1:
                        pe.wait_ge(m_in[1 - k], 16 + 48 * (b * (NH // 2) + hh + 1))
                        cols(b, h + 1, 0)
                    if ahead == 2:
                        rows(b, h + 2, kt)
                    if kt == 2 and ahead >= 1:
                        turn_max(b, h + 1, 1 - k)
                    if kt == 5 and not first:
                        turn_o(b, h - 1, 1 - k, h + 2 if ahead >= 1 else NH)
                    values(b, h, k, kt)

            def batch(b, prep):
                pe.wait_ge(aug_in[0], 192 * (b + 1))
                pe.wait_ge(xv_in, 16 * (b + 1))
                for qt in range(NT):
                    rows(b, 0, qt)
                    v_chunk(b, qt)
                if prep:
                    pe.wait_ge(xq_in, 16 * (b + 2))
                for qt in range(NT):
                    rows(b, 1, qt)
                    if prep:
                        if qt < 2:
                            pe.wait_ge(v_ev, b * NT + NT - 1 + qt)
                        qk_chunk(b + 1, qt)
                turn_max_first(b)
                pe.wait_ge(v_ev, b * NT + NT)
                if prep:
                    pe.wait_ge(qk_ev, (b + 2) * NQK * NHALF)
                pe.wait_ge(m_in[0], 16 + 48 * (b * (NH // 2) + 1))
                cols(b, 0, 0)
                slot(b, 0, 0, 0, 2, True)
                slot(b, 1, 1, 1, 2, False)
                hold(pe, passed, aug_in[1], 192 * (b + 1))
                with pe.Fori(1, PAIRS - 1) as p:
                    slot(b, 2 * p, 0, p, 2, False)
                    slot(b, 2 * p + 1, 1, p + 1, 2, False)
                slot(b, NH - 2, 0, PAIRS - 1, 1, False)
                slot(b, NH - 1, 1, PAIRS - 1, 0, False)
                turn_o(b, NH - 1, 1, NH)

            def turn_max_first(b):
                n = b * NH
                pe.wait_ge(m_split, n + 1)
                pe.wait_ge(norm_done, n + 2)
                pe.transpose(ps_m, mparts[:, 0, :, :].rearrange("p c t -> p (c t)"), identb[:, :]).then_inc(mt_done, 1)

            pe.sem_inc(pv_done, RING)
            pe.sem_inc(ot_done, 2)
            for s in m_in:
                pe.sem_inc(s, 16)
            pe.sem_inc(ctx_st, 16)
            pe.wait_ge(w_in, 64)
            pe.wait_ge(xq_in, 16)
            for c in range(NQK * NHALF):
                qk_chunk(0, c)
            pe.wait_ge(qk_ev, NQK * NHALF)
            pe.wait_ge(const, 8)
            with pe.Fori(0, B - 1) as b:
                batch(b, True)
            batch(B - 1, False)


def feed_forward(nc, x, ctx_in, outT, out_b, gatesT, w_gate, w_up, w_down, rows_in, rows_out, out, sem):
    T, D = x.shape
    NE = w_gate.shape[0] - 1
    FI = w_gate.shape[2]
    TT = T // P
    DK = D // P
    FCH = [(i, min(P, FI - i)) for i in range(0, FI, P)]
    NC = len(FCH)
    TOPK = 2
    UNITS = rows_in.shape[0] // P
    EPS = 1e-5
    U = 4
    NG = NE + 1
    assert TT % U == 0 and UNITS % U == 0

    def wait(eng, s, value):
        if not (isinstance(value, int) and value <= 0):
            eng.wait_ge(s, value)

    def steps(eng, step, first, last, peel=0):
        for t in range(first, first + peel):
            step(t, t % U)
        with eng.Fori((first + peel) // U, last // U) as i:
            for k in range(U):
                step(i * U + k, k)

    with ExitStack() as ctx:
        def sb(name, shape, dt=F32):
            return ctx.enter_context(nc.sbuf_tensor("ff_" + name, shape, dt))

        def pb(name, shape, dt=F32):
            return ctx.enter_context(nc.psum_tensor("ff_" + name, shape, dt))

        wg = sb("wg", [P, DK, NE + 1, FI])
        wu = sb("wu", [P, DK, NE + 1, FI])
        wd = sb("wd", [P, NC, NE + 1, D])
        wo = sb("wo", [P, DK, D])
        ob = sb("ob", [P, D])
        gates = sb("gates", [P, DK, NG])
        eps = sb("eps", [P, 1])
        ident = sb("ident", [P, P])

        c_in = sb("c_in", [P, U, D])
        x_in = sb("x_in", [P, U, D])
        cT = sb("cT", [P, 2, DK, P])
        res = sb("res", [P, U, D])
        x1 = sb("x1", [P, U, D])
        x1T = sb("x1T", [P, 2, DK, P])
        stats = sb("stats", [P, U, 6])
        mv = sb("mv", [P, U, 2])
        std = sb("std", [P, U, 1])
        rstd = sb("rstd", [P, U, 1])
        logits = sb("logits", [P, TT, NG])

        wide = [P, TT, NE]
        probs = sb("router_probs", wide)
        rest = sb("router_rest", wide)
        first = sb("router_first", wide)
        second = sb("router_second", wide)
        score = sb("router_score", wide)
        order = sb("router_order", wide)
        chosen = sb("router_chosen", wide, BF16)
        scan = [sb(f"router_scan{i}", wide) for i in range(2)]
        place = sb("router_place", wide)
        tops = sb("router_tops", [P, 5, TT, 1])
        weights = sb("weights", [P, 3, TT, 1])
        pos = sb("pos", [P, TOPK, TT], mybir.dt.uint32)
        posf = sb("posf", [P, TOPK, TT])
        need_i = sb("need_i", [P, 2, NE], mybir.dt.int32)
        need = sb("need", [P, 4, NE])
        unit_no = sb("unit_no", [1, UNITS])
        unit_ex = sb("unit_ex", [1, 2, UNITS])
        unit_tab = sb("unit_tab", [1, UNITS], mybir.dt.int32)
        before = sb("before", [P, P], BF16)
        ones = sb("ones", [P, P], BF16)

        u_in = sb("u_in", [P, U, D])
        uT = sb("uT", [P, 2, DK, P])
        silu = sb("silu", [P, 2, FI])
        hid = sb("hid", [P, 2, FI])
        hT = sb("hT", [P, 2, NC, P])
        u_out = sb("u_out", [P, U, D])
        to = sb("to", [P, U, TOPK, 1], mybir.dt.uint32)

        s_in = sb("s_in", [P, U, D])
        y_in = sb("y_in", [P, TOPK, U, D])
        wsl = sb("wsl", [P, U, 3, 1])

        ps_t = pb("ps_t", [P, DK, P])
        ps_o = pb("ps_o", [P, D])
        ps_t2 = pb("ps_t2", [P, DK, P])
        ps_l = pb("ps_l", [P, 64])
        ps_g = pb("ps_g", [P, MM_N])
        ps_u = pb("ps_u", [P, MM_N])
        ps_h = pb("ps_h", [P, NC, P])
        ps_y = pb("ps_y", [P, MM_N])

        small_in = sem("small_in")
        big_in = sem("big_in")
        const = sem("const")
        c_ld = [sem(f"c_ld{k}") for k in range(U)]
        x1_st = [sem(f"x1_st{k}") for k in range(U)]
        cturn = sem("cturn")
        c_ev = sem("c_ev")
        proj = sem("proj")
        r_step = sem("r_step")
        std_done = sem("std_done")
        n_step = sem("n_step")
        xturn = sem("xturn")
        xt_ev = sem("xt_ev")
        logit = sem("logit")
        l_ev = sem("l_ev")
        rt = sem("rt")
        rexp = sem("rexp")
        rcount = sem("rcount")
        u_ld = [sem(f"u_ld{k}") for k in range(U)]
        uturn = sem("uturn")
        ut_ev = sem("ut_ev")
        gu = sem("gu")
        silu_done = sem("silu_done")
        h_done = sem("h_done")
        hturn = sem("hturn")
        ht_ev = sem("ht_ev")
        ht_ev2 = sem("ht_ev2")
        down = sem("down")
        y_ev = sem("y_ev")
        y_st = [sem(f"y_st{k}") for k in range(U)]
        to_done = sem("to_done")
        sent = [sem(f"sent{k}") for k in range(U)]
        f_ld = [sem(f"f_ld{k}") for k in range(U)]
        got = [sem(f"got{k}") for k in range(U)]
        f_idx = sem("f_idx")
        f_step = sem("f_step")
        f_std = sem("f_std")
        f_norm = sem("f_norm")
        passed = sem("passed")
        o_st = [sem(f"o_st{k}") for k in range(U)]

        def tile_of(a, t):
            return a[bass.ds(t * P, P), :]

        R_SUB = 2
        R_CHOSEN = R_SUB + 3 + 2 + 5 + 1 + 5 + 2 + TOPK + 1
        R_ALL = (R_CHOSEN + 1 + 2 * (TT.bit_length() - 1) + 2 + 5 + 2 * (NE.bit_length() - 1) + 3
                 + 2 * TOPK + 1 + 1 + (NE - 1) + 1)
        block = ctx.enter_context(nc.Block())

        @block.sync
        def _(sp):
            sp.dma_start(wo[:, :, :], outT.rearrange("(c p) n -> p c n", p=P)).then_inc(small_in, 16)
            sp.dma_start(ob[:, :], out_b.partition_broadcast(P)).then_inc(small_in, 16)
            sp.dma_start(gates[:, :, :], gatesT.rearrange("(c p) n -> p c n", p=P)).then_inc(small_in, 16)

            def load(t, k):
                wait(sp, cturn, t - U + 1)
                wait(sp, r_step, 4 * (t - U) + 1)
                sp.dma_start(c_in[:, k, :], tile_of(ctx_in, t)).then_inc(c_ld[k], 16)
                sp.dma_start(x_in[:, k, :], tile_of(x, t)).then_inc(c_ld[k], 16)

            def store(t, k):
                sp.wait_ge(n_step, 2 * t + 2)
                sp.dma_start(tile_of(rows_in, t), x1[:, k, :]).then_inc(x1_st[k], 16)

            for t in range(U):
                load(t, t)
            for d in range(DK):
                sp.dma_start(wg[:, d, :, :], w_gate[:, d * P:(d + 1) * P, :].rearrange("e p n -> p e n")).then_inc(big_in, 16)
                sp.dma_start(wu[:, d, :, :], w_up[:, d * P:(d + 1) * P, :].rearrange("e p n -> p e n")).then_inc(big_in, 16)
            for c, (i, n) in enumerate(FCH):
                sp.dma_start(wd[0:n, c, :, :], w_down[:, i:i + n, :].rearrange("e p n -> p e n")).then_inc(big_in, 16)

            def first_part(t, k):
                store(t - U, k)
                load(t, k)
            steps(sp, first_part, U, TT)
            for k in range(U):
                store(TT - U + k, k)

            def load_unit(u, k):
                wait(sp, uturn, u - U + 1)
                sp.dma_start(u_in[:, k, :], tile_of(rows_in, u)).then_inc(u_ld[k], 16)

            def store_unit(u, k):
                sp.wait_ge(y_ev, u + 1)
                sp.dma_start(tile_of(rows_out, u), u_out[:, k, :]).then_inc(y_st[k], 16)

            for k in range(U):
                sp.wait_ge(x1_st[k], 16 * (TT // U) + 16)
            for u in range(U):
                load_unit(u, u)
            with sp.Fori(1, TT // U) as i:
                for k in range(U):
                    hold(sp, passed, sent[k], 2 * 16 * i)
                    load_unit(i * U + k, k)
                    store_unit(i * U + k - U, k)
            for k in range(U):
                sp.wait_ge(sent[k], 2 * 16 * (TT // U))
            with sp.Fori(TT // U, UNITS // U) as i:
                for k in range(U):
                    load_unit(i * U + k, k)
                    store_unit(i * U + k - U, k)
            for k in range(U):
                store_unit(UNITS - U + k, k)

            def load_last(t, k):
                wait(sp, f_step, 5 * (t - U) + 3)
                sp.dma_start(x_in[:, k, :], tile_of(rows_in, t)).then_inc(f_ld[k], 16)
                sp.dma_start(s_in[:, k, :], tile_of(rows_out, t)).then_inc(f_ld[k], 16)

            def store_last(t, k):
                sp.wait_ge(f_norm, 2 * t + 2)
                sp.dma_start(tile_of(out, t), x1[:, k, :]).then_inc(o_st[k], 16)

            for k in range(U):
                sp.wait_ge(y_st[k], 16 * (UNITS // U) + 16)
            for t in range(U):
                load_last(t, t)

            def last_part(t, k):
                load_last(t, k)
                store_last(t - U, k)
            steps(sp, last_part, U, TT)
            for k in range(U):
                store_last(TT - U + k, k)
            for k in range(U):
                sp.wait_ge(o_st[k], 16 * (TT // U) + 16)

        @block.gpsimd
        def _(pool):
            nc.gpsimd.memset(ident[:, :], 0.0).then_inc(const, 1)
            nc.gpsimd.memset(before[:, :], 1.0).then_inc(const, 1)
            nc.gpsimd.memset(ones[:, :], 1.0).then_inc(const, 1)
            nc.gpsimd.memset(eps[:, :], EPS).then_inc(const, 1)
            pool.wait_ge(const, 4)
            nc.gpsimd.affine_select(out=ident[:, :], in_=ident[:, :], compare_op=ALU.not_equal, fill=1.0,
                                    base=0, pattern=[[-1, P]], channel_multiplier=1).then_inc(const, 1)
            nc.gpsimd.affine_select(out=before[:, :], in_=before[:, :], compare_op=ALU.is_gt, fill=0.0,
                                    base=0, pattern=[[1, P]], channel_multiplier=-1).then_inc(const, 1)
            nc.gpsimd.iota(order[:, :, :], pattern=[[0, TT], [-1, NE]], base=NE, channel_multiplier=0,
                           allow_small_or_imprecise_dtypes=True).then_inc(const, 1)
            nc.gpsimd.iota(unit_no[:, :], pattern=[[1, UNITS]], base=-TT, channel_multiplier=0,
                           allow_small_or_imprecise_dtypes=True).then_inc(const, 1)

            def send(i, k):
                t = i * U + k
                pool.wait_ge(u_ld[k], 16 * (i + 1))
                hold(pool, passed, to_done, t + 1)
                for c in range(TOPK):
                    nc.gpsimd.indirect_dma_start(
                        out=rows_in, out_offset=bass.IndirectOffsetOnAxis(ap=to[:, k, c, :], axis=0),
                        in_=u_in[:, k, :], in_offset=None).then_inc(sent[k], 16)

            with pool.Fori(0, TT // U) as i:
                for k in range(U):
                    send(i, k)

            def fetch(i, k):
                t = i * U + k
                hold(pool, passed, f_idx, 2 * t + 2)
                for c in range(TOPK):
                    nc.gpsimd.indirect_dma_start(
                        out=y_in[:, c, k, :], out_offset=None, in_=rows_out,
                        in_offset=bass.IndirectOffsetOnAxis(ap=to[:, k, c, :], axis=0)).then_inc(got[k], 16)

            for k in range(U):
                pool.wait_ge(y_st[k], 16 * (UNITS // U) + 16)
            with pool.Fori(0, TT // U) as i:
                for k in range(U):
                    fetch(i, k)

        @block.scalar
        def _(act):
            act.wait_ge(const, 8)
            for s in (*y_st, *x1_st, *o_st):
                act.sem_inc(s, 16)

            def turned_ctx(t, k):
                act.wait_ge(cturn, t + 1)
                wait(act, proj, t - 1)
                nc.scalar.activation(cT[:, k % 2, :, :], ps_t[:, :, :], ACT.Copy).then_inc(c_ev, 1)

            def sqrt(t, k):
                act.wait_ge(r_step, 4 * t + 4)
                nc.scalar.activation(std[:, k, :], mv[:, k, 1:2], ACT.Sqrt, bias=eps[:, 0:1]).then_inc(std_done, 1)

            def turned_x1(t, k):
                act.wait_ge(xturn, t + 1)
                wait(act, logit, t - 1)
                nc.scalar.activation(x1T[:, k % 2, :, :], ps_t2[:, :, :], ACT.Copy).then_inc(xt_ev, 1)

            def first_part(t, k):
                turned_ctx(t, k)
                if not (isinstance(t, int) and t < 1):
                    sqrt(t - 1, (k - 1) % U)
                if not (isinstance(t, int) and t < 2):
                    turned_x1(t - 2, (k - 2) % U)
            steps(act, first_part, 0, TT, peel=U)
            sqrt(TT - 1, U - 1)
            turned_x1(TT - 2, U - 2)
            turned_x1(TT - 1, U - 1)

            act.wait_ge(rt, R_SUB)
            nc.scalar.activation(probs[:, :, :], rest[:, :, :], ACT.Exp).then_inc(rexp, 1)
            nc.scalar.activation(tops[:, 4, :, :], logits[:, :, NE:NG], ACT.Exp, scale=-1.0).then_inc(rexp, 1)

            def turned_unit(u, k):
                act.wait_ge(uturn, u + 1)
                wait(act, gu, u - 1)
                nc.scalar.activation(uT[:, k % 2, :, :], ps_t[:, :, :], ACT.Copy).then_inc(ut_ev, 1)

            def gate(u, k):
                act.wait_ge(gu, u + 1)
                wait(act, h_done, u - 1)
                nc.scalar.activation(silu[:, k % 2, :], ps_g[:, 0:FI], ACT.Silu).then_inc(silu_done, 1)

            def last_chunk(u, k):
                act.wait_ge(hturn, u + 1)
                wait(act, ht_ev, u + 1)
                n = FCH[-1][1]
                nc.scalar.activation(hT[0:n, k % 2, NC - 1, :], ps_h[0:n, NC - 1, :], ACT.Copy).then_inc(ht_ev2, 1)

            def result(u, k, stored):
                act.wait_ge(down, u + 1)
                wait(act, y_st[k], stored + 16)
                nc.scalar.activation(u_out[:, k, :], ps_y[:, 0:D], ACT.Copy).then_inc(y_ev, 1)

            def unit(u, k, i):
                gate(u, k)
                if not (isinstance(u, int) and u == UNITS - 1):
                    turned_unit(u + 1, (k + 1) % U)
                if not (isinstance(u, int) and u == 0):
                    result(u - 1, (k - 1) % U, 16 * (i if k else i - 1))
                last_chunk(u, k)

            turned_unit(0, 0)
            for k in range(U):
                unit(k, k, 0)
            with act.Fori(1, UNITS // U - 1) as i:
                for k in range(U):
                    unit(i * U + k, k, i)
            for k in range(U):
                unit(UNITS - U + k, k, UNITS // U - 1)
            result(UNITS - 1, U - 1, 16 * (UNITS // U - 1))

            with act.Fori(0, TT // U) as i:
                for k in range(U):
                    act.wait_ge(f_step, 5 * (i * U + k) + 5)
                    nc.scalar.activation(std[:, k, :], mv[:, k, 1:2], ACT.Sqrt, bias=eps[:, 0:1]).then_inc(f_std, 1)

        @block.vector
        def _(dve):
            dve.wait_ge(small_in, 48)

            def residual(t, k, i):
                dve.wait_ge(proj, t + 1)
                dve.wait_ge(c_ld[k], 32 * (i + 1))
                wait(dve, n_step, 2 * (t - U) + 2)
                nc.vector.tensor_tensor(res[:, k, :], ps_o[:, :], x_in[:, k, :], ALU.add).then_inc(r_step, 1)
                dve.wait_ge(r_step, 4 * t + 1)
                nc.vector.tensor_tensor(res[:, k, :], res[:, k, :], ob[:, :], ALU.add).then_inc(r_step, 1)
                dve.wait_ge(r_step, 4 * t + 2)
                nc.vector.bn_stats(stats[:, k, :], res[:, k, :]).then_inc(r_step, 1)
                hold(dve, passed, r_step, 4 * t + 3)
                nc.vector.bn_aggr(mv[:, k, :], stats[:, k, :]).then_inc(r_step, 1)

            def normalise(t, k, i):
                dve.wait_ge(std_done, t + 1)
                nc.vector.reciprocal(rstd[:, k, :], std[:, k, :]).then_inc(n_step, 1)
                dve.wait_ge(n_step, 2 * t + 1)
                wait(dve, x1_st[k], 16 * i + 16)
                wait(dve, xturn, t - U + 2)
                nc.vector.tensor_scalar(x1[:, k, :], res[:, k, :], mv[:, k, 0:1], rstd[:, k, 0:1],
                                        ALU.subtract, ALU.mult).then_inc(n_step, 1)

            def take_logits(t):
                dve.wait_ge(logit, t + 1)
                nc.vector.tensor_copy(logits[:, bass.ds(t, 1), :].rearrange("p t e -> p (t e)"),
                                      ps_l[:, 0:NG]).then_inc(l_ev, 1)

            def first_part(t, k, i):
                if not (isinstance(t, int) and t < 3):
                    take_logits(t - 3)
                residual(t, k, i)
                if not (isinstance(t, int) and t < 1):
                    normalise(t - 1, (k - 1) % U, i if k else i - 1)
            for k in range(U):
                first_part(k, k, 0)
            with dve.Fori(1, TT // U) as i:
                for k in range(U):
                    first_part(i * U + k, k, i)
            normalise(TT - 1, U - 1, TT // U - 1)
            for t in range(TT - 3, TT):
                take_logits(t)

            n = [0]

            def r(op):
                n[0] += 1
                op.then_inc(rt, 1)
                dve.wait_ge(rt, n[0])

            def wide_of(a):
                return a.broadcast_to(wide)

            V = nc.vector
            dve.wait_ge(l_ev, TT)
            lg = logits[:, :, 0:NE]
            r(V.tensor_reduce(tops[:, 0, :, :], lg, AX.X, ALU.max))
            r(V.tensor_tensor(rest[:, :, :], lg, wide_of(tops[:, 0, :, :]), ALU.subtract))
            assert n[0] == R_SUB
            dve.wait_ge(rexp, 2)
            r(V.tensor_reduce(tops[:, 1, :, :], probs[:, :, :], AX.X, ALU.add))
            r(V.reciprocal(tops[:, 0, :, :], tops[:, 1, :, :]))
            r(V.tensor_tensor(probs[:, :, :], probs[:, :, :], wide_of(tops[:, 0, :, :]), ALU.mult))
            r(V.tensor_scalar(tops[:, 4, :, :], tops[:, 4, :, :], 1.0, None, ALU.add))
            r(V.reciprocal(weights[:, 2, :, :], tops[:, 4, :, :]))

            def choose(of, top, mask):
                r(V.tensor_reduce(top, of[:, :, :], AX.X, ALU.max))
                r(V.tensor_tensor(score[:, :, :], of[:, :, :], wide_of(top), ALU.is_equal))
                r(V.tensor_tensor(score[:, :, :], score[:, :, :], order[:, :, :], ALU.mult))
                r(V.tensor_reduce(tops[:, 3, :, :], score[:, :, :], AX.X, ALU.max))
                r(V.tensor_tensor(mask[:, :, :], score[:, :, :], wide_of(tops[:, 3, :, :]), ALU.is_equal))

            choose(probs, tops[:, 0, :, :], first)
            r(V.scalar_tensor_tensor(rest[:, :, :], first[:, :, :], -2.0, probs[:, :, :], ALU.mult, ALU.add))
            choose(rest, tops[:, 1, :, :], second)
            r(V.tensor_tensor(tops[:, 2, :, :], tops[:, 0, :, :], tops[:, 1, :, :], ALU.add))
            r(V.reciprocal(tops[:, 3, :, :], tops[:, 2, :, :]))
            for c in range(TOPK):
                r(V.tensor_tensor(weights[:, c, :, :], tops[:, c, :, :], tops[:, 3, :, :], ALU.mult))
            r(V.tensor_tensor(chosen[:, :, :], first[:, :, :], second[:, :, :], ALU.add))
            assert n[0] == R_CHOSEN
            dve.wait_ge(rcount, 2)
            totals = ps_u[:, 0:TT * NE].rearrange("p (t e) -> p t e", e=NE)
            inside = ps_g[:, 0:TT * NE].rearrange("p (t e) -> p t e", e=NE)
            r(V.tensor_copy(scan[0][:, :, :], totals))
            s, d = 0, 1
            while d < TT:
                r(V.tensor_copy(scan[1 - s][:, 0:d, :], scan[s][:, 0:d, :]))
                r(V.tensor_tensor(scan[1 - s][:, d:TT, :], scan[s][:, d:TT, :], scan[s][:, 0:TT - d, :], ALU.add))
                s, d = 1 - s, 2 * d
            r(V.tensor_tensor(place[:, :, :], scan[s][:, :, :], totals, ALU.subtract))
            r(V.tensor_tensor(place[:, :, :], place[:, :, :], inside, ALU.add))
            r(V.tensor_scalar(need[:, 0, :], scan[s][:, TT - 1, :], float(P - 1), None, ALU.add))
            r(V.tensor_copy(need_i[:, 0, :], need[:, 0, :]))
            r(V.tensor_scalar(need_i[:, 1, :], need_i[:, 0, :], P.bit_length() - 1, None, ALU.arith_shift_right))
            r(V.tensor_copy(need[:, 1, :], need_i[:, 1, :]))
            r(V.tensor_copy(need[:, 0, :], need_i[:, 1, :]))
            a, d = 1, 1
            while d < NE:
                b = 3 - a
                r(V.tensor_copy(need[:, b, 0:d], need[:, a, 0:d]))
                r(V.tensor_tensor(need[:, b, d:NE], need[:, a, d:NE], need[:, a, 0:NE - d], ALU.add))
                a, d = b, 2 * d
            r(V.tensor_tensor(need[:, 3, :], need[:, a, :], need[:, 0, :], ALU.subtract))
            r(V.tensor_scalar(need[:, 3, :], need[:, 3, :], float(P), float(T), ALU.mult, ALU.add))
            r(V.tensor_tensor(place[:, :, :], place[:, :, :],
                              need[:, 3:4, :].broadcast_to(wide), ALU.add))
            for c, mask in enumerate((first, second)):
                r(V.tensor_tensor(score[:, :, :], place[:, :, :], mask[:, :, :], ALU.mult))
                r(V.tensor_reduce(posf[:, c, :], score[:, :, :], AX.X, ALU.add))
            r(V.tensor_copy(pos[:, :, :], posf[:, :, :]))
            r(V.tensor_scalar(unit_ex[:, 0, :], unit_no[:, :], 0.0, float(NE), ALU.is_lt, ALU.mult))
            for e in range(NE - 1):
                r(V.scalar_tensor_tensor(unit_ex[:, (e + 1) % 2, :], unit_no[:, :], need[0:1, a, e:e + 1],
                                         unit_ex[:, e % 2, :], ALU.is_ge, ALU.add))
            r(V.tensor_copy(unit_tab[:, :], unit_ex[:, (NE - 1) % 2, :]))
            assert n[0] == R_ALL, n[0]

            def address(i, k):
                wait(dve, sent[k], 32 * i)
                t = i * U + k
                V.tensor_copy(to[:, k, :, :], pos[:, :, bass.ds(t, 1)]).then_inc(to_done, 1)

            def unit(u, k, i):
                dve.wait_ge(silu_done, u + 1)
                wait(dve, hturn, u - 1)
                V.tensor_tensor(hid[:, k % 2, :], silu[:, k % 2, :], ps_u[:, 0:FI], ALU.mult).then_inc(h_done, 1)
                dve.wait_ge(hturn, u + 1)
                wait(dve, down, u - 1)
                V.tensor_copy(hT[:, k % 2, 0:NC - 1, :], ps_h[:, 0:NC - 1, :]).then_inc(ht_ev, 1)

            for k in range(U):
                address(0, k)
            for k in range(U):
                unit(k, k, 0)
                address(1, k)
            with dve.Fori(1, TT // U - 1) as i:
                for k in range(U):
                    unit(i * U + k, k, i)
                    address(i + 1, k)
            with dve.Fori(TT // U - 1, UNITS // U) as i:
                for k in range(U):
                    unit(i * U + k, k, i)

            def slots(i, k):
                wait(dve, got[k], 32 * i)
                wait(dve, f_step, 5 * (i * U + k - U) + 3)
                t = i * U + k
                V.tensor_copy(to[:, k, :, :], pos[:, :, bass.ds(t, 1)]).then_inc(f_idx, 1)
                V.tensor_copy(wsl[:, k, :, :], weights[:, :, bass.ds(t, 1), :].rearrange("p c t o -> p c (t o)")
                              ).then_inc(f_idx, 1)

            def total(t, k, i):
                dve.wait_ge(f_ld[k], 32 * (i + 1))
                dve.wait_ge(got[k], 32 * (i + 1))
                dve.wait_ge(f_idx, 2 * t + 2)
                wait(dve, f_norm, 2 * (t - U) + 2)
                V.scalar_tensor_tensor(res[:, k, :], s_in[:, k, :], wsl[:, k, 2, :], x_in[:, k, :],
                                       ALU.mult, ALU.add).then_inc(f_step, 1)
                for c in range(TOPK):
                    dve.wait_ge(f_step, 5 * t + 1 + c)
                    V.scalar_tensor_tensor(res[:, k, :], y_in[:, c, k, :], wsl[:, k, c, :], res[:, k, :],
                                           ALU.mult, ALU.add).then_inc(f_step, 1)
                dve.wait_ge(f_step, 5 * t + 3)
                V.bn_stats(stats[:, k, :], res[:, k, :]).then_inc(f_step, 1)
                hold(dve, passed, f_step, 5 * t + 4)
                V.bn_aggr(mv[:, k, :], stats[:, k, :]).then_inc(f_step, 1)

            def finish(t, k, i):
                dve.wait_ge(f_std, t + 1)
                V.reciprocal(rstd[:, k, :], std[:, k, :]).then_inc(f_norm, 1)
                dve.wait_ge(f_norm, 2 * t + 1)
                wait(dve, o_st[k], 16 * i + 16)
                V.tensor_scalar(x1[:, k, :], res[:, k, :], mv[:, k, 0:1], rstd[:, k, 0:1],
                                ALU.subtract, ALU.mult).then_inc(f_norm, 1)

            for k in range(U):
                dve.wait_ge(sent[k], 32 * (TT // U))
            for k in range(U):
                slots(0, k)

            def last_part(i, k, more):
                t = i * U + k
                total(t, k, i)
                if more:
                    slots(i + 1, k)
                if not (isinstance(t, int) and t < 1):
                    finish(t - 1, (k - 1) % U, i if k else i - 1)

            for k in range(U):
                last_part(0, k, True)
            with dve.Fori(1, TT // U - 1) as i:
                for k in range(U):
                    last_part(i, k, True)
            for k in range(U):
                last_part(TT // U - 1, k, False)
            finish(TT - 1, U - 1, TT // U - 1)

        @block.tensor
        def _(pe):
            pe.wait_ge(const, 8)
            pe.wait_ge(small_in, 48)

            def turn_ctx(t, k, i):
                pe.wait_ge(c_ld[k], 32 * (i + 1))
                wait(pe, c_ev, t)
                for d in range(DK):
                    mm = pe.transpose(ps_t[:, d, :], c_in[:, k, d * P:(d + 1) * P], ident[:, :])
                mm.then_inc(cturn, 1)

            def project(t, k):
                pe.wait_ge(c_ev, t + 1)
                wait(pe, r_step, 4 * (t - 1) + 1)
                for d in range(DK):
                    mm = pe.matmul(ps_o[:, :], cT[:, k % 2, d, :], wo[:, d, :], start=(d == 0), stop=(d == DK - 1))
                mm.then_inc(proj, 1)

            def turn_x1(t, k):
                pe.wait_ge(n_step, 2 * t + 2)
                wait(pe, xt_ev, t)
                for d in range(DK):
                    mm = pe.transpose(ps_t2[:, d, :], x1[:, k, d * P:(d + 1) * P], ident[:, :])
                mm.then_inc(xturn, 1)

            def route(t, k):
                pe.wait_ge(xt_ev, t + 1)
                wait(pe, l_ev, t)
                for d in range(DK):
                    mm = pe.matmul(ps_l[:, 0:NG], x1T[:, k % 2, d, :], gates[:, d, :],
                                   start=(d == 0), stop=(d == DK - 1))
                mm.then_inc(logit, 1)

            def first_part(t, k, i):
                turn_ctx(t, k, i)
                old = not (isinstance(t, int) and t < 2)
                if old:
                    turn_x1(t - 2, (k - 2) % U)
                project(t, k)
                if old:
                    route(t - 2, (k - 2) % U)
            for k in range(U):
                first_part(k, k, 0)
            with pe.Fori(1, TT // U) as i:
                for k in range(U):
                    first_part(i * U + k, k, i)
            for t in (TT - 2, TT - 1):
                turn_x1(t, t % U)
                route(t, t % U)

            pe.wait_ge(rt, R_CHOSEN)
            flat = chosen[:, :, :].rearrange("p t e -> p (t e)")
            pe.matmul(ps_g[:, 0:TT * NE], before[:, :], flat, start=True, stop=True).then_inc(rcount, 1)
            pe.matmul(ps_u[:, 0:TT * NE], ones[:, :], flat, start=True, stop=True).then_inc(rcount, 1)

            def turn_unit(u, k, i):
                pe.wait_ge(u_ld[k], 16 * (i + 1))
                wait(pe, ut_ev, u)
                for d in range(DK):
                    mm = pe.transpose(ps_t[:, d, :], u_in[:, k, d * P:(d + 1) * P], ident[:, :])
                mm.then_inc(uturn, 1)

            def expert_of(u):
                return pe.value_load(unit_tab[0:1, bass.ds(u, 1)], min_val=0, max_val=NE)

            def gate_up(u, k):
                e = expert_of(u)
                pe.wait_ge(ut_ev, u + 1)
                wait(pe, h_done, u)
                for w, bank in ((wg, ps_g), (wu, ps_u)):
                    for d in range(DK):
                        mm = pe.matmul(bank[:, 0:FI], uT[:, k % 2, d, :],
                                       w[:, d, bass.ds(e, 1), :].rearrange("p e n -> p (e n)"),
                                       start=(d == 0), stop=(d == DK - 1))
                mm.then_inc(gu, 1)

            def turn_hidden(u, k):
                pe.wait_ge(h_done, u + 1)
                wait(pe, ht_ev, u)
                wait(pe, ht_ev2, u)
                for c, (i, n) in enumerate(FCH):
                    mm = pe.transpose(ps_h[0:n, c, :], hid[:, k % 2, i:i + n], ident[:, :])
                mm.then_inc(hturn, 1)

            def project_down(u, k):
                e = expert_of(u)
                pe.wait_ge(ht_ev, u + 1)
                pe.wait_ge(ht_ev2, u + 1)
                wait(pe, y_ev, u)
                for c, (_, n) in enumerate(FCH):
                    mm = pe.matmul(ps_y[:, 0:D], hT[0:n, k % 2, c, :],
                                   wd[0:n, c, bass.ds(e, 1), :].rearrange("p e n -> p (e n)"),
                                   start=(c == 0), stop=(c == NC - 1))
                mm.then_inc(down, 1)

            def unit(u, k, i):
                gate_up(u, k)
                if not (isinstance(u, int) and u == UNITS - 1):
                    turn_unit(u + 1, (k + 1) % U, i if k < U - 1 else i + 1)
                if not (isinstance(u, int) and u == 0):
                    project_down(u - 1, (k - 1) % U)
                turn_hidden(u, k)

            pe.wait_ge(big_in, 16 * (2 * DK + NC))
            pe.wait_ge(rt, R_ALL)
            turn_unit(0, 0, 0)
            for k in range(U):
                unit(k, k, 0)
            with pe.Fori(1, UNITS // U - 1) as i:
                for k in range(U):
                    unit(i * U + k, k, i)
            for k in range(U):
                unit(UNITS - U + k, k, UNITS // U - 1)
            project_down(UNITS - 1, U - 1)


_INS = ["x", "xT", "wqkT", "wvT", "qk_b", "v_b", "outT", "out_b", "gatesT", "w_gate", "w_up", "w_down"]


def build(nc, ins, out):
    B, D, S = ins["xT"].shape
    T = B * S
    NE = ins["w_gate"].shape[0] - 1
    TOPK = 2
    routed = T // P * TOPK + NE
    units = T // P + routed
    ctx_d = nc.dram_tensor("ctx_d", (B, S, D), F32).ap()
    qk_parts = nc.dram_tensor("qk_parts", (2, 3, D, S), BF16).ap()
    rows_in = nc.dram_tensor("rows_in", (units * P, D), F32).ap()
    rows_out = nc.dram_tensor("rows_out", (units * P, D), F32).ap()

    for part in range(2):
        with ExitStack() as sems:
            def sem(name):
                return sems.enter_context(nc.semaphore(("at_", "ff_")[part] + name))

            if part == 0:
                attention(nc, ins["xT"], ins["wqkT"], ins["wvT"], ins["qk_b"], ins["v_b"], ctx_d, qk_parts,
                          rows_in[T:units * P, :], sem)
            else:
                feed_forward(nc, ins["x"], ctx_d.rearrange("b s d -> (b s) d"), ins["outT"], ins["out_b"],
                             ins["gatesT"], ins["w_gate"], ins["w_up"], ins["w_down"], rows_in, rows_out,
                             out.rearrange("b s d -> (b s) d"), sem)


def kernel(L0_attn_x, L0_attn_qkv_w, L0_attn_qkv_b, L0_attn_out_w, L0_attn_out_b, L0_ffn_gate_w, L0_ffn_w_gate,
           L0_ffn_w_up, L0_ffn_w_down, L0_ffn_sw_gate, L0_ffn_sw_up, L0_ffn_sw_down, L0_ffn_shared_gate_w):
    import numpy as np
    import concourse.bacc as bacc
    from concourse.bass_utils import run_bass_kernel_spmd

    x = np.asarray(L0_attn_x)
    B, S, D = x.shape
    qkv_w, qkv_b = np.asarray(L0_attn_qkv_w), np.asarray(L0_attn_qkv_b)
    arrays = {
        "x": x.reshape(B * S, D),
        "xT": x.transpose(0, 2, 1),
        "wqkT": qkv_w[:2 * D].T,
        "wvT": qkv_w[2 * D:].T,
        "qk_b": qkv_b[:2 * D].reshape(-1, P).T,
        "v_b": qkv_b[2 * D:],
        "outT": np.asarray(L0_attn_out_w).T,
        "out_b": np.asarray(L0_attn_out_b),
        "gatesT": np.concatenate([np.asarray(L0_ffn_gate_w), np.asarray(L0_ffn_shared_gate_w)]).T,
        "w_gate": np.concatenate([np.asarray(L0_ffn_w_gate), np.asarray(L0_ffn_sw_gate)[None]]),
        "w_up": np.concatenate([np.asarray(L0_ffn_w_up), np.asarray(L0_ffn_sw_up)[None]]),
        "w_down": np.concatenate([np.asarray(L0_ffn_w_down), np.asarray(L0_ffn_sw_down)[None]]),
    }
    nc = bacc.Bacc("TRN2", target_bir_lowering=False, num_devices=1)
    ins = {}
    for name in _INS:
        arrays[name] = np.ascontiguousarray(arrays[name])
        ins[name] = nc.dram_tensor(f"in_{name}", arrays[name].shape, mybir.dt.from_np(arrays[name].dtype),
                                   kind="ExternalInput").ap()
    out = nc.dram_tensor("out", (B, S, D), F32, kind="ExternalOutput").ap()
    build(nc, ins, out)
    r = run_bass_kernel_spmd(nc, [{f"in_{name}": arrays[name] for name in _INS}], core_ids=[0])
    return r.results[0]["out"]
```

```python
from contextlib import ExitStack

import concourse.bass as bass
from concourse import mybir

F32 = mybir.dt.float32
BF16 = mybir.dt.bfloat16
ALU = mybir.AluOpType
ACT = mybir.ActivationFunctionType
AX = mybir.AxisListType

P = 128
NH = 16
HD = 16
MM_N = 512
VW = 32

Q_PART = (0, 0, 0, 1, 1, 2)
K_PART = (0, 1, 2, 0, 1, 0)
KS = len(Q_PART) * HD
MROWS = 3


def hold(eng, passed, s, value):
    eng.wait_ge(s, value)
    eng.sem_inc(passed, 1)


def attention(nc, xT, wqkT, wvT, qk_b, v_b, ctx_out, qk_parts, blank, sem):
    B, D, S = xT.shape
    DK = D // P
    NT = S // P
    NHALF = S // MM_N
    NQK = 2 * D // P
    HT = P // HD
    RING = 8
    QC = S // 4
    SCALE = 1.0 / HD ** 0.5
    PAIRS = NH // 2
    NCH = NT + NQK * NHALF
    TILES = (0, 2, 1, 3)

    with ExitStack() as ctx:
        def sb(name, shape, dt=F32):
            return ctx.enter_context(nc.sbuf_tensor(name, shape, dt))

        def pb(name, shape, dt=F32):
            return ctx.enter_context(nc.psum_tensor(name, shape, dt))

        q_aug = sb("q_aug", [P, NH, S], BF16)
        k_aug = sb("k_aug", [P, NH, S], BF16)
        probs = sb("probs", [P, RING, S])
        qk_sb = sb("qk_sb", [P, NQK, S])
        parts = sb("parts", [P, 2, 3, S], BF16)
        x_v = sb("x_v", [P, DK, S])
        x_qk = sb("x_qk", [P, DK, S])
        wqk_sb = sb("wqk_sb", [P, DK, 2 * D])
        wv_sb = sb("wv_sb", [P, DK, D])
        qkb_sb = sb("qkb_sb", [P, NQK])
        vb_sb = sb("vb_sb", [P, D])
        v_sb = sb("v_sb", [P, NT, D])
        v_st = sb("v_st", [P, 2, NT, VW])
        ctx_sb = sb("ctx_sb", [P, NT, D])
        o_sb = sb("o_sb", [P, 2, QC])
        rden = sb("rden", [P, 2, 2, 4, 1])
        rmax = sb("rmax", [P, 2, NT])
        rres = sb("rres", [P, 2, NT])
        mparts = sb("mparts", [P, 2, MROWS, NT], BF16)
        m_rows = sb("m_rows", [MROWS * NT, 2, P], BF16)
        zeros = sb("zeros", [P, D])
        identf = sb("identf", [P, P])
        identb = sb("identb", [P, P], BF16)

        ps_rows = [pb(f"ps_rows{i}", [P, S]) for i in range(2)]
        ps_cols = [pb(f"ps_cols{i}", [P, MM_N]) for i in range(2)]
        ps_o = pb("ps_o", [P, QC])
        ps_misc = pb("ps_misc", [P, MM_N])
        ps_m = ps_misc[0:MROWS * NT, 256:256 + P // 2].bitcast(BF16)
        ps_ot = ps_misc[:, 0:256].rearrange("p (j n) -> p j n", j=2)

        w_in = sem("w_in")
        xv_in = sem("xv_in")
        xq_in = sem("xq_in")
        const = sem("const")
        chunk_done = sem("chunk_done")
        v_ev = sem("v_ev")
        qk_ev = sem("qk_ev")
        split_step = sem("split_step")
        parts_out = [sem(f"parts_out{i}") for i in range(2)]
        aug_in = [sem(f"aug_in{i}") for i in range(2)]
        rows_done = sem("rows_done")
        rows_free = sem("rows_free")
        cols_done = sem("cols_done")
        exp_done = sem("exp_done")
        pv_done = sem("pv_done")
        v_staged = sem("v_staged")
        o_ev = sem("o_ev")
        ot_done = sem("ot_done")
        norm_done = sem("norm_done")
        norm_step = sem("norm_step")
        dve_step = sem("dve_step")
        m_split = sem("m_split")
        mt_done = sem("mt_done")
        m_ev = sem("m_ev")
        m_in = [sem(f"m_in{i}") for i in range(2)]
        passed = sem("passed")
        ctx_st = sem("ctx_st")
        blanked = sem("blanked")

        half = [slice(0, NH // 2), slice(NH // 2, NH)]

        def split(ns, eng, nb, i, step):
            t = TILES[i]
            src = qk_sb[:, t, :]
            pt = parts[:, i % 2, :, :]
            zero = zeros[:, 0:1].broadcast_to([P, S])
            if step == 0:
                eng.wait_ge(qk_ev, nb * NQK * NHALF + 2 * t + 2)
                if i >= 2:
                    eng.wait_ge(parts_out[i % 2], nb * 32 + 16)
                else:
                    eng.wait_ge(parts_out[i % 2], nb * 32)
            for c in (0, 1) if step == 0 else (2, 3):
                if not (step == 0 and c == 0):
                    eng.wait_ge(split_step, nb * 16 + 4 * i + c)
                if c == 0:
                    op = ns.tensor_tensor(pt[:, 0, :], src, zero, ALU.add)
                elif c == 1:
                    op = ns.tensor_tensor(src, src, pt[:, 0, :], ALU.subtract)
                elif c == 2:
                    op = ns.tensor_tensor(pt[:, 1, :], src, zero, ALU.add)
                else:
                    op = ns.tensor_tensor(pt[:, 2, :], src, pt[:, 1, :], ALU.subtract)
                op.then_inc(split_step, 1)

        block = ctx.enter_context(nc.Block())

        @block.sync
        def _(sp):
            sp.dma_start(wqk_sb[:, :, :], wqkT.rearrange("(c p) n -> p c n", p=P)).then_inc(w_in, 16)
            sp.dma_start(x_qk[:, :, :], xT[0].rearrange("(c p) n -> p c n", p=P)).then_inc(xq_in, 16)
            sp.dma_start(qkb_sb[:, :], qk_b).then_inc(w_in, 16)
            sp.dma_start(wv_sb[:, :, :], wvT.rearrange("(c p) n -> p c n", p=P)).then_inc(w_in, 16)
            sp.dma_start(vb_sb[:, :], v_b.partition_broadcast(P)).then_inc(w_in, 16)
            sp.dma_start(x_v[:, :, :], xT[0].rearrange("(c p) n -> p c n", p=P)).then_inc(xv_in, 16)

            def store_parts(nb, i):
                t = TILES[i]
                side, hf = t // 2, t % 2
                hold(sp, passed, split_step, nb * 16 + 4 * i + 4)
                hold(sp, passed, aug_in[hf], nb * 192)
                dst = qk_parts[side, :, hf * P:(hf + 1) * P, :].rearrange("c p s -> p c s")
                sp.dma_start(dst, parts[:, i % 2, :, :]).then_inc(parts_out[i % 2], 16)

            def load_aug(nb, hf, first=False):
                for i in (2 * hf, 2 * hf + 1):
                    hold(sp, passed, parts_out[i % 2], nb * 32 + 16 * (i // 2) + 16)
                if not first:
                    sp.wait_ge(cols_done, (nb - 1) * 256 + (hf + 1) * 128)
                for side, (aug, part) in enumerate(((q_aug, Q_PART), (k_aug, K_PART))):
                    for j, c in enumerate(part):
                        src = qk_parts[side, c, hf * P:(hf + 1) * P, :].rearrange("(h d) s -> d h s", d=HD)
                        sp.dma_start(aug[HD * j:HD * j + HD, half[hf], :], src).then_inc(aug_in[hf], 16)

            sp.wait_ge(chunk_done, NQK * NHALF)
            sp.dma_start(x_qk[:, :, :], xT[1].rearrange("(c p) n -> p c n", p=P)).then_inc(xq_in, 16)
            for i in range(NQK):
                store_parts(0, i)
                if i % 2:
                    load_aug(0, i // 2, True)

            def batch(b, prep, xq):
                def rows(h, k):
                    sp.wait_ge(m_ev, b * NH + h + 1)
                    for r in range(MROWS):
                        sp.dma_start(q_aug[KS + r:KS + r + 1, bass.ds(h, 1), :].rearrange("r h s -> r (h s)"),
                                     m_rows[NT * r:NT * (r + 1), k, :]).then_inc(m_in[k], 16)

                rows(0, 0)
                if prep:
                    sp.wait_ge(chunk_done, b * NCH + NCH + NCH - NT)
                    sp.dma_start(x_v[:, :, :], xT[b + 1].rearrange("(c p) n -> p c n", p=P)).then_inc(xv_in, 16)
                if xq:
                    sp.dma_start(x_qk[:, :, :], xT[b + 2].rearrange("(c p) n -> p c n", p=P)).then_inc(xq_in, 16)
                rows_b = blank.shape[0] // B
                for h in range(NH - 1):
                    rows(h + 1, (h + 1) % 2)
                    for j in range(h, rows_b // P, NH - 1):
                        sp.dma_start(blank[bass.ds(b * rows_b + j * P, P), :], zeros[:, :]).then_inc(blanked, 16)
                    if prep and h in (2, 4, 6, 8):
                        store_parts(b + 1, h // 2 - 1)
                    if prep and h == 9:
                        load_aug(b + 1, 0)
                sp.wait_ge(norm_done, b * NH + NH + 2)
                sp.dma_start(ctx_out[b].rearrange("(t p) d -> p t d", p=P), ctx_sb[:, :, :]).then_inc(ctx_st, 16)
                if prep:
                    load_aug(b + 1, 1)

            with sp.Fori(0, B - 2) as b:
                batch(b, True, True)
            batch(B - 2, True, False)
            batch(B - 1, False, False)
            sp.wait_ge(ctx_st, 16 * B + 16)
            sp.wait_ge(blanked, 16 * (blank.shape[0] // P))

        @block.gpsimd
        def _(pool):
            for m in (identf, identb, zeros):
                nc.gpsimd.memset(m[:, :], 0.0).then_inc(const, 1)
            nc.gpsimd.memset(v_st[:, :, :, HD + 1:VW], 0.0).then_inc(const, 1)
            nc.gpsimd.memset(v_st[:, :, :, HD:HD + 1], 1.0).then_inc(const, 1)
            pool.wait_ge(const, 5)
            nc.gpsimd.memset(k_aug[KS:KS + MROWS, :, :], -1.0).then_inc(const, 1)
            pool.wait_ge(const, 6)
            for m in (identf, identb):
                nc.gpsimd.affine_select(out=m[:, :], in_=m[:, :], compare_op=ALU.not_equal, fill=1.0,
                                        base=0, pattern=[[-1, P]], channel_multiplier=1).then_inc(const, 1)

            pool.sem_inc(v_staged, 1)

            def stage_v(b, h, k):
                n = b * NH + h
                pool.wait_ge(pv_done, 8 * n + 1)
                nc.gpsimd.tensor_tensor(v_st[:, k, :, 0:HD], v_sb[:, :, h * HD:(h + 1) * HD],
                                        zeros[:, 0:NT * HD].rearrange("p (t d) -> p t d", d=HD),
                                        ALU.add).then_inc(v_staged, 1)

            def batch(b, prep):
                pool.wait_ge(v_ev, NT * b + NT)
                stage_v(b, 0, 0)
                if prep:
                    for i in range(NQK):
                        stage_v(b, 2 * i + 1, 1)
                        split(nc.gpsimd, pool, b + 1, i, 0)
                        stage_v(b, 2 * i + 2, 0)
                        split(nc.gpsimd, pool, b + 1, i, 1)
                for h in range(9 if prep else 1, NH):
                    stage_v(b, h, h % 2)

            with pool.Fori(0, B - 1) as b:
                batch(b, True)
            batch(B - 1, False)

        @block.scalar
        def _(act):
            def evac_qk(nb, c):
                t, j = c // NHALF, c % NHALF
                act.wait_ge(chunk_done, nb * NCH + c + 1)
                if c == 0:
                    act.wait_ge(split_step, nb * 16)
                nc.scalar.activation(qk_sb[:, t, j * MM_N:(j + 1) * MM_N], ps_cols[c % 2][:, :], ACT.Identity,
                                     bias=qkb_sb[:, t:t + 1]).then_inc(qk_ev, 1)

            def evac_o(b, h, k):
                n = b * NH + h
                act.wait_ge(pv_done, RING + 8 * n + 8)
                act.wait_ge(ot_done, n + 1)
                nc.scalar.activation(o_sb[:, k, :], ps_o[:, :], ACT.Copy).then_inc(o_ev, 1)

            def exps(b, h, k, first=False):
                for kt in range(NT):
                    n = (b * NH + h) * NT + kt
                    act.wait_ge(pv_done, n + 1)
                    for j in range(NHALF):
                        act.wait_ge(cols_done, 2 * n + j + 1)
                        nc.scalar.activation(probs[:, kt, j * MM_N:(j + 1) * MM_N], ps_cols[j][:, :],
                                             ACT.Exp, scale=SCALE).then_inc(exp_done, 1)
                    if kt == 0 and not first:
                        evac_o(b, h - 1, 1 - k)

            def batch(b, prep):
                if prep:
                    for c in range(NQK * NHALF):
                        evac_qk(b + 1, c)
                exps(b, 0, 0, True)
                exps(b, 1, 1)
                with act.Fori(1, PAIRS) as p:
                    exps(b, 2 * p, 0)
                    exps(b, 2 * p + 1, 1)
                evac_o(b, NH - 1, 1)

            act.wait_ge(w_in, 64)
            for c in range(NQK * NHALF):
                evac_qk(0, c)
            act.sem_inc(exp_done, 2)
            act.sem_inc(o_ev, 1)
            with act.Fori(0, B - 1) as b:
                batch(b, True)
            batch(B - 1, False)

        @block.vector
        def _(dve):
            dve.sem_inc(rows_free, 2)
            dve.sem_inc(norm_done, 2)
            dve.wait_ge(const, 8)
            for i in range(NQK):
                split(nc.vector, dve, 0, i, 0)
                split(nc.vector, dve, 0, i, 1)

            def row_max(b, h, k, qt):
                n = (b * NH + h) * NT + qt
                dve.wait_ge(rows_done, n + 1)
                nc.vector.tensor_reduce(rmax[:, k, qt:qt + 1], ps_rows[qt % 2][:, :], AX.X,
                                        ALU.max).then_inc(rows_free, 1)

            def split_max(b, h, k):
                n = b * NH + h
                dve.wait_ge(rows_free, 2 + 8 * n + 8)
                nc.vector.tensor_copy(mparts[:, k, 0, :], rmax[:, k, :]).then_inc(dve_step, 1)
                dve.wait_ge(dve_step, 3 * n + 1)
                nc.vector.tensor_tensor(rres[:, k, :], rmax[:, k, :], mparts[:, k, 0, :],
                                        ALU.subtract).then_inc(dve_step, 1)
                dve.wait_ge(dve_step, 3 * n + 2)
                nc.vector.tensor_copy(mparts[:, k, 1, :], rres[:, k, :]).then_inc(dve_step, 1)
                dve.wait_ge(dve_step, 3 * n + 3)
                nc.vector.tensor_tensor(mparts[:, k, 2, :], rres[:, k, :], mparts[:, k, 1, :],
                                        ALU.subtract).then_inc(m_split, 1)

            def evac_m(b, h, k, hh):
                n = b * NH + h
                dve.wait_ge(mt_done, n + 1)
                dve.wait_ge(m_in[k], 16 + 48 * (b * (NH // 2) + hh))
                nc.vector.tensor_copy(m_rows[:, k, :], ps_m).then_inc(m_ev, 1)

            def norm(b, h, k):
                n = b * NH + h
                dve.wait_ge(ot_done, n + 3)
                view = ps_ot.rearrange("p j (c w) -> p j c w", w=VW)
                nc.vector.reciprocal(rden[:, k, :, :, :], view[:, :, :, HD:HD + 1]).then_inc(norm_step, 1)
                dve.wait_ge(norm_step, n + 1)
                out = ctx_sb[:, :, bass.ds(h * HD, HD)].rearrange("p (c j) d -> p j c d", j=2)
                nc.vector.tensor_tensor(out, view[:, :, :, 0:HD],
                                        rden[:, k, :, :, :].broadcast_to([P, 2, 4, HD]),
                                        ALU.mult).then_inc(norm_done, 1)

            def evac_v(b, c):
                dve.wait_ge(chunk_done, (b + 1) * NCH - NT + c + 1)
                if c == 0:
                    dve.wait_ge(v_staged, b * NH + 1)
                nc.vector.tensor_tensor(v_sb[:, c, :], ps_cols[c % 2][:, 0:D], vb_sb[:, :], ALU.add).then_inc(v_ev, 1)

            def slot(b, h, k, hh, ahead, first):
                for qt in range(NT):
                    if ahead == 2:
                        row_max(b, h + 2, k, qt)
                    if qt == 2 and ahead >= 1:
                        evac_m(b, h + 1, 1 - k, hh)
                    if qt == 5 and not first:
                        norm(b, h - 1, 1 - k)
                if ahead == 2:
                    split_max(b, h + 2, k)

            def batch(b):
                for qt in range(NT):
                    row_max(b, 0, 0, qt)
                    evac_v(b, qt)
                split_max(b, 0, 0)
                for qt in range(NT):
                    row_max(b, 1, 1, qt)
                    if qt == 4:
                        evac_m(b, 0, 0, 0)
                split_max(b, 1, 1)
                dve.wait_ge(ctx_st, 16 * b + 16)
                slot(b, 0, 0, 0, 2, True)
                slot(b, 1, 1, 1, 2, False)
                with dve.Fori(1, PAIRS - 1) as p:
                    slot(b, 2 * p, 0, p, 2, False)
                    slot(b, 2 * p + 1, 1, p + 1, 2, False)
                slot(b, NH - 2, 0, PAIRS - 1, 1, False)
                slot(b, NH - 1, 1, PAIRS, 0, False)
                norm(b, NH - 1, 1)

            with dve.Fori(0, B) as b:
                batch(b)

        @block.tensor
        def _(pe):
            def qk_chunk(nb, c):
                t, j = c // NHALF, c % NHALF
                if c >= 2:
                    pe.wait_ge(qk_ev, nb * NQK * NHALF + c - 1)
                for d in range(DK):
                    mm = pe.matmul(ps_cols[c % 2][:, :], wqk_sb[:, d, t * P:(t + 1) * P],
                                   x_qk[:, d, j * MM_N:(j + 1) * MM_N], start=(d == 0), stop=(d == DK - 1))
                mm.then_inc(chunk_done, 1)

            def v_chunk(b, c):
                if c >= 2:
                    pe.wait_ge(v_ev, b * NT + c - 1)
                for d in range(DK):
                    mm = pe.matmul(ps_cols[c % 2][:, 0:D], x_v[:, d, c * P:(c + 1) * P], wv_sb[:, d, :],
                                   start=(d == 0), stop=(d == DK - 1))
                mm.then_inc(chunk_done, 1)

            def rows(b, h, qt):
                n = (b * NH + h) * NT + qt
                pe.wait_ge(rows_free, n + 1)
                for j in range(NHALF):
                    mm = pe.matmul(ps_rows[qt % 2][:, j * MM_N:(j + 1) * MM_N],
                                   q_aug[0:KS, bass.ds(h, 1), qt * P:(qt + 1) * P].rearrange("p h s -> p (h s)"),
                                   k_aug[0:KS, bass.ds(h, 1), j * MM_N:(j + 1) * MM_N].rearrange("p h s -> p (h s)"),
                                   start=True, stop=True)
                mm.then_inc(rows_done, 1)

            def cols(b, h, kt):
                n = (b * NH + h) * NT + kt
                for j in range(NHALF):
                    pe.wait_ge(exp_done, 2 * n + j + 1)
                    pe.matmul(ps_cols[j][:, :],
                              k_aug[0:KS + MROWS, bass.ds(h, 1), kt * P:(kt + 1) * P].rearrange("p h s -> p (h s)"),
                              q_aug[0:KS + MROWS, bass.ds(h, 1), j * MM_N:(j + 1) * MM_N].rearrange("p h s -> p (h s)"),
                              start=True, stop=True).then_inc(cols_done, 1)

            def values(b, h, k, kt):
                n = b * NH + h
                if kt == 0:
                    pe.wait_ge(o_ev, n + 1)
                    pe.wait_ge(v_staged, n + 2)
                pe.wait_ge(exp_done, 2 * (n * NT + kt) + 4)
                for c in range(4):
                    mm = pe.matmul(ps_o[VW * c:VW * (c + 1), :], v_st[:, k, kt, :],
                                   probs[:, kt, c * QC:(c + 1) * QC], start=(kt == 0), stop=(kt == NT - 1),
                                   tile_position=(0, VW * c))
                mm.then_inc(pv_done, 1)

            def turn_max(b, h, k):
                n = b * NH + h
                pe.wait_ge(m_split, n + 1)
                pe.wait_ge(m_ev, n)
                pe.wait_ge(norm_done, n)
                pe.transpose(ps_m, mparts[:, k, :, :].rearrange("p c t -> p (c t)"), identb[:, :]).then_inc(mt_done, 1)

            def turn_o(b, h, k, m_evs):
                n = b * NH + h
                pe.wait_ge(o_ev, n + 2)
                pe.wait_ge(m_ev, b * NH + m_evs)
                pe.wait_ge(norm_done, n + 2)
                for j in range(2):
                    mm = pe.transpose(ps_ot[:, j, :], o_sb[:, k, j * P:(j + 1) * P], identf[:, :])
                mm.then_inc(ot_done, 1)

            def slot(b, h, k, hh, ahead, first):
                for kt in range(NT):
                    if kt < NT - 1:
                        cols(b, h, kt + 1)
                    elif ahead >= 1:
                        pe.wait_ge(m_in[1 - k], 16 + 48 * (b * (NH // 2) + hh + 1))
                        cols(b, h + 1, 0)
                    if ahead == 2:
                        rows(b, h + 2, kt)
                    if kt == 2 and ahead >= 1:
                        turn_max(b, h + 1, 1 - k)
                    if kt == 5 and not first:
                        turn_o(b, h - 1, 1 - k, h + 2 if ahead >= 1 else NH)
                    values(b, h, k, kt)

            def batch(b, prep):
                pe.wait_ge(aug_in[0], 192 * (b + 1))
                pe.wait_ge(xv_in, 16 * (b + 1))
                for qt in range(NT):
                    rows(b, 0, qt)
                    v_chunk(b, qt)
                if prep:
                    pe.wait_ge(xq_in, 16 * (b + 2))
                for qt in range(NT):
                    rows(b, 1, qt)
                    if prep:
                        if qt < 2:
                            pe.wait_ge(v_ev, b * NT + NT - 1 + qt)
                        qk_chunk(b + 1, qt)
                    if qt == 3:
                        turn_max_first(b)
                pe.wait_ge(v_ev, b * NT + NT)
                if prep:
                    pe.wait_ge(qk_ev, (b + 2) * NQK * NHALF)
                pe.wait_ge(m_in[0], 16 + 48 * (b * (NH // 2) + 1))
                cols(b, 0, 0)
                slot(b, 0, 0, 0, 2, True)
                slot(b, 1, 1, 1, 2, False)
                hold(pe, passed, aug_in[1], 192 * (b + 1))
                with pe.Fori(1, PAIRS - 1) as p:
                    slot(b, 2 * p, 0, p, 2, False)
                    slot(b, 2 * p + 1, 1, p + 1, 2, False)
                slot(b, NH - 2, 0, PAIRS - 1, 1, False)
                slot(b, NH - 1, 1, PAIRS - 1, 0, False)
                turn_o(b, NH - 1, 1, NH)

            def turn_max_first(b):
                n = b * NH
                pe.wait_ge(m_split, n + 1)
                pe.wait_ge(norm_done, n + 2)
                pe.transpose(ps_m, mparts[:, 0, :, :].rearrange("p c t -> p (c t)"), identb[:, :]).then_inc(mt_done, 1)

            pe.sem_inc(pv_done, RING)
            pe.sem_inc(ot_done, 2)
            for s in m_in:
                pe.sem_inc(s, 16)
            pe.sem_inc(ctx_st, 16)
            pe.wait_ge(w_in, 64)
            pe.wait_ge(xq_in, 16)
            for c in range(NQK * NHALF):
                qk_chunk(0, c)
            pe.wait_ge(qk_ev, NQK * NHALF)
            pe.wait_ge(const, 8)
            with pe.Fori(0, B - 1) as b:
                batch(b, True)
            batch(B - 1, False)


def feed_forward(nc, x, ctx_in, outT, out_b, gatesT, w_gate, w_up, w_down, x1_rows, shared_rows, rows_in, rows_out, out, sem):
    T, D = x.shape
    NE = w_gate.shape[0] - 1
    FI = w_gate.shape[2]
    TT = T // P
    DK = D // P
    FCH = [(i, min(P, FI - i)) for i in range(0, FI, P)]
    NC = len(FCH)
    TOPK = 2
    ROUTED = rows_in.shape[0] // P
    UNITS = TT + ROUTED
    EPS = 1e-5
    U = 4
    NG = NE + 1
    assert TT % U == 0 and UNITS % U == 0

    def wait(eng, s, value):
        if not (isinstance(value, int) and value <= 0):
            eng.wait_ge(s, value)

    def pipeline(eng, step, behind):
        for t in range(2 * U):
            step(t, t % U, t // U)
        with eng.Fori(2, TT // U) as i:
            for k in range(U):
                step(i * U + k, k, i)
        for t in range(TT, TT + behind):
            step(t, t % U, t // U)

    def live(t):
        return not isinstance(t, int) or 0 <= t < TT

    HALF = TT // 2
    PHASES = ((0, HALF), (HALF, HALF + ROUTED), (HALF + ROUTED, UNITS))
    SEND, EXPERTS, SUM = range(3)
    LAST = HALF + ROUTED
    assert all(a % U == 0 for a, _ in PHASES)

    def units(eng, step, behind, peel=1):
        for ph, (a, b) in enumerate(PHASES):
            for u in range(a, a + peel * U):
                step(u, u % U, u // U, ph)
            with eng.Fori(a // U + peel, b // U) as i:
                for k in range(U):
                    step(i * U + k, k, i, ph)
        for u in range(UNITS, UNITS + behind):
            step(u, u % U, u // U, None)

    def phase(u, ph):
        if not isinstance(u, int):
            return ph
        return next((p for p, (a, b) in enumerate(PHASES) if a <= u < b), None)

    def rows_of(u, ph):
        ph = phase(u, ph)
        if ph == SEND:
            return tile_of(x1_rows, u), tile_of(shared_rows, u)
        if ph == EXPERTS:
            return tile_of(rows_in, u - HALF), tile_of(rows_out, u - HALF)
        return tile_of(x1_rows, u - ROUTED), None

    def tile_of(a, t):
        return a[bass.ds(t * P, P), :]

    def body(k, i, lag):
        return i + (k - lag) // U

    with ExitStack() as ctx:
        def sb(name, shape, dt=F32):
            return ctx.enter_context(nc.sbuf_tensor("ff_" + name, shape, dt))

        def pb(name, shape, dt=F32):
            return ctx.enter_context(nc.psum_tensor("ff_" + name, shape, dt))

        wg = sb("wg", [P, DK, NE + 1, FI])
        wu = sb("wu", [P, DK, NE + 1, FI])
        wd = sb("wd", [P, NC, NE + 1, D])
        wo = sb("wo", [P, DK, D])
        ob = sb("ob", [P, D])
        gates = sb("gates", [P, DK, NG])
        eps = sb("eps", [P, 1])
        minus_half = sb("minus_half", [P, 1])
        ident = sb("ident", [P, P])

        c_in = sb("c_in", [P, U, D])
        x_in = sb("x_in", [P, U, D])
        cT = sb("cT", [P, 2, DK, P])
        res = sb("res", [P, U, D])
        x1 = sb("x1", [P, U, D])
        x1T = sb("x1T", [P, 2, DK, P])
        stats = sb("stats", [P, U, 6])
        mv = sb("mv", [P, U, 2])
        std = sb("std", [P, U, 1])
        rstd = sb("rstd", [P, U, 1])
        logits = sb("logits", [P, TT, NG])

        wide = [P, TT, NE]
        probs = sb("router_probs", wide)
        rest = sb("router_rest", wide)
        first = sb("router_first", wide)
        second = sb("router_second", wide)
        score = sb("router_score", wide)
        order = sb("router_order", wide)
        chosen = sb("router_chosen", wide, BF16)
        scan = [sb(f"router_scan{i}", wide) for i in range(2)]
        place = sb("router_place", wide)
        tops = sb("router_tops", [P, 5, TT, 1])
        weights = sb("weights", [P, 3, TT, 1])
        pos = sb("pos", [P, TOPK, TT], mybir.dt.uint32)
        posf = sb("posf", [P, TOPK, TT])
        need_i = sb("need_i", [P, 2, NE], mybir.dt.int32)
        need = sb("need", [P, 4, NE])
        unit_no = sb("unit_no", [1, UNITS])
        unit_ex = sb("unit_ex", [1, 2, UNITS])
        unit_tab = sb("unit_tab", [1, UNITS], mybir.dt.int32)
        before = sb("before", [P, P], BF16)
        ones = sb("ones", [P, P], BF16)

        HC = NC * P
        u_in = sb("u_in", [P, U, D])
        uT = sb("uT", [P, 2, DK, P])
        silu = sb("silu", [P, 2, FI])
        hid = sb("hid", [P, 2, HC])
        hT = sb("hT", [P, 2, NC, P])
        u_out = sb("u_out", [P, U, D])
        to = sb("to", [P, U, TOPK, 2, 1], mybir.dt.uint32)
        wsl = sb("wsl", [P, U, 3, 2, 1])
        y_in = sb("y_in", [P, U, 2, TOPK, D])
        x_send = y_in[:, :, 0, :, :]
        s_in = sb("s_in", [P, U, D])
        sums = sb("sums", [P, U, 2, D])
        normed = sb("normed", [P, U, 2, D])
        stats2 = sb("stats2", [P, U, 2, 6])
        mv2 = sb("mv2", [P, U, 2, 2])
        veps = sb("veps", [P, U, 2, 1])
        rstd2 = sb("rstd2", [P, U, 2, 1])
        shift = sb("shift", [P, U, 2, 1])

        ps_t = pb("ps_t", [P, DK, P])
        ps_o = pb("ps_o", [P, D])
        ps_t2 = pb("ps_t2", [P, DK, P])
        ps_l = pb("ps_l", [P, 64])
        ps_g = pb("ps_g", [P, MM_N])
        ps_u = pb("ps_u", [P, MM_N])
        ps_h = pb("ps_h", [P, NC, P])
        ps_y = pb("ps_y", [P, MM_N])
        ct_banks = (ps_t[:, :, :], ps_g[:, 0:D].rearrange("p (d n) -> p d n", n=P))
        pr_banks = (ps_o[:, :], ps_u[:, 0:D])
        xt_banks = (ps_t2[:, :, :], ps_y[:, 0:D].rearrange("p (d n) -> p d n", n=P))
        lo_banks = (ps_l[:, 0:NG], ps_h[:, 0, 0:NG])

        small_in = sem("small_in")
        big_in = sem("big_in")
        const = sem("const")
        c_ld = [sem(f"c_ld{k}") for k in range(U)]
        x_ld = [sem(f"x_ld{k}") for k in range(U)]
        biased = sem("biased")
        x1_st = [sem(f"x1_st{k}") for k in range(U)]
        cturn = sem("cturn")
        c_ev = sem("c_ev")
        proj = sem("proj")
        r_step = sem("r_step")
        std_done = sem("std_done")
        n_step = sem("n_step")
        xturn = sem("xturn")
        xt_ev = sem("xt_ev")
        logit = sem("logit")
        l_ev = sem("l_ev")
        rt = sem("rt")
        rexp = sem("rexp")
        rcount = sem("rcount")
        u_ld = [sem(f"u_ld{k}") for k in range(U)]
        uturn = sem("uturn")
        ut_ev = sem("ut_ev")
        gu = sem("gu")
        silu_done = sem("silu_done")
        h_done = sem("h_done")
        hturn = sem("hturn")
        ht_ev = sem("ht_ev")
        down = sem("down")
        y_ev = sem("y_ev")
        y_st = [sem(f"y_st{k}") for k in range(U)]
        send_ld = [sem(f"send_ld{k}") for k in range(U)]
        sent = [sem(f"sent{k}") for k in range(U)]
        slot_done = sem("slot_done")
        s_ld = [sem(f"s_ld{k}") for k in range(U)]
        got = [sem(f"got{k}") for k in range(U)]
        f_step = sem("f_step")
        f_std = sem("f_std")
        f_shift = sem("f_shift")
        f_norm = sem("f_norm")
        passed = sem("passed")
        o_st = [sem(f"o_st{k}") for k in range(U)]

        R_SUB = 2
        R_CHOSEN = R_SUB + 3 + 2 + 5 + 1 + 5 + 2 + TOPK + 1
        R_ALL = (R_CHOSEN + 1 + 2 * (TT.bit_length() - 1) + 2 + 5 + 2 * (NE.bit_length() - 1) + 3
                 + 2 * TOPK + 1 + 1 + NE + 1)
        F_SUMS, F_STEPS = 2 * TOPK, 2 * TOPK + 4
        block = ctx.enter_context(nc.Block())

        @block.sync
        def _(sp):
            sp.dma_start(wo[:, :, :], outT.rearrange("(c p) n -> p c n", p=P)).then_inc(small_in, 16)
            sp.dma_start(ob[:, :], out_b.partition_broadcast(P)).then_inc(small_in, 16)
            sp.dma_start(gates[:, :, :], gatesT.rearrange("(c p) n -> p c n", p=P)).then_inc(small_in, 16)

            def load_ctx(t, k):
                wait(sp, cturn, t - U + 1)
                sp.dma_start(c_in[:, k, :], tile_of(ctx_in, t)).then_inc(c_ld[k], 16)

            def load_x(t, k):
                wait(sp, r_step, 3 * (t - U) + 1)
                sp.dma_start(x_in[:, k, :], tile_of(x, t)).then_inc(x_ld[k], 16)

            def store(t, k):
                sp.wait_ge(n_step, 2 * t + 2)
                sp.dma_start(tile_of(x1_rows, t), x1[:, k, :]).then_inc(x1_st[k], 16)

            def first_part(t, k, i):
                if live(t):
                    load_ctx(t, k)
                if live(t - 1):
                    load_x(t - 1, (k - 1) % U)
                if live(t - 7):
                    store(t - 7, (k - 7) % U)

            def load_weights(e, k):
                one = bass.ds(e, 1)
                full = (NC - 1) * P
                if k < 2:
                    w, src = ((wg, w_gate), (wu, w_up))[k]
                    sp.dma_start(w[:, :, one, :].rearrange("p c e n -> p c (e n)"),
                                 src[one, :, :].rearrange("e (c p) n -> p (e c) n", p=P)).then_inc(big_in, 16)
                elif k == 2:
                    sp.dma_start(wd[:, 0:NC - 1, one, :].rearrange("p c e n -> p c (e n)"),
                                 w_down[one, 0:full, :].rearrange("e (c p) n -> p (e c) n", p=P)).then_inc(big_in, 16)
                else:
                    sp.dma_start(wd[0:FI - full, NC - 1, one, :].rearrange("p e n -> p (e n)"),
                                 w_down[one, full:FI, :].rearrange("e p n -> p (e n)")).then_inc(big_in, 16)

            for t in range(2 * U):
                first_part(t, t % U, t // U)
                if t >= U:
                    load_weights(NE, t % U)
            with sp.Fori(2, 2 + NE) as i:
                for k in range(U):
                    first_part(i * U + k, k, i)
                    load_weights(i - 2, k)
            with sp.Fori(2 + NE, TT // U) as i:
                for k in range(U):
                    first_part(i * U + k, k, i)
            for t in range(TT, TT + 7):
                first_part(t, t % U, t // U)

            def load_unit(u, k, ph):
                wait(sp, y_ev, u - U + 1)
                sp.dma_start(u_in[:, k, :], rows_of(u, ph)[0]).then_inc(u_ld[k], 16)

            def load_send(t, k, i):
                wait(sp, sent[k], 2 * TOPK * 16 * i)
                for h in range(2):
                    sp.dma_start(x_send[:, k, h, :], tile_of(x1_rows, t + h * HALF)).then_inc(send_ld[k], 16)

            def store_unit(u, k, ph):
                sp.wait_ge(y_ev, u + 1)
                sp.dma_start(rows_of(u, ph)[1], u_out[:, k, :]).then_inc(y_st[k], 16)

            def load_shared(q, k):
                wait(sp, f_step, F_STEPS * (q - U) + 1)
                sp.dma_start(s_in[:, k, :], tile_of(shared_rows, q)).then_inc(s_ld[k], 16)

            def store_sums(q, k):
                sp.wait_ge(f_norm, 2 * q + 2)
                for h in range(2):
                    sp.dma_start(tile_of(out, q + h * HALF), normed[:, k, h, :]).then_inc(o_st[k], 16)

            for k in range(U):
                sp.wait_ge(x1_st[k], 16 * (TT // U) + 16)

            def unit(u, k, i, ph):
                if isinstance(u, int) and u == HALF:
                    for j in range(U):
                        sp.wait_ge(sent[j], 2 * TOPK * 16 * (HALF // U))
                if isinstance(u, int) and u == LAST:
                    for j in range(U):
                        sp.wait_ge(y_st[j], 16 * (HALF // U) + 16)
                if phase(u, ph) is not None:
                    load_unit(u, k, ph)
                if phase(u, ph) == SEND:
                    load_send(u, k, i)
                if phase(u - 4, ph) in (SEND, EXPERTS):
                    store_unit(u - 4, k, ph)
                if phase(u - 1, ph) == SUM:
                    load_shared(u - 1 - LAST, (k - 1) % U)
                if phase(u - 8, ph) == SUM:
                    store_sums(u - 8 - LAST, k)
            units(sp, unit, 8, peel=2)
            for k in range(U):
                sp.wait_ge(o_st[k], 2 * 16 * (HALF // U) + 16)

        @block.gpsimd
        def _(pool):
            nc.gpsimd.memset(ident[:, :], 0.0).then_inc(const, 1)
            nc.gpsimd.memset(before[:, :], 1.0).then_inc(const, 1)
            nc.gpsimd.memset(ones[:, :], 1.0).then_inc(const, 1)
            nc.gpsimd.memset(eps[:, :], EPS).then_inc(const, 1)
            nc.gpsimd.memset(minus_half[:, :], -0.5).then_inc(const, 1)
            nc.gpsimd.memset(hid[:, :, FI:HC], 0.0).then_inc(const, 1)
            pool.wait_ge(const, 6)
            nc.gpsimd.affine_select(out=ident[:, :], in_=ident[:, :], compare_op=ALU.not_equal, fill=1.0,
                                    base=0, pattern=[[-1, P]], channel_multiplier=1).then_inc(const, 1)
            nc.gpsimd.affine_select(out=before[:, :], in_=before[:, :], compare_op=ALU.is_gt, fill=0.0,
                                    base=0, pattern=[[1, P]], channel_multiplier=-1).then_inc(const, 1)
            nc.gpsimd.iota(order[:, :, :], pattern=[[0, TT], [-1, NE]], base=NE, channel_multiplier=0,
                           allow_small_or_imprecise_dtypes=True).then_inc(const, 1)
            nc.gpsimd.iota(unit_no[:, :], pattern=[[1, UNITS]], base=-HALF, channel_multiplier=0,
                           allow_small_or_imprecise_dtypes=True).then_inc(const, 1)

            pool.wait_ge(small_in, 48)

            def bias(t, k, i):
                pool.wait_ge(x_ld[k], 16 * (i + 1))
                nc.gpsimd.tensor_tensor(x_in[:, k, :], x_in[:, k, :], ob[:, :], ALU.add).then_inc(biased, 1)
            pipeline(pool, bias, 0)

            def send(u, k, i):
                pool.wait_ge(send_ld[k], 2 * 16 * (i + 1))
                hold(pool, passed, slot_done, 2 * u + 1)
                for h in range(2):
                    for c in range(TOPK):
                        nc.gpsimd.indirect_dma_start(
                            out=rows_in, out_offset=bass.IndirectOffsetOnAxis(ap=to[:, k, c, h, :], axis=0),
                            in_=x_send[:, k, h, :], in_offset=None).then_inc(sent[k], 16)

            with pool.Fori(0, HALF // U) as i:
                for k in range(U):
                    send(i * U + k, k, i)

            def fetch(q, k):
                if not (isinstance(q, int) and q < U):
                    hold(pool, passed, f_step, F_STEPS * (q - U) + F_SUMS)
                hold(pool, passed, slot_done, 2 * (HALF + q) + 1)
                for h in range(2):
                    for c in range(TOPK):
                        nc.gpsimd.indirect_dma_start(
                            out=y_in[:, k, h, c, :], out_offset=None, in_=rows_out,
                            in_offset=bass.IndirectOffsetOnAxis(ap=to[:, k, c, h, :], axis=0)).then_inc(got[k], 16)

            def inverse(q, k):
                pool.wait_ge(f_step, F_STEPS * q + F_STEPS)
                nc.gpsimd.tensor_tensor(veps[:, k, :, :], mv2[:, k, :, 1:2],
                                        eps[:, :].rearrange("p (h o) -> p h o", h=1).broadcast_to([P, 2, 1]),
                                        ALU.add).then_inc(f_std, 1)
                pool.wait_ge(f_std, 2 * q + 1)
                nc.gpsimd.tensor_tensor(rstd2[:, k, :, :], veps[:, k, :, :],
                                        minus_half[:, :].rearrange("p (h o) -> p h o", h=1).broadcast_to([P, 2, 1]),
                                        ALU.pow).then_inc(f_std, 1)

            for k in range(U):
                pool.wait_ge(y_st[k], 16 * (LAST // U) + 16)
            for q in range(U):
                fetch(q, q)
            with pool.Fori(1, HALF // U) as i:
                for k in range(U):
                    fetch(i * U + k, k)
                    inverse(i * U + k - U, k)
            for k in range(U):
                inverse(HALF - U + k, k)

        @block.scalar
        def _(act):
            act.wait_ge(const, 10)
            for s in (*y_st, *x1_st, *o_st):
                act.sem_inc(s, 16)

            def turned_ctx(t, k):
                act.wait_ge(cturn, t + 1)
                wait(act, proj, t - 1)
                nc.scalar.activation(cT[:, k % 2, :, :], ct_banks[k % 2], ACT.Copy).then_inc(c_ev, 1)

            def sqrt(t, k):
                act.wait_ge(r_step, 3 * t + 3)
                nc.scalar.activation(std[:, k, :], mv[:, k, 1:2], ACT.Sqrt, bias=eps[:, 0:1]).then_inc(std_done, 1)

            def turned_x1(t, k):
                act.wait_ge(xturn, t + 1)
                wait(act, logit, t - 1)
                nc.scalar.activation(x1T[:, k % 2, :, :], xt_banks[k % 2], ACT.Copy).then_inc(xt_ev, 1)

            def first_part(t, k, i):
                if live(t - 4):
                    turned_x1(t - 4, (k - 4) % U)
                if live(t):
                    turned_ctx(t, k)
                if live(t - 2):
                    sqrt(t - 2, (k - 2) % U)
            pipeline(act, first_part, 4)

            act.wait_ge(rt, R_SUB)
            nc.scalar.activation(probs[:, :, :], rest[:, :, :], ACT.Exp).then_inc(rexp, 1)
            nc.scalar.activation(tops[:, 4, :, :], logits[:, :, NE:NG], ACT.Exp, scale=-1.0).then_inc(rexp, 1)

            def turned_unit(u, k):
                act.wait_ge(uturn, u + 1)
                wait(act, gu, u - 1)
                nc.scalar.activation(uT[:, k % 2, :, :], ps_t[:, :, :], ACT.Copy).then_inc(ut_ev, 1)

            def gate(u, k):
                act.wait_ge(gu, u + 1)
                wait(act, h_done, u - 1)
                nc.scalar.activation(silu[:, k % 2, :], ps_g[:, 0:FI], ACT.Silu).then_inc(silu_done, 1)

            def turned_hidden(u, k):
                act.wait_ge(hturn, u + 1)
                wait(act, down, u - 1)
                nc.scalar.activation(hT[:, k % 2, :, :], ps_h[:, :, :], ACT.Copy).then_inc(ht_ev, 1)

            def result(u, k, i):
                act.wait_ge(down, u + 1)
                act.wait_ge(y_st[k], 16 * i + 16)
                nc.scalar.activation(u_out[:, k, :], ps_y[:, 0:D], ACT.Copy).then_inc(y_ev, 1)

            def normalise(q, k, i):
                act.wait_ge(f_shift, q + 1)
                act.wait_ge(o_st[k], 2 * 16 * i + 16)
                for h in range(2):
                    nc.scalar.activation(normed[:, k, h, :], sums[:, k, h, :], ACT.Identity,
                                         bias=shift[:, k, h, :], scale=rstd2[:, k, h, :]).then_inc(f_norm, 1)

            def unit(u, k, i, ph):
                if phase(u - 2, ph) is not None:
                    turned_hidden(u - 2, (k - 2) % U)
                if phase(u - 1, ph) is not None:
                    gate(u - 1, (k - 1) % U)
                if phase(u, ph) is not None:
                    turned_unit(u, k)
                if phase(u - 6, ph) == SUM:
                    normalise(u - 6 - LAST, (k - 6) % U, body(k, i, 6) - LAST // U)
                if phase(u - 2, ph) == EXPERTS:
                    result(u - 2, (k - 2) % U, body(k, i, 2))
            units(act, unit, 6, peel=2)

        @block.vector
        def _(dve):
            V = nc.vector

            def residual(t, k):
                dve.wait_ge(proj, t + 1)
                dve.wait_ge(biased, t + 1)
                wait(dve, n_step, 2 * (t - U) + 2)
                V.tensor_tensor(res[:, k, :], pr_banks[k % 2], x_in[:, k, :], ALU.add).then_inc(r_step, 1)

            def statistics(t, k):
                dve.wait_ge(r_step, 3 * t + 1)
                V.bn_stats(stats[:, k, :], res[:, k, :]).then_inc(r_step, 1)

            def variance(t, k):
                hold(dve, passed, r_step, 3 * t + 2)
                V.bn_aggr(mv[:, k, :], stats[:, k, :]).then_inc(r_step, 1)

            def inverse(t, k):
                dve.wait_ge(std_done, t + 1)
                V.reciprocal(rstd[:, k, :], std[:, k, :]).then_inc(n_step, 1)

            def normalise(t, k, i):
                dve.wait_ge(n_step, 2 * t + 1)
                wait(dve, x1_st[k], 16 * i + 16)
                wait(dve, xturn, t - U + 1)
                V.tensor_scalar(x1[:, k, :], res[:, k, :], mv[:, k, 0:1], rstd[:, k, 0:1],
                                ALU.subtract, ALU.mult).then_inc(n_step, 1)

            def take_logits(t, k):
                dve.wait_ge(logit, t + 1)
                V.tensor_copy(logits[:, bass.ds(t, 1), :].rearrange("p t e -> p (t e)"),
                              lo_banks[k % 2]).then_inc(l_ev, 1)

            def first_part(t, k, i):
                if live(t - 2):
                    residual(t - 2, (k - 2) % U)
                if live(t - 3):
                    inverse(t - 3, (k - 3) % U)
                if live(t - 5):
                    take_logits(t - 5, (k - 5) % U)
                if live(t - 2):
                    statistics(t - 2, (k - 2) % U)
                if live(t - 3):
                    normalise(t - 3, (k - 3) % U, body(k, i, 3))
                if live(t - 2):
                    variance(t - 2, (k - 2) % U)
            pipeline(dve, first_part, 5)

            n = [0]

            def r(op):
                n[0] += 1
                op.then_inc(rt, 1)
                dve.wait_ge(rt, n[0])

            def wide_of(a):
                return a.broadcast_to(wide)

            dve.wait_ge(l_ev, TT)
            lg = logits[:, :, 0:NE]
            r(V.tensor_reduce(tops[:, 0, :, :], lg, AX.X, ALU.max))
            r(V.tensor_tensor(rest[:, :, :], lg, wide_of(tops[:, 0, :, :]), ALU.subtract))
            assert n[0] == R_SUB
            dve.wait_ge(rexp, 2)
            r(V.tensor_reduce(tops[:, 1, :, :], probs[:, :, :], AX.X, ALU.add))
            r(V.reciprocal(tops[:, 0, :, :], tops[:, 1, :, :]))
            r(V.tensor_tensor(probs[:, :, :], probs[:, :, :], wide_of(tops[:, 0, :, :]), ALU.mult))
            r(V.tensor_scalar(tops[:, 4, :, :], tops[:, 4, :, :], 1.0, None, ALU.add))
            r(V.reciprocal(weights[:, 2, :, :], tops[:, 4, :, :]))

            def choose(of, top, mask):
                r(V.tensor_reduce(top, of[:, :, :], AX.X, ALU.max))
                r(V.tensor_tensor(score[:, :, :], of[:, :, :], wide_of(top), ALU.is_equal))
                r(V.tensor_tensor(score[:, :, :], score[:, :, :], order[:, :, :], ALU.mult))
                r(V.tensor_reduce(tops[:, 3, :, :], score[:, :, :], AX.X, ALU.max))
                r(V.tensor_tensor(mask[:, :, :], score[:, :, :], wide_of(tops[:, 3, :, :]), ALU.is_equal))

            choose(probs, tops[:, 0, :, :], first)
            r(V.scalar_tensor_tensor(rest[:, :, :], first[:, :, :], -2.0, probs[:, :, :], ALU.mult, ALU.add))
            choose(rest, tops[:, 1, :, :], second)
            r(V.tensor_tensor(tops[:, 2, :, :], tops[:, 0, :, :], tops[:, 1, :, :], ALU.add))
            r(V.reciprocal(tops[:, 3, :, :], tops[:, 2, :, :]))
            for c in range(TOPK):
                r(V.tensor_tensor(weights[:, c, :, :], tops[:, c, :, :], tops[:, 3, :, :], ALU.mult))
            r(V.tensor_tensor(chosen[:, :, :], first[:, :, :], second[:, :, :], ALU.add))
            assert n[0] == R_CHOSEN
            dve.wait_ge(rcount, 2)
            totals = ps_u[:, 0:TT * NE].rearrange("p (t e) -> p t e", e=NE)
            inside = ps_g[:, 0:TT * NE].rearrange("p (t e) -> p t e", e=NE)
            r(V.tensor_copy(scan[0][:, :, :], totals))
            s, d = 0, 1
            while d < TT:
                r(V.tensor_copy(scan[1 - s][:, 0:d, :], scan[s][:, 0:d, :]))
                r(V.tensor_tensor(scan[1 - s][:, d:TT, :], scan[s][:, d:TT, :], scan[s][:, 0:TT - d, :], ALU.add))
                s, d = 1 - s, 2 * d
            r(V.tensor_tensor(place[:, :, :], scan[s][:, :, :], totals, ALU.subtract))
            r(V.tensor_tensor(place[:, :, :], place[:, :, :], inside, ALU.add))
            r(V.tensor_scalar(need[:, 0, :], scan[s][:, TT - 1, :], float(P - 1), None, ALU.add))
            r(V.tensor_copy(need_i[:, 0, :], need[:, 0, :]))
            r(V.tensor_scalar(need_i[:, 1, :], need_i[:, 0, :], P.bit_length() - 1, None, ALU.arith_shift_right))
            r(V.tensor_copy(need[:, 1, :], need_i[:, 1, :]))
            r(V.tensor_copy(need[:, 0, :], need_i[:, 1, :]))
            a, d = 1, 1
            while d < NE:
                b = 3 - a
                r(V.tensor_copy(need[:, b, 0:d], need[:, a, 0:d]))
                r(V.tensor_tensor(need[:, b, d:NE], need[:, a, d:NE], need[:, a, 0:NE - d], ALU.add))
                a, d = b, 2 * d
            r(V.tensor_tensor(need[:, 3, :], need[:, a, :], need[:, 0, :], ALU.subtract))
            r(V.tensor_scalar(need[:, 3, :], need[:, 3, :], float(P), None, ALU.mult))
            r(V.tensor_tensor(place[:, :, :], place[:, :, :],
                              need[:, 3:4, :].broadcast_to(wide), ALU.add))
            for c, mask in enumerate((first, second)):
                r(V.tensor_tensor(score[:, :, :], place[:, :, :], mask[:, :, :], ALU.mult))
                r(V.tensor_reduce(posf[:, c, :], score[:, :, :], AX.X, ALU.add))
            r(V.tensor_copy(pos[:, :, :], posf[:, :, :]))
            r(V.tensor_scalar(unit_ex[:, 0, :], unit_no[:, :], 0.0, float(NE), ALU.is_lt, ALU.mult))
            for e in range(NE):
                r(V.scalar_tensor_tensor(unit_ex[:, (e + 1) % 2, :], unit_no[:, :], need[0:1, a, e:e + 1],
                                         unit_ex[:, e % 2, :], ALU.is_ge, ALU.add))
            r(V.tensor_copy(unit_tab[:, :], unit_ex[:, NE % 2, :]))
            assert n[0] == R_ALL, n[0]

            def split_pos(a):
                return a.rearrange("p c (h t) -> p c h t", h=2)

            def slots(u, k, i, ph):
                t = u if ph == SEND else u - LAST
                if ph == SEND:
                    wait(dve, sent[k], 2 * TOPK * 16 * i)
                    wait(dve, y_ev, u - U + 1)
                else:
                    wait(dve, got[k], 2 * TOPK * 16 * (i - LAST // U))
                    wait(dve, f_step, F_STEPS * (t - U) + F_SUMS)
                V.tensor_copy(to[:, k, :, :, :], split_pos(pos[:, :, :])[:, :, :, bass.ds(t, 1)]).then_inc(slot_done, 1)
                V.tensor_copy(wsl[:, k, :, :, :],
                              split_pos(weights[:, :, :, :].rearrange("p c t o -> p c (t o)"))[:, :, :, bass.ds(t, 1)]
                              ).then_inc(slot_done, 1)

            def hidden(u, k):
                dve.wait_ge(silu_done, u + 1)
                wait(dve, hturn, u - 1)
                V.tensor_tensor(hid[:, k % 2, 0:FI], silu[:, k % 2, :], ps_u[:, 0:FI], ALU.mult).then_inc(h_done, 1)

            def shared_result(u, k, i, ph):
                dve.wait_ge(down, u + 1)
                if ph == SEND:
                    dve.wait_ge(slot_done, 2 * u + 2)
                    dve.wait_ge(y_st[k], 16 * i + 16)
                    into, h = u_out[:, k, :], 0
                else:
                    q = u - LAST
                    dve.wait_ge(slot_done, 2 * (HALF + q) + 2)
                    wait(dve, f_norm, 2 * (q - U) + 2)
                    into, h = sums[:, k, 1, :], 1
                V.scalar_tensor_tensor(into, ps_y[:, 0:D], wsl[:, k, 2, h, :], u_in[:, k, :],
                                       ALU.mult, ALU.add).then_inc(y_ev, 1)

            def add_experts(q, k, i):
                dve.wait_ge(got[k], 2 * TOPK * 16 * (i + 1))
                dve.wait_ge(s_ld[k], 16 * (i + 1))
                dve.wait_ge(y_ev, q + LAST + 1)
                for c in range(TOPK):
                    for h in range(2):
                        if c:
                            dve.wait_ge(f_step, F_STEPS * q + 1 + h)
                        old = s_in[:, k, :] if (c, h) == (0, 0) else sums[:, k, h, :]
                        V.scalar_tensor_tensor(sums[:, k, h, :], y_in[:, k, h, c, :], wsl[:, k, c, h, :], old,
                                               ALU.mult, ALU.add).then_inc(f_step, 1)

            def statistics2(q, k):
                for h in range(2):
                    dve.wait_ge(f_step, F_STEPS * q + 3 + h)
                    V.bn_stats(stats2[:, k, h, :], sums[:, k, h, :]).then_inc(f_step, 1)
                for h in range(2):
                    hold(dve, passed, f_step, F_STEPS * q + 5 + h)
                    V.bn_aggr(mv2[:, k, h, :], stats2[:, k, h, :]).then_inc(f_step, 1)

            def mean_shift(q, k):
                dve.wait_ge(f_std, 2 * q + 2)
                V.scalar_tensor_tensor(shift[:, k, :, :], mv2[:, k, :, 0:1], -1.0, rstd2[:, k, :, :],
                                       ALU.mult, ALU.mult).then_inc(f_shift, 1)

            def unit(u, k, i, ph):
                p3 = phase(u - 3, ph)
                if p3 in (SEND, SUM):
                    shared_result(u - 3, (k - 3) % U, body(k, i, 3), p3)
                if phase(u - 4, ph) == SUM:
                    add_experts(u - 4 - LAST, k, i - 1 - LAST // U)
                if phase(u, ph) in (SEND, SUM):
                    slots(u, k, i, phase(u, ph))
                if phase(u - 1, ph) is not None:
                    hidden(u - 1, (k - 1) % U)
                if phase(u - 4, ph) == SUM:
                    statistics2(u - 4 - LAST, k)
                if phase(u - 6, ph) == SUM:
                    mean_shift(u - 6 - LAST, (k - 6) % U)
            units(dve, unit, 6, peel=2)

        @block.tensor
        def _(pe):
            pe.wait_ge(const, 7)
            pe.wait_ge(small_in, 48)

            def turn_ctx(t, k, i):
                pe.wait_ge(c_ld[k], 16 * (i + 1))
                wait(pe, c_ev, t - 1)
                for d in range(DK):
                    mm = pe.transpose(ct_banks[k % 2][:, d, :], c_in[:, k, d * P:(d + 1) * P], ident[:, :])
                mm.then_inc(cturn, 1)

            def project(t, k):
                pe.wait_ge(c_ev, t + 1)
                wait(pe, r_step, 3 * (t - 2) + 1)
                for d in range(DK):
                    mm = pe.matmul(pr_banks[k % 2], cT[:, k % 2, d, :], wo[:, d, :], start=(d == 0), stop=(d == DK - 1))
                mm.then_inc(proj, 1)

            def turn_x1(t, k):
                pe.wait_ge(n_step, 2 * t + 2)
                wait(pe, xt_ev, t - 1)
                for d in range(DK):
                    mm = pe.transpose(xt_banks[k % 2][:, d, :], x1[:, k, d * P:(d + 1) * P], ident[:, :])
                mm.then_inc(xturn, 1)

            def route(t, k):
                pe.wait_ge(xt_ev, t + 1)
                wait(pe, l_ev, t - 1)
                for d in range(DK):
                    mm = pe.matmul(lo_banks[k % 2], x1T[:, k % 2, d, :], gates[:, d, :],
                                   start=(d == 0), stop=(d == DK - 1))
                mm.then_inc(logit, 1)

            def first_part(t, k, i):
                if live(t - 4):
                    turn_x1(t - 4, (k - 4) % U)
                if live(t):
                    turn_ctx(t, k, i)
                if live(t - 1):
                    project(t - 1, (k - 1) % U)
                if live(t - 4):
                    route(t - 4, (k - 4) % U)
            pipeline(pe, first_part, 4)

            pe.wait_ge(const, 10)
            pe.wait_ge(rt, R_CHOSEN)
            flat = chosen[:, :, :].rearrange("p t e -> p (t e)")
            pe.matmul(ps_g[:, 0:TT * NE], before[:, :], flat, start=True, stop=True).then_inc(rcount, 1)
            pe.matmul(ps_u[:, 0:TT * NE], ones[:, :], flat, start=True, stop=True).then_inc(rcount, 1)

            def turn_unit(u, k, i):
                pe.wait_ge(u_ld[k], 16 * (i + 1))
                wait(pe, ut_ev, u)
                for d in range(DK):
                    mm = pe.transpose(ps_t[:, d, :], u_in[:, k, d * P:(d + 1) * P], ident[:, :])
                mm.then_inc(uturn, 1)

            def expert_of(u):
                return pe.value_load(unit_tab[0:1, bass.ds(u, 1)], min_val=0, max_val=NE)

            def gate_up(u, k, e):
                pe.wait_ge(ut_ev, u + 1)
                wait(pe, h_done, u)
                for w, bank in ((wg, ps_g), (wu, ps_u)):
                    for d in range(DK):
                        mm = pe.matmul(bank[:, 0:FI], uT[:, k % 2, d, :],
                                       w[:, d, bass.ds(e, 1), :].rearrange("p e n -> p (e n)"),
                                       start=(d == 0), stop=(d == DK - 1))
                mm.then_inc(gu, 1)

            def turn_hidden(u, k):
                pe.wait_ge(h_done, u + 1)
                wait(pe, ht_ev, u)
                for c in range(NC):
                    mm = pe.transpose(ps_h[:, c, :], hid[:, k % 2, c * P:(c + 1) * P], ident[:, :])
                mm.then_inc(hturn, 1)

            def project_down(u, k, e):
                pe.wait_ge(ht_ev, u + 1)
                wait(pe, y_ev, u)
                for c, (_, n) in enumerate(FCH):
                    mm = pe.matmul(ps_y[:, 0:D], hT[0:n, k % 2, c, :],
                                   wd[0:n, c, bass.ds(e, 1), :].rearrange("p e n -> p (e n)"),
                                   start=(c == 0), stop=(c == NC - 1))
                mm.then_inc(down, 1)

            def unit(u, k, i):
                before_last = expert_of(u - 2) if live_unit(u - 2) else None
                last = expert_of(u - 1) if live_unit(u - 1) else None
                if live_unit(u - 2):
                    turn_hidden(u - 2, (k - 2) % U)
                if live_unit(u - 1):
                    gate_up(u - 1, (k - 1) % U, last)
                if live_unit(u):
                    turn_unit(u, k, i)
                if live_unit(u - 2):
                    project_down(u - 2, (k - 2) % U, before_last)

            def live_unit(u):
                return not isinstance(u, int) or 0 <= u < UNITS

            pe.wait_ge(big_in, 16 * U * (NE + 1))
            pe.wait_ge(rt, R_ALL)
            for k in range(U):
                unit(k, k, 0)
            with pe.Fori(1, UNITS // U) as i:
                for k in range(U):
                    unit(i * U + k, k, i)
            for k in range(2):
                unit(UNITS + k, k, UNITS // U)


_INS = ["x", "xT", "wqkT", "wvT", "qk_b", "v_b", "outT", "out_b", "gatesT", "w_gate", "w_up", "w_down"]


def build(nc, ins, out):
    B, D, S = ins["xT"].shape
    T = B * S
    NE = ins["w_gate"].shape[0] - 1
    TOPK = 2
    routed = T // P * TOPK + NE
    ctx_d = nc.dram_tensor("ctx_d", (B, S, D), F32).ap()
    qk_parts = nc.dram_tensor("qk_parts", (2, 3, D, S), BF16).ap()
    x1_rows = nc.dram_tensor("x1_rows", (T, D), F32).ap()
    shared_rows = nc.dram_tensor("shared_rows", (T // 2, D), F32).ap()
    rows_in = nc.dram_tensor("rows_in", (routed * P, D), F32).ap()
    rows_out = nc.dram_tensor("rows_out", (routed * P, D), F32).ap()

    for part in range(2):
        with ExitStack() as sems:
            def sem(name):
                return sems.enter_context(nc.semaphore(("at_", "ff_")[part] + name))

            if part == 0:
                attention(nc, ins["xT"], ins["wqkT"], ins["wvT"], ins["qk_b"], ins["v_b"], ctx_d, qk_parts,
                          rows_in, sem)
            else:
                feed_forward(nc, ins["x"], ctx_d.rearrange("b s d -> (b s) d"), ins["outT"], ins["out_b"],
                             ins["gatesT"], ins["w_gate"], ins["w_up"], ins["w_down"], x1_rows, shared_rows, rows_in,
                             rows_out,
                             out.rearrange("b s d -> (b s) d"), sem)


def kernel(L0_attn_x, L0_attn_qkv_w, L0_attn_qkv_b, L0_attn_out_w, L0_attn_out_b, L0_ffn_gate_w, L0_ffn_w_gate,
           L0_ffn_w_up, L0_ffn_w_down, L0_ffn_sw_gate, L0_ffn_sw_up, L0_ffn_sw_down, L0_ffn_shared_gate_w):
    import numpy as np
    import concourse.bacc as bacc
    from concourse.bass_utils import run_bass_kernel_spmd

    x = np.asarray(L0_attn_x)
    B, S, D = x.shape
    qkv_w, qkv_b = np.asarray(L0_attn_qkv_w), np.asarray(L0_attn_qkv_b)
    arrays = {
        "x": x.reshape(B * S, D),
        "xT": x.transpose(0, 2, 1),
        "wqkT": qkv_w[:2 * D].T,
        "wvT": qkv_w[2 * D:].T,
        "qk_b": qkv_b[:2 * D].reshape(-1, P).T,
        "v_b": qkv_b[2 * D:],
        "outT": np.asarray(L0_attn_out_w).T,
        "out_b": np.asarray(L0_attn_out_b),
        "gatesT": np.concatenate([np.asarray(L0_ffn_gate_w), np.asarray(L0_ffn_shared_gate_w)]).T,
        "w_gate": np.concatenate([np.asarray(L0_ffn_w_gate), np.asarray(L0_ffn_sw_gate)[None]]),
        "w_up": np.concatenate([np.asarray(L0_ffn_w_up), np.asarray(L0_ffn_sw_up)[None]]),
        "w_down": np.concatenate([np.asarray(L0_ffn_w_down), np.asarray(L0_ffn_sw_down)[None]]),
    }
    nc = bacc.Bacc("TRN2", target_bir_lowering=False, num_devices=1)
    ins = {}
    for name in _INS:
        arrays[name] = np.ascontiguousarray(arrays[name])
        ins[name] = nc.dram_tensor(f"in_{name}", arrays[name].shape, mybir.dt.from_np(arrays[name].dtype),
                                   kind="ExternalInput").ap()
    out = nc.dram_tensor("out", (B, S, D), F32, kind="ExternalOutput").ap()
    build(nc, ins, out)
    r = run_bass_kernel_spmd(nc, [{f"in_{name}": arrays[name] for name in _INS}], core_ids=[0])
    return r.results[0]["out"]
```

```python
from contextlib import ExitStack

import concourse.bass as bass
from concourse import mybir

F32 = mybir.dt.float32
BF16 = mybir.dt.bfloat16
ALU = mybir.AluOpType
ACT = mybir.ActivationFunctionType
AX = mybir.AxisListType
F32R = mybir.dt.float32r

P = 128
NH = 16
HD = 16
MM_N = 512
VW = 32

Q_PART = (0, 0, 0, 1, 1, 2)
K_PART = (0, 1, 2, 0, 1, 0)
KS = len(Q_PART) * HD
MROWS = 3

HI, LO = 0, 1
THREE = ((LO, HI), (HI, LO), (HI, HI))


def hold(eng, passed, s, value):
    eng.wait_ge(s, value)
    eng.sem_inc(passed, 1)


def attention(nc, xT, wqkT, wvT, qk_b, v_b, ctx_out, qk_parts, blank, sem):
    B, D, S = xT.shape
    DK = D // P
    NT = S // P
    NHALF = S // MM_N
    NQK = 2 * D // P
    RING = 8
    QC = S // 4
    SCALE = 1.0 / HD ** 0.5
    PAIRS = NH // 2
    NCH = NT + NQK * NHALF
    TILES = (0, 2, 1, 3)

    with ExitStack() as ctx:
        def sb(name, shape, dt=F32):
            return ctx.enter_context(nc.sbuf_tensor(name, shape, dt))

        def pb(name, shape, dt=F32):
            return ctx.enter_context(nc.psum_tensor(name, shape, dt))

        q_aug = sb("q_aug", [P, NH, S], BF16)
        k_aug = sb("k_aug", [P, NH, S], BF16)
        probs = sb("probs", [P, RING, S])
        qk_sb = sb("qk_sb", [P, NQK, S])
        parts = sb("parts", [P, 2, 3, S], BF16)
        PARTS = ("hi", "lo")
        x_v = [sb(f"x_v_{p}", [P, DK, S], F32R) for p in PARTS]
        x_qk = [sb(f"x_qk_{p}", [P, DK, S], F32R) for p in PARTS]
        wqk_sb = [sb(f"wqk_{p}", [P, DK, 2 * D], F32R) for p in PARTS]
        wv_sb = [sb(f"wv_{p}", [P, DK, D], F32R) for p in PARTS]
        x_raw = sb("x_raw", [P, DK, S])
        wqk_raw = probs[:, 0, :].rearrange("p (c n) -> p c n", c=DK)
        wv_raw = probs[:, 1, 0:DK * D].rearrange("p (c n) -> p c n", c=DK)
        x_first = probs[:, 2:2 + DK, :]
        qkb_sb = sb("qkb_sb", [P, NQK])
        vb_sb = sb("vb_sb", [P, D])
        v_sb = sb("v_sb", [P, NT, D])
        v_st = sb("v_st", [P, 2, NT, VW])
        ctx_sb = sb("ctx_sb", [P, NT, D])
        o_sb = sb("o_sb", [P, 2, QC])
        rden = sb("rden", [P, 2, 2, 4, 1])
        rmax = sb("rmax", [P, 2, NT])
        rres = sb("rres", [P, 2, NT])
        mparts = sb("mparts", [P, 2, MROWS, NT], BF16)
        m_rows = sb("m_rows", [MROWS * NT, 2, P], BF16)
        zeros = sb("zeros", [P, D])
        identf = sb("identf", [P, P])
        identb = sb("identb", [P, P], BF16)

        ps_rows = [pb(f"ps_rows{i}", [P, S]) for i in range(2)]
        ps_cols = [pb(f"ps_cols{i}", [P, MM_N]) for i in range(2)]
        ps_o = pb("ps_o", [P, QC])
        ps_misc = pb("ps_misc", [P, MM_N])
        ps_m = ps_misc[0:MROWS * NT, 256:256 + P // 2].bitcast(BF16)
        ps_ot = ps_misc[:, 0:256].rearrange("p (j n) -> p j n", j=2)

        w_in = sem("w_in")
        first_in = sem("first_in")
        raw_in = sem("raw_in")
        w_split = sem("w_split")
        w_ready = sem("w_ready")
        xv_ready = sem("xv_ready")
        xq_ready = sem("xq_ready")
        const = sem("const")
        chunk_done = sem("chunk_done")
        v_ev = sem("v_ev")
        qk_ev = sem("qk_ev")
        split_step = sem("split_step")
        parts_out = [sem(f"parts_out{i}") for i in range(2)]
        aug_in = [sem(f"aug_in{i}") for i in range(2)]
        rows_done = sem("rows_done")
        rows_free = sem("rows_free")
        cols_done = sem("cols_done")
        exp_done = sem("exp_done")
        pv_done = sem("pv_done")
        v_staged = sem("v_staged")
        o_ev = sem("o_ev")
        ot_done = sem("ot_done")
        norm_done = sem("norm_done")
        norm_step = sem("norm_step")
        dve_step = sem("dve_step")
        m_split = sem("m_split")
        mt_done = sem("mt_done")
        m_ev = sem("m_ev")
        m_in = [sem(f"m_in{i}") for i in range(2)]
        passed = sem("passed")
        ctx_st = sem("ctx_st")
        blanked = sem("blanked")

        half = [slice(0, NH // 2), slice(NH // 2, NH)]

        def split(ns, eng, nb, i, step):
            t = TILES[i]
            src = qk_sb[:, t, :]
            pt = parts[:, i % 2, :, :]
            zero = zeros[:, 0:1].broadcast_to([P, S])
            if step == 0:
                eng.wait_ge(qk_ev, nb * NQK * NHALF + 2 * t + 2)
                if i >= 2:
                    eng.wait_ge(parts_out[i % 2], nb * 32 + 16)
                else:
                    eng.wait_ge(parts_out[i % 2], nb * 32)
            for c in (0, 1) if step == 0 else (2, 3):
                if not (step == 0 and c == 0):
                    eng.wait_ge(split_step, nb * 16 + 4 * i + c)
                if c == 0:
                    op = ns.tensor_tensor(pt[:, 0, :], src, zero, ALU.add)
                elif c == 1:
                    op = ns.tensor_tensor(src, src, pt[:, 0, :], ALU.subtract)
                elif c == 2:
                    op = ns.tensor_tensor(pt[:, 1, :], src, zero, ALU.add)
                else:
                    op = ns.tensor_tensor(pt[:, 2, :], src, pt[:, 1, :], ALU.subtract)
                op.then_inc(split_step, 1)

        block = ctx.enter_context(nc.Block())

        @block.sync
        def _(sp):
            def xT_of(b):
                return xT[b].rearrange("(c p) n -> p c n", p=P)

            sp.dma_start(wqk_raw, wqkT.rearrange("(c p) n -> p c n", p=P)).then_inc(w_in, 16)
            sp.dma_start(x_first, xT_of(0)).then_inc(first_in, 16)
            sp.dma_start(qkb_sb[:, :], qk_b).then_inc(w_in, 16)
            sp.dma_start(wv_raw, wvT.rearrange("(c p) n -> p c n", p=P)).then_inc(w_in, 16)
            sp.dma_start(vb_sb[:, :], v_b.partition_broadcast(P)).then_inc(w_in, 16)
            sp.dma_start(x_raw[:, :, :], xT_of(1)).then_inc(raw_in, 16)

            def store_parts(nb, i):
                t = TILES[i]
                side, hf = t // 2, t % 2
                hold(sp, passed, split_step, nb * 16 + 4 * i + 4)
                hold(sp, passed, aug_in[hf], nb * 192)
                dst = qk_parts[side, :, hf * P:(hf + 1) * P, :].rearrange("c p s -> p c s")
                sp.dma_start(dst, parts[:, i % 2, :, :]).then_inc(parts_out[i % 2], 16)

            def load_aug(nb, hf, first=False):
                for i in (2 * hf, 2 * hf + 1):
                    hold(sp, passed, parts_out[i % 2], nb * 32 + 16 * (i // 2) + 16)
                if not first:
                    sp.wait_ge(cols_done, (nb - 1) * 256 + (hf + 1) * 128)
                for side, (aug, part) in enumerate(((q_aug, Q_PART), (k_aug, K_PART))):
                    for j, c in enumerate(part):
                        src = qk_parts[side, c, hf * P:(hf + 1) * P, :].rearrange("(h d) s -> d h s", d=HD)
                        sp.dma_start(aug[HD * j:HD * j + HD, half[hf], :], src).then_inc(aug_in[hf], 16)

            for i in range(NQK):
                store_parts(0, i)
                if i % 2:
                    load_aug(0, i // 2, True)

            def batch(b, prep, xq):
                def rows(h, k):
                    sp.wait_ge(m_ev, b * NH + h + 1)
                    for r in range(MROWS):
                        sp.dma_start(q_aug[KS + r:KS + r + 1, bass.ds(h, 1), :].rearrange("r h s -> r (h s)"),
                                     m_rows[NT * r:NT * (r + 1), k, :]).then_inc(m_in[k], 16)

                rows(0, 0)
                if prep:
                    sp.wait_ge(xq_ready, 2 * (b + 2))
                    sp.dma_start(x_raw[:, :, :], xT_of(b + 1)).then_inc(raw_in, 16)
                rows_b = blank.shape[0] // B
                for h in range(NH - 1):
                    rows(h + 1, (h + 1) % 2)
                    for j in range(h, rows_b // P, NH - 1):
                        sp.dma_start(blank[bass.ds(b * rows_b + j * P, P), :], zeros[:, :]).then_inc(blanked, 16)
                    if prep and h in (2, 4, 6, 8):
                        store_parts(b + 1, h // 2 - 1)
                    if prep and h == 9:
                        load_aug(b + 1, 0)
                    if xq and h == 11:
                        sp.wait_ge(xv_ready, 2 * (b + 2))
                        sp.dma_start(x_raw[:, :, :], xT_of(b + 2)).then_inc(raw_in, 16)
                sp.wait_ge(norm_done, b * NH + NH + 2)
                sp.dma_start(ctx_out[b].rearrange("(t p) d -> p t d", p=P), ctx_sb[:, :, :]).then_inc(ctx_st, 16)
                if prep:
                    load_aug(b + 1, 1)

            with sp.Fori(0, B - 2) as b:
                batch(b, True, True)
            batch(B - 2, True, False)
            batch(B - 1, False, False)
            sp.wait_ge(ctx_st, 16 * B + 16)
            sp.wait_ge(blanked, 16 * (blank.shape[0] // P))

        @block.gpsimd
        def _(pool):
            for m in (identf, identb, zeros):
                nc.gpsimd.memset(m[:, :], 0.0).then_inc(const, 1)
            nc.gpsimd.memset(v_st[:, :, :, HD + 1:VW], 0.0).then_inc(const, 1)
            nc.gpsimd.memset(v_st[:, :, :, HD:HD + 1], 1.0).then_inc(const, 1)
            pool.wait_ge(const, 5)
            nc.gpsimd.memset(k_aug[KS:KS + MROWS, :, :], -1.0).then_inc(const, 1)
            pool.wait_ge(const, 6)
            for m in (identf, identb):
                nc.gpsimd.affine_select(out=m[:, :], in_=m[:, :], compare_op=ALU.not_equal, fill=1.0,
                                        base=0, pattern=[[-1, P]], channel_multiplier=1).then_inc(const, 1)

            pool.sem_inc(v_staged, 1)

            def split_x(parts, ready, nb, part):
                if part == LO:
                    pool.wait_ge(ready, 2 * nb + 1)
                other = (zeros[:, 0:1].rearrange("p (c n) -> p c n", c=1).broadcast_to([P, DK, S])
                         if part == HI else parts[HI][:, :, :].bitcast(F32))
                nc.gpsimd.tensor_tensor(parts[part][:, :, :], x_raw[:, :, :], other,
                                        (ALU.add, ALU.subtract)[part]).then_inc(ready, 1)

            pool.wait_ge(const, 8)
            pool.wait_ge(w_in, 64)
            pool.wait_ge(raw_in, 16)
            pool.wait_ge(chunk_done, NQK * NHALF)
            for part in (HI, LO):
                split_x(x_qk, xq_ready, 1, part)

            def stage_v(b, h, k):
                n = b * NH + h
                pool.wait_ge(pv_done, 8 * n + 1)
                bias = vb_sb[:, h * HD:(h + 1) * HD].rearrange("p (t d) -> p t d", t=1)
                nc.gpsimd.tensor_tensor(v_st[:, k, :, 0:HD], v_sb[:, :, h * HD:(h + 1) * HD],
                                        bias.broadcast_to([P, NT, HD]), ALU.add).then_inc(v_staged, 1)

            def batch(b, prep, xq):
                pool.wait_ge(v_ev, NT * b + NT)
                stage_v(b, 0, 0)
                if prep:
                    for i in range(NQK):
                        stage_v(b, 2 * i + 1, 1)
                        split(nc.gpsimd, pool, b + 1, i, 0)
                        stage_v(b, 2 * i + 2, 0)
                        split(nc.gpsimd, pool, b + 1, i, 1)
                for h in range(9 if prep else 1, NH):
                    stage_v(b, h, h % 2)
                    if prep and h in (9, 10):
                        if h == 9:
                            pool.wait_ge(raw_in, 16 * (2 * b + 2))
                            pool.wait_ge(chunk_done, b * NCH + NCH + NCH - NT)
                        split_x(x_v, xv_ready, b + 1, h - 9)
                    if xq and h in (13, 14):
                        if h == 13:
                            pool.wait_ge(raw_in, 16 * (2 * b + 3))
                        split_x(x_qk, xq_ready, b + 2, h - 13)

            with pool.Fori(0, B - 2) as b:
                batch(b, True, True)
            batch(B - 2, True, False)
            batch(B - 1, False, False)

        @block.scalar
        def _(act):
            def evac_qk(nb, c):
                t, j = c // NHALF, c % NHALF
                act.wait_ge(chunk_done, nb * NCH + c + 1)
                if c == 0:
                    act.wait_ge(split_step, nb * 16)
                nc.scalar.activation(qk_sb[:, t, j * MM_N:(j + 1) * MM_N], ps_cols[c % 2][:, :], ACT.Identity,
                                     bias=qkb_sb[:, t:t + 1]).then_inc(qk_ev, 1)

            def evac_v(b, c):
                act.wait_ge(chunk_done, (b + 1) * NCH - NT + c + 1)
                if c == 0:
                    act.wait_ge(v_staged, b * NH + 1)
                nc.scalar.activation(v_sb[:, c, :], ps_cols[c % 2][:, 0:D], ACT.Copy).then_inc(v_ev, 1)

            def evac_o(b, h, k):
                n = b * NH + h
                act.wait_ge(pv_done, RING + 8 * n + 8)
                act.wait_ge(ot_done, n + 1)
                nc.scalar.activation(o_sb[:, k, :], ps_o[:, :], ACT.Copy).then_inc(o_ev, 1)

            def exps(b, h, k, first=False):
                for kt in range(NT):
                    n = (b * NH + h) * NT + kt
                    act.wait_ge(pv_done, n + 1)
                    for j in range(NHALF):
                        act.wait_ge(cols_done, 2 * n + j + 1)
                        nc.scalar.activation(probs[:, kt, j * MM_N:(j + 1) * MM_N], ps_cols[j][:, :],
                                             ACT.Exp, scale=SCALE).then_inc(exp_done, 1)
                    if kt == 0 and not first:
                        evac_o(b, h - 1, 1 - k)

            def batch(b, prep):
                for c in range(NT):
                    evac_v(b, c)
                if prep:
                    for c in range(NQK * NHALF):
                        evac_qk(b + 1, c)
                exps(b, 0, 0, True)
                exps(b, 1, 1)
                with act.Fori(1, PAIRS) as p:
                    exps(b, 2 * p, 0)
                    exps(b, 2 * p + 1, 1)
                evac_o(b, NH - 1, 1)

            act.wait_ge(w_in, 64)
            nc.scalar.activation(wqk_sb[HI][:, :, :], wqk_raw, ACT.Copy).then_inc(w_split, 1)
            act.wait_ge(first_in, 16)
            nc.scalar.activation(x_qk[HI][:, :, :], x_first, ACT.Copy).then_inc(xq_ready, 1)
            nc.scalar.activation(wv_sb[HI][:, :, :], wv_raw, ACT.Copy).then_inc(w_split, 1)
            nc.scalar.activation(x_v[HI][:, :, :], x_first, ACT.Copy).then_inc(xv_ready, 1)
            for c in range(NQK * NHALF):
                evac_qk(0, c)
            act.sem_inc(exp_done, 2)
            act.sem_inc(o_ev, 1)
            with act.Fori(0, B - 1) as b:
                batch(b, True)
            batch(B - 1, False)

        @block.vector
        def _(dve):
            dve.sem_inc(rows_free, 2)
            dve.sem_inc(norm_done, 2)
            for s, n, low, high, raw, done in ((w_split, 1, wqk_sb[LO], wqk_sb[HI], wqk_raw, w_ready),
                                               (xq_ready, 1, x_qk[LO], x_qk[HI], x_first, xq_ready),
                                               (w_split, 2, wv_sb[LO], wv_sb[HI], wv_raw, w_ready),
                                               (xv_ready, 1, x_v[LO], x_v[HI], x_first, xv_ready)):
                dve.wait_ge(s, n)
                nc.vector.tensor_tensor(low[:, :, :], raw, high[:, :, :].bitcast(F32), ALU.subtract).then_inc(done, 1)
            dve.wait_ge(const, 8)
            for i in range(NQK):
                split(nc.vector, dve, 0, i, 0)
                split(nc.vector, dve, 0, i, 1)

            def row_max(b, h, k, qt):
                n = (b * NH + h) * NT + qt
                dve.wait_ge(rows_done, n + 1)
                nc.vector.tensor_reduce(rmax[:, k, qt:qt + 1], ps_rows[qt % 2][:, :], AX.X,
                                        ALU.max).then_inc(rows_free, 1)

            def split_max(b, h, k):
                n = b * NH + h
                dve.wait_ge(rows_free, 2 + 8 * n + 8)
                nc.vector.tensor_copy(mparts[:, k, 0, :], rmax[:, k, :]).then_inc(dve_step, 1)
                dve.wait_ge(dve_step, 3 * n + 1)
                nc.vector.tensor_tensor(rres[:, k, :], rmax[:, k, :], mparts[:, k, 0, :],
                                        ALU.subtract).then_inc(dve_step, 1)
                dve.wait_ge(dve_step, 3 * n + 2)
                nc.vector.tensor_copy(mparts[:, k, 1, :], rres[:, k, :]).then_inc(dve_step, 1)
                dve.wait_ge(dve_step, 3 * n + 3)
                nc.vector.tensor_tensor(mparts[:, k, 2, :], rres[:, k, :], mparts[:, k, 1, :],
                                        ALU.subtract).then_inc(m_split, 1)

            def evac_m(b, h, k, hh):
                n = b * NH + h
                dve.wait_ge(mt_done, n + 1)
                dve.wait_ge(m_in[k], 16 + 48 * (b * (NH // 2) + hh))
                nc.vector.tensor_copy(m_rows[:, k, :], ps_m).then_inc(m_ev, 1)

            def norm(b, h, k):
                n = b * NH + h
                dve.wait_ge(ot_done, n + 3)
                view = ps_ot.rearrange("p j (c w) -> p j c w", w=VW)
                nc.vector.reciprocal(rden[:, k, :, :, :], view[:, :, :, HD:HD + 1]).then_inc(norm_step, 1)
                dve.wait_ge(norm_step, n + 1)
                out = ctx_sb[:, :, bass.ds(h * HD, HD)].rearrange("p (c j) d -> p j c d", j=2)
                nc.vector.tensor_tensor(out, view[:, :, :, 0:HD],
                                        rden[:, k, :, :, :].broadcast_to([P, 2, 4, HD]),
                                        ALU.mult).then_inc(norm_done, 1)

            def slot(b, h, k, hh, ahead, first):
                for qt in range(NT):
                    if ahead == 2:
                        row_max(b, h + 2, k, qt)
                    if qt == 2 and ahead >= 1:
                        evac_m(b, h + 1, 1 - k, hh)
                    if qt == 5 and not first:
                        norm(b, h - 1, 1 - k)
                if ahead == 2:
                    split_max(b, h + 2, k)

            def batch(b):
                for qt in range(NT):
                    row_max(b, 0, 0, qt)
                split_max(b, 0, 0)
                for qt in range(NT):
                    row_max(b, 1, 1, qt)
                    if qt == 4:
                        evac_m(b, 0, 0, 0)
                split_max(b, 1, 1)
                dve.wait_ge(ctx_st, 16 * b + 16)
                slot(b, 0, 0, 0, 2, True)
                slot(b, 1, 1, 1, 2, False)
                with dve.Fori(1, PAIRS - 1) as p:
                    slot(b, 2 * p, 0, p, 2, False)
                    slot(b, 2 * p + 1, 1, p + 1, 2, False)
                slot(b, NH - 2, 0, PAIRS - 1, 1, False)
                slot(b, NH - 1, 1, PAIRS, 0, False)
                norm(b, NH - 1, 1)

            with dve.Fori(0, B) as b:
                batch(b)

        @block.tensor
        def _(pe):
            def qk_chunk(nb, c):
                t, j = c // NHALF, c % NHALF
                if c >= 2:
                    pe.wait_ge(qk_ev, nb * NQK * NHALF + c - 1)
                for n, (x, w) in enumerate(THREE):
                    for d in range(DK):
                        mm = pe.matmul(ps_cols[c % 2][:, :], wqk_sb[w][:, d, t * P:(t + 1) * P],
                                       x_qk[x][:, d, j * MM_N:(j + 1) * MM_N],
                                       start=(n == d == 0), stop=(n == 2 and d == DK - 1))
                mm.then_inc(chunk_done, 1)

            def v_chunk(b, c):
                if c >= 2:
                    pe.wait_ge(v_ev, b * NT + c - 1)
                for n, (x, w) in enumerate(THREE):
                    for d in range(DK):
                        mm = pe.matmul(ps_cols[c % 2][:, 0:D], x_v[x][:, d, c * P:(c + 1) * P], wv_sb[w][:, d, :],
                                       start=(n == d == 0), stop=(n == 2 and d == DK - 1))
                mm.then_inc(chunk_done, 1)

            def rows(b, h, qt):
                n = (b * NH + h) * NT + qt
                pe.wait_ge(rows_free, n + 1)
                for j in range(NHALF):
                    mm = pe.matmul(ps_rows[qt % 2][:, j * MM_N:(j + 1) * MM_N],
                                   q_aug[0:KS, bass.ds(h, 1), qt * P:(qt + 1) * P].rearrange("p h s -> p (h s)"),
                                   k_aug[0:KS, bass.ds(h, 1), j * MM_N:(j + 1) * MM_N].rearrange("p h s -> p (h s)"),
                                   start=True, stop=True)
                mm.then_inc(rows_done, 1)

            def cols(b, h, kt):
                n = (b * NH + h) * NT + kt
                for j in range(NHALF):
                    pe.wait_ge(exp_done, 2 * n + j + 1)
                    pe.matmul(ps_cols[j][:, :],
                              k_aug[0:KS + MROWS, bass.ds(h, 1), kt * P:(kt + 1) * P].rearrange("p h s -> p (h s)"),
                              q_aug[0:KS + MROWS, bass.ds(h, 1), j * MM_N:(j + 1) * MM_N].rearrange("p h s -> p (h s)"),
                              start=True, stop=True).then_inc(cols_done, 1)

            def values(b, h, k, kt):
                n = b * NH + h
                if kt == 0:
                    pe.wait_ge(o_ev, n + 1)
                    pe.wait_ge(v_staged, n + 2)
                pe.wait_ge(exp_done, 2 * (n * NT + kt) + 4)
                for c in range(4):
                    mm = pe.matmul(ps_o[VW * c:VW * (c + 1), :], v_st[:, k, kt, :],
                                   probs[:, kt, c * QC:(c + 1) * QC], start=(kt == 0), stop=(kt == NT - 1),
                                   tile_position=(0, VW * c))
                mm.then_inc(pv_done, 1)

            def turn_max(b, h, k):
                n = b * NH + h
                pe.wait_ge(m_split, n + 1)
                pe.wait_ge(m_ev, n)
                pe.wait_ge(norm_done, n)
                pe.transpose(ps_m, mparts[:, k, :, :].rearrange("p c t -> p (c t)"), identb[:, :]).then_inc(mt_done, 1)

            def turn_o(b, h, k, m_evs):
                n = b * NH + h
                pe.wait_ge(o_ev, n + 2)
                pe.wait_ge(m_ev, b * NH + m_evs)
                pe.wait_ge(norm_done, n + 2)
                for j in range(2):
                    mm = pe.transpose(ps_ot[:, j, :], o_sb[:, k, j * P:(j + 1) * P], identf[:, :])
                mm.then_inc(ot_done, 1)

            def slot(b, h, k, hh, ahead, first):
                for kt in range(NT):
                    if kt == 0 and first:
                        rows(b, h + 2, 0)
                    if kt < NT - 1:
                        cols(b, h, kt + 1)
                    elif ahead >= 1:
                        pe.wait_ge(m_in[1 - k], 16 + 48 * (b * (NH // 2) + hh + 1))
                        cols(b, h + 1, 0)
                    if ahead == 2 and not (kt == 0 and first):
                        rows(b, h + 2, kt)
                    if kt == 2 and ahead >= 1:
                        turn_max(b, h + 1, 1 - k)
                    if kt == 5 and not first:
                        turn_o(b, h - 1, 1 - k, h + 2 if ahead >= 1 else NH)
                    values(b, h, k, kt)

            def batch(b, prep):
                pe.wait_ge(xv_ready, 2 * (b + 1))
                early = isinstance(b, int) and b == 0
                if early:
                    for c in range(NT):
                        v_chunk(b, c)
                pe.wait_ge(aug_in[0], 192 * (b + 1))
                for qt in range(NT):
                    rows(b, 0, qt)
                    if not early:
                        v_chunk(b, qt)
                if prep:
                    pe.wait_ge(xq_ready, 2 * (b + 2))
                for qt in range(NT):
                    if prep:
                        if qt < 2:
                            pe.wait_ge(v_ev, b * NT + NT - 1 + qt)
                        qk_chunk(b + 1, qt)
                    rows(b, 1, qt)
                    if qt == 3:
                        turn_max_first(b)
                pe.wait_ge(v_ev, b * NT + NT)
                if prep:
                    pe.wait_ge(qk_ev, (b + 2) * NQK * NHALF)
                pe.wait_ge(m_in[0], 16 + 48 * (b * (NH // 2) + 1))
                cols(b, 0, 0)
                slot(b, 0, 0, 0, 2, True)
                slot(b, 1, 1, 1, 2, False)
                hold(pe, passed, aug_in[1], 192 * (b + 1))
                with pe.Fori(1, PAIRS - 1) as p:
                    slot(b, 2 * p, 0, p, 2, False)
                    slot(b, 2 * p + 1, 1, p + 1, 2, False)
                slot(b, NH - 2, 0, PAIRS - 1, 1, False)
                slot(b, NH - 1, 1, PAIRS - 1, 0, False)
                turn_o(b, NH - 1, 1, NH)

            def turn_max_first(b):
                n = b * NH
                pe.wait_ge(m_split, n + 1)
                pe.wait_ge(norm_done, n + 2)
                pe.transpose(ps_m, mparts[:, 0, :, :].rearrange("p c t -> p (c t)"), identb[:, :]).then_inc(mt_done, 1)

            pe.sem_inc(pv_done, RING)
            pe.sem_inc(ot_done, 2)
            for s in m_in:
                pe.sem_inc(s, 16)
            pe.sem_inc(ctx_st, 16)
            pe.wait_ge(w_ready, 2)
            pe.wait_ge(xq_ready, 2)
            for c in range(NQK * NHALF):
                qk_chunk(0, c)
            pe.wait_ge(qk_ev, NQK * NHALF)
            pe.wait_ge(const, 8)
            batch(0, True)
            with pe.Fori(1, B - 1) as b:
                batch(b, True)
            batch(B - 1, False)


def feed_forward(nc, x, ctx_in, outT, out_b, gatesT, w_gate, w_up, w_down, x1_rows, shared_rows,
                 rows_in, rows_out, out, sem):
    T, D = x.shape
    NE = w_gate.shape[0] - 1
    FI = w_gate.shape[2]
    TT = T // P
    DK = D // P
    FCH = [(i, min(P, FI - i)) for i in range(0, FI, P)]
    NC = len(FCH)
    TOPK = 2
    ROUTED = rows_in.shape[0] // P
    UNITS = TT + ROUTED
    EPS = 1e-5
    U = 4
    NG = NE + 1
    assert TT % U == 0 and UNITS % U == 0

    def wait(eng, s, value):
        if not (isinstance(value, int) and value <= 0):
            eng.wait_ge(s, value)

    def pipeline(eng, step, behind, beside=None, until=2, first=False):
        for t in range(2 * U):
            step(t, t % U, t // U)
        if beside:
            with eng.Fori(2, until) as i:
                for k in range(U):
                    if first:
                        beside(i, k)
                    step(i * U + k, k, i)
                    if not first:
                        beside(i, k)
        with eng.Fori(until, TT // U) as i:
            for k in range(U):
                step(i * U + k, k, i)
        for t in range(TT, TT + behind):
            step(t, t % U, t // U)

    def live(t):
        return not isinstance(t, int) or 0 <= t < TT

    HALF = TT // 2
    PHASES = ((0, HALF), (HALF, HALF + ROUTED), (HALF + ROUTED, UNITS))
    SEND, EXPERTS, SUM = range(3)
    LAST = HALF + ROUTED
    assert all(a % U == 0 for a, _ in PHASES)

    def units(eng, step, behind, peel=1):
        for ph, (a, b) in enumerate(PHASES):
            for u in range(a, a + peel * U):
                step(u, u % U, u // U, ph)
            with eng.Fori(a // U + peel, b // U) as i:
                for k in range(U):
                    step(i * U + k, k, i, ph)
        for u in range(UNITS, UNITS + behind):
            step(u, u % U, u // U, None)

    def phase(u, ph):
        if not isinstance(u, int):
            return ph
        return next((p for p, (a, b) in enumerate(PHASES) if a <= u < b), None)

    def rows_of(u, ph):
        ph = phase(u, ph)
        if ph == SEND:
            return tile_of(x1_rows, u), tile_of(shared_rows, u)
        if ph == EXPERTS:
            return tile_of(rows_in, u - HALF), tile_of(rows_out, u - HALF)
        return tile_of(x1_rows, u - ROUTED), None

    def tile_of(a, t):
        return a[bass.ds(t * P, P), :]

    def body(k, i, lag):
        return i + (k - lag) // U

    with ExitStack() as ctx:
        def sb(name, shape, dt=F32):
            return ctx.enter_context(nc.sbuf_tensor("ff_" + name, shape, dt))

        def pb(name, shape, dt=F32):
            return ctx.enter_context(nc.psum_tensor("ff_" + name, shape, dt))

        w_gu = [[sb(f"w_{m}_{part}", [P, DK, NE + 1, FI], F32R) for part in ("hi", "lo")] for m in ("gate", "up")]
        w_dn = [sb(f"w_down_{part}", [P, NC, NE + 1, D], F32R) for part in ("hi", "lo")]
        gates = sb("gates", [P, DK, NG])
        eps = sb("eps", [P, 1])
        minus_half = sb("minus_half", [P, 1])
        ident = sb("ident", [P, P])
        stats = sb("stats", [P, U, 6])
        mv = sb("mv", [P, U, 2])
        std = sb("std", [P, U, 1])
        rstd = sb("rstd", [P, U, 1])
        weights = sb("weights", [P, 3, TT, 1])
        pos = sb("pos", [P, TOPK, TT], mybir.dt.uint32)
        unit_tab = sb("unit_tab", [1, UNITS], mybir.dt.int32)
        before = sb("before", [P, P], BF16)
        ones = sb("ones", [P, P], BF16)
        to = sb("to", [P, U, TOPK, 2, 1], mybir.dt.uint32)
        wsl = sb("wsl", [P, U, 3, 2, 1])
        stats2 = sb("stats2", [P, U, 2, 6])
        mv2 = sb("mv2", [P, U, 2, 2])
        veps = sb("veps", [P, U, 2, 1])
        rstd2 = sb("rstd2", [P, U, 2, 1])
        shift = sb("shift", [P, U, 2, 1])

        def over(name, shape, dt=F32):
            return area.enter_context(nc.sbuf_tensor("ff_" + name, shape, dt))

        HC = NC * P
        wide = [P, TT, NE]
        with ExitStack() as area:
            logits = over("logits", [P, TT, NG])
            raw_gu = over("raw_gu", [P, 2, DK, FI])
            raw_dn = over("raw_dn", [P, NC, D])
            c_in = over("c_in", [P, U, D])
            x_in = over("x_in", [P, U, D])
            cT = over("cT", [P, 2, DK, P])
            res = over("res", [P, U, D])
            x1T = over("x1T", [P, 2, DK, P])
            over("spare", [P, (4 * DK * P + 4 * NC * P + 2 * HC + 3 * U * D + 4 * D)
                           - (TT * NG + 2 * DK * FI + NC * D + 3 * U * D + 4 * DK * P)])
            x1 = over("x1", [P, U, D])
            wo = over("wo", [P, DK, D])
            ob = over("ob", [P, D])

        with ExitStack() as area:
            over("logits_again", [P, TT, NG])
            probs = over("router_probs", wide)
            rest = over("router_rest", wide)
            first = over("router_first", wide)
            second = over("router_second", wide)
            score = over("router_score", wide)
            order = over("router_order", wide)
            chosen = over("router_chosen", wide, BF16)
            scan = [over(f"router_scan{i}", wide) for i in range(2)]
            place = over("router_place", wide)
            tops = over("router_tops", [P, 5, TT, 1])
            posf = over("posf", [P, TOPK, TT])
            need_i = over("need_i", [P, 2, NE], mybir.dt.int32)
            need = over("need", [P, 4, NE])
            unit_no = over("unit_no", [1, UNITS])
            unit_ex = over("unit_ex", [1, 2, UNITS])

        with ExitStack() as area:
            uT = [over(f"uT_{part}", [P, 2, DK, P], F32R) for part in ("hi", "lo")]
            hT = [over(f"hT_{part}", [P, 2, NC, P], F32R) for part in ("hi", "lo")]
            hid = over("hid", [P, 2, HC])
            s_in = over("s_in", [P, U, D])
            sums = over("sums", [P, U, 2, D])
            normed = over("normed", [P, 2, 2, D])
            u_in = over("u_in", [P, U, D])
            y_in = over("y_in", [P, U, 2, TOPK, D])
        u_out = sums[:, :, 0, :]
        x_send = y_in[:, :, 0, :, :]

        ps_t = pb("ps_t", [P, DK, P])
        ps_o = pb("ps_o", [P, D])
        ps_t2 = pb("ps_t2", [P, DK, P])
        ps_l = pb("ps_l", [P, 64])
        ps_g = pb("ps_g", [P, MM_N])
        ps_u = pb("ps_u", [P, MM_N])
        ps_h = pb("ps_h", [P, NC, P])
        ps_y = pb("ps_y", [P, MM_N])
        ct_banks = (ps_t[:, :, :], ps_g[:, 0:D].rearrange("p (d n) -> p d n", n=P))
        pr_banks = (ps_o[:, :], ps_u[:, 0:D])
        xt_banks = (ps_t2[:, :, :], ps_y[:, 0:D].rearrange("p (d n) -> p d n", n=P))
        lo_banks = (ps_l[:, 0:NG], ps_h[:, 0, 0:NG])

        small_in = sem("small_in")
        w_ld = [sem(f"w_ld{k}") for k in range(U)]
        w_hi_done = sem("w_hi_done")
        w_lo_done = [sem(f"w_lo_done{k}") for k in range(U)]
        const = sem("const")
        c_ld = [sem(f"c_ld{k}") for k in range(U)]
        x_ld = [sem(f"x_ld{k}") for k in range(U)]
        biased = sem("biased")
        x1_st = [sem(f"x1_st{k}") for k in range(U)]
        cturn = sem("cturn")
        c_ev = sem("c_ev")
        proj = sem("proj")
        r_step = sem("r_step")
        std_done = sem("std_done")
        n_step = sem("n_step")
        xturn = sem("xturn")
        xt_ev = sem("xt_ev")
        logit = sem("logit")
        l_ev = sem("l_ev")
        rt = sem("rt")
        rexp = sem("rexp")
        rcount = sem("rcount")
        u_ld = [sem(f"u_ld{k}") for k in range(U)]
        uturn = sem("uturn")
        ut_ev = sem("ut_ev")
        gate_done = sem("gate_done")
        gu = sem("gu")
        silu_done = sem("silu_done")
        h_done = sem("h_done")
        hturn = sem("hturn")
        ut_lo = sem("ut_lo")
        ht_ev = sem("ht_ev")
        ht_lo = sem("ht_lo")
        down = sem("down")
        y_ev = sem("y_ev")
        y_st = [sem(f"y_st{k}") for k in range(U)]
        send_ld = [sem(f"send_ld{k}") for k in range(U)]
        sent = [sem(f"sent{k}") for k in range(U)]
        slot_done = sem("slot_done")
        s_ld = [sem(f"s_ld{k}") for k in range(U)]
        got = [sem(f"got{k}") for k in range(U)]
        f_step = sem("f_step")
        f_std = sem("f_std")
        f_shift = sem("f_shift")
        f_norm = sem("f_norm")
        passed = sem("passed")
        o_st = [sem(f"o_st{k}") for k in range(2)]

        R_SUB = 2
        R_CHOSEN = R_SUB + 3 + 2 + 5 + 1 + 5 + 2 + TOPK + 1
        R_ALL = (R_CHOSEN + 1 + 2 * (TT.bit_length() - 1) + 2 + 5 + 2 * (NE.bit_length() - 1) + 3
                 + 2 * TOPK + 1 + 1 + NE + 1)
        F_SUMS, F_STEPS = 2 * TOPK, 2 * TOPK + 4
        block = ctx.enter_context(nc.Block())

        def quarter(e, k, part=None):
            if k < 2:
                return (raw_gu[:, k, :, :] if part is None else
                        w_gu[k][part][:, :, bass.ds(e, 1), :].rearrange("p c e n -> p c (e n)"))
            p, c = (slice(0, P), slice(0, NC - 1)) if k == 2 else (slice(0, FCH[-1][1]), slice(NC - 1, NC))
            return (raw_dn[p, c, :] if part is None else
                    w_dn[part][p, c, bass.ds(e, 1), :].rearrange("p c e n -> p c (e n)"))

        def subtract_high(ns, eng, i, k):
            eng.wait_ge(w_hi_done, U * (i - 2) + k + 1)
            ns.tensor_tensor(quarter(i - 2, k, 1), quarter(i - 2, k), quarter(i - 2, k, 0).bitcast(F32),
                             ALU.subtract).then_inc(w_lo_done[k], 1)

        @block.sync
        def _(sp):
            sp.dma_start(wo[:, :, :], outT.rearrange("(c p) n -> p c n", p=P)).then_inc(small_in, 16)
            sp.dma_start(ob[:, :], out_b.partition_broadcast(P)).then_inc(small_in, 16)
            sp.dma_start(gates[:, :, :], gatesT.rearrange("(c p) n -> p c n", p=P)).then_inc(small_in, 16)

            def load_ctx(t, k):
                wait(sp, cturn, t - U + 1)
                sp.dma_start(c_in[:, k, :], tile_of(ctx_in, t)).then_inc(c_ld[k], 16)

            def load_x(t, k):
                wait(sp, r_step, 3 * (t - U) + 1)
                sp.dma_start(x_in[:, k, :], tile_of(x, t)).then_inc(x_ld[k], 16)

            def store(t, k):
                sp.wait_ge(n_step, 2 * t + 2)
                sp.dma_start(tile_of(x1_rows, t), x1[:, k, :]).then_inc(x1_st[k], 16)

            def first_part(t, k, i):
                if live(t):
                    load_ctx(t, k)
                if live(t - 1):
                    load_x(t - 1, (k - 1) % U)
                if live(t - 7):
                    store(t - 7, (k - 7) % U)

            def load_weights(e, k):
                sp.wait_ge(w_lo_done[k], e + 1)
                one = bass.ds(e, 1)
                full = (NC - 1) * P
                if k < 2:
                    src = (w_gate, w_up)[k][one, :, :].rearrange("e (c p) n -> p (e c) n", p=P)
                elif k == 2:
                    src = w_down[one, 0:full, :].rearrange("e (c p) n -> p (e c) n", p=P)
                else:
                    src = w_down[one, full:FI, :].rearrange("e p n -> p e n")
                sp.dma_start(quarter(e, k), src).then_inc(w_ld[k], 16)

            pipeline(sp, first_part, 7, lambda i, k: load_weights(i - 2, k), NE + 3)

            def load_unit(u, k, ph):
                wait(sp, y_ev, u - U + 1)
                sp.dma_start(u_in[:, k, :], rows_of(u, ph)[0]).then_inc(u_ld[k], 16)

            def load_send(t, k, i):
                wait(sp, sent[k], 2 * TOPK * 16 * i)
                for h in range(2):
                    sp.dma_start(x_send[:, k, h, :], tile_of(x1_rows, t + h * HALF)).then_inc(send_ld[k], 16)

            def store_unit(u, k, ph):
                sp.wait_ge(y_ev, u + 1)
                sp.dma_start(rows_of(u, ph)[1], u_out[:, k, :]).then_inc(y_st[k], 16)

            def load_shared(q, k):
                wait(sp, f_step, F_STEPS * (q - U) + 1)
                sp.dma_start(s_in[:, k, :], tile_of(shared_rows, q)).then_inc(s_ld[k], 16)

            def store_sums(q, k):
                sp.wait_ge(f_norm, 2 * q + 2)
                for h in range(2):
                    sp.dma_start(tile_of(out, q + h * HALF), normed[:, k % 2, h, :]).then_inc(o_st[k % 2], 16)

            for k in range(U):
                sp.wait_ge(x1_st[k], 16 * (TT // U) + 16)
            sp.wait_ge(xturn, TT)

            def unit(u, k, i, ph):
                if isinstance(u, int) and u == HALF:
                    for j in range(U):
                        sp.wait_ge(sent[j], 2 * TOPK * 16 * (HALF // U))
                if isinstance(u, int) and u == LAST:
                    for j in range(U):
                        sp.wait_ge(y_st[j], 16 * (HALF // U) + 16)
                if phase(u, ph) is not None:
                    load_unit(u, k, ph)
                if phase(u, ph) == SEND:
                    load_send(u, k, i)
                if phase(u - 4, ph) in (SEND, EXPERTS):
                    store_unit(u - 4, k, ph)
                if phase(u - 1, ph) == SUM:
                    load_shared(u - 1 - LAST, (k - 1) % U)
                if phase(u - 7, ph) == SUM:
                    store_sums(u - 7 - LAST, (k - 7) % U)
            units(sp, unit, 7, peel=2)
            for s in o_st:
                sp.wait_ge(s, 16 * HALF + 16)

        @block.gpsimd
        def _(pool):
            nc.gpsimd.memset(ident[:, :], 0.0).then_inc(const, 1)
            nc.gpsimd.memset(before[:, :], 1.0).then_inc(const, 1)
            nc.gpsimd.memset(ones[:, :], 1.0).then_inc(const, 1)
            nc.gpsimd.memset(eps[:, :], EPS).then_inc(const, 1)
            nc.gpsimd.memset(minus_half[:, :], -0.5).then_inc(const, 1)
            pool.wait_ge(const, 5)
            nc.gpsimd.affine_select(out=ident[:, :], in_=ident[:, :], compare_op=ALU.not_equal, fill=1.0,
                                    base=0, pattern=[[-1, P]], channel_multiplier=1).then_inc(const, 1)
            nc.gpsimd.affine_select(out=before[:, :], in_=before[:, :], compare_op=ALU.is_gt, fill=0.0,
                                    base=0, pattern=[[1, P]], channel_multiplier=-1).then_inc(const, 1)
            pool.wait_ge(small_in, 48)

            def bias(t, k, i):
                pool.wait_ge(x_ld[k], 16 * (i + 1))
                nc.gpsimd.tensor_tensor(x_in[:, k, :], x_in[:, k, :], ob[:, :], ALU.add).then_inc(biased, 1)

            def low_part(i, k):
                if k % 2:
                    subtract_high(nc.gpsimd, pool, i, k)
            pipeline(pool, bias, 0, low_part, NE + 3)

            pool.wait_ge(l_ev, TT)
            nc.gpsimd.iota(order[:, :, :], pattern=[[0, TT], [-1, NE]], base=NE, channel_multiplier=0,
                           allow_small_or_imprecise_dtypes=True).then_inc(const, 1)
            nc.gpsimd.iota(unit_no[:, :], pattern=[[1, UNITS]], base=-HALF, channel_multiplier=0,
                           allow_small_or_imprecise_dtypes=True).then_inc(const, 1)

            pool.wait_ge(rt, R_ALL)
            nc.gpsimd.memset(hid[:, :, FI:HC], 0.0).then_inc(const, 1)

            def send(u, k, i):
                pool.wait_ge(send_ld[k], 2 * 16 * (i + 1))
                hold(pool, passed, slot_done, 2 * u + 1)
                for h in range(2):
                    for c in range(TOPK):
                        nc.gpsimd.indirect_dma_start(
                            out=rows_in, out_offset=bass.IndirectOffsetOnAxis(ap=to[:, k, c, h, :], axis=0),
                            in_=x_send[:, k, h, :], in_offset=None).then_inc(sent[k], 16)

            with pool.Fori(0, HALF // U) as i:
                for k in range(U):
                    send(i * U + k, k, i)

            def fetch(q, k):
                if not (isinstance(q, int) and q < U):
                    hold(pool, passed, f_step, F_STEPS * (q - U) + F_SUMS)
                hold(pool, passed, slot_done, 2 * (HALF + q) + 1)
                for h in range(2):
                    for c in range(TOPK):
                        nc.gpsimd.indirect_dma_start(
                            out=y_in[:, k, h, c, :], out_offset=None, in_=rows_out,
                            in_offset=bass.IndirectOffsetOnAxis(ap=to[:, k, c, h, :], axis=0)).then_inc(got[k], 16)

            def inverse(q, k):
                pool.wait_ge(f_step, F_STEPS * q + F_STEPS)
                nc.gpsimd.tensor_tensor(veps[:, k, :, :], mv2[:, k, :, 1:2],
                                        eps[:, :].rearrange("p (h o) -> p h o", h=1).broadcast_to([P, 2, 1]),
                                        ALU.add).then_inc(f_std, 1)
                pool.wait_ge(f_std, 2 * q + 1)
                nc.gpsimd.tensor_tensor(rstd2[:, k, :, :], veps[:, k, :, :],
                                        minus_half[:, :].rearrange("p (h o) -> p h o", h=1).broadcast_to([P, 2, 1]),
                                        ALU.pow).then_inc(f_std, 1)

            for k in range(U):
                pool.wait_ge(y_st[k], 16 * (LAST // U) + 16)
            for q in range(U):
                fetch(q, q)
            with pool.Fori(1, HALF // U) as i:
                for k in range(U):
                    fetch(i * U + k, k)
                    inverse(i * U + k - U, k)
            for k in range(U):
                inverse(HALF - U + k, k)

        @block.scalar
        def _(act):
            act.wait_ge(const, 7)
            for s in (*y_st, *x1_st, *o_st):
                act.sem_inc(s, 16)
            for s in w_lo_done:
                act.sem_inc(s, 1)

            def turned_ctx(t, k):
                act.wait_ge(cturn, t + 1)
                wait(act, proj, t - 1)
                nc.scalar.activation(cT[:, k % 2, :, :], ct_banks[k % 2], ACT.Copy).then_inc(c_ev, 1)

            def sqrt(t, k):
                act.wait_ge(r_step, 3 * t + 3)
                nc.scalar.activation(std[:, k, :], mv[:, k, 1:2], ACT.Sqrt, bias=eps[:, 0:1]).then_inc(std_done, 1)

            def turned_x1(t, k):
                act.wait_ge(xturn, t + 1)
                wait(act, logit, t - 1)
                nc.scalar.activation(x1T[:, k % 2, :, :], xt_banks[k % 2], ACT.Copy).then_inc(xt_ev, 1)

            def first_part(t, k, i):
                if live(t - 4):
                    turned_x1(t - 4, (k - 4) % U)
                if live(t):
                    turned_ctx(t, k)
                if live(t - 2):
                    sqrt(t - 2, (k - 2) % U)
            def high_part(i, k):
                act.wait_ge(w_ld[k], 16 * (i - 1))
                nc.scalar.activation(quarter(i - 2, k, 0), quarter(i - 2, k), ACT.Copy).then_inc(w_hi_done, 1)
            pipeline(act, first_part, 4, high_part, NE + 3, first=True)

            act.wait_ge(rt, R_SUB)
            nc.scalar.activation(probs[:, :, :], rest[:, :, :], ACT.Exp).then_inc(rexp, 1)
            nc.scalar.activation(tops[:, 4, :, :], logits[:, :, NE:NG], ACT.Exp, scale=-1.0).then_inc(rexp, 1)

            def turned_unit(u, k):
                act.wait_ge(uturn, u + 1)
                wait(act, gu, u - 1)
                nc.scalar.activation(uT[0][:, k % 2, :, :], ps_t[:, :, :], ACT.Copy).then_inc(ut_ev, 1)

            def gate(u, k):
                act.wait_ge(gate_done, u + 1)
                wait(act, hturn, u - 1)
                nc.scalar.activation(hid[:, k % 2, 0:FI], ps_g[:, 0:FI], ACT.Silu).then_inc(silu_done, 1)

            def turned_hidden(u, k):
                act.wait_ge(hturn, u + 1)
                wait(act, down, u - 1)
                nc.scalar.activation(hT[0][:, k % 2, :, :], ps_h[:, :, :], ACT.Copy).then_inc(ht_ev, 1)

            def result(u, k, i):
                act.wait_ge(down, u + 1)
                act.wait_ge(y_st[k], 16 * i + 16)
                nc.scalar.activation(u_out[:, k, :], ps_y[:, 0:D], ACT.Copy).then_inc(y_ev, 1)

            def normalise(q, k, i):
                act.wait_ge(f_shift, q + 1)
                act.wait_ge(o_st[k % 2], 2 * 16 * (2 * i + k // 2) + 16)
                for h in range(2):
                    nc.scalar.activation(normed[:, k % 2, h, :], sums[:, k, h, :], ACT.Identity,
                                         bias=shift[:, k, h, :], scale=rstd2[:, k, h, :]).then_inc(f_norm, 1)

            def unit(u, k, i, ph):
                if phase(u - 2, ph) is not None:
                    turned_hidden(u - 2, (k - 2) % U)
                if phase(u - 1, ph) is not None:
                    gate(u - 1, (k - 1) % U)
                if phase(u, ph) is not None:
                    turned_unit(u, k)
                if phase(u - 5, ph) == SUM:
                    normalise(u - 5 - LAST, (k - 5) % U, body(k, i, 5) - LAST // U)
                if phase(u - 2, ph) == EXPERTS:
                    result(u - 2, (k - 2) % U, body(k, i, 2))
            units(act, unit, 5, peel=2)

        @block.vector
        def _(dve):
            V = nc.vector

            def residual(t, k):
                dve.wait_ge(proj, t + 1)
                dve.wait_ge(biased, t + 1)
                wait(dve, n_step, 2 * (t - U) + 2)
                V.tensor_tensor(res[:, k, :], pr_banks[k % 2], x_in[:, k, :], ALU.add).then_inc(r_step, 1)

            def statistics(t, k):
                dve.wait_ge(r_step, 3 * t + 1)
                V.bn_stats(stats[:, k, :], res[:, k, :]).then_inc(r_step, 1)

            def variance(t, k):
                hold(dve, passed, r_step, 3 * t + 2)
                V.bn_aggr(mv[:, k, :], stats[:, k, :]).then_inc(r_step, 1)

            def inverse(t, k):
                dve.wait_ge(std_done, t + 1)
                V.reciprocal(rstd[:, k, :], std[:, k, :]).then_inc(n_step, 1)

            def normalise(t, k, i):
                dve.wait_ge(n_step, 2 * t + 1)
                wait(dve, x1_st[k], 16 * i + 16)
                wait(dve, xturn, t - U + 1)
                V.tensor_scalar(x1[:, k, :], res[:, k, :], mv[:, k, 0:1], rstd[:, k, 0:1],
                                ALU.subtract, ALU.mult).then_inc(n_step, 1)

            def take_logits(t, k):
                dve.wait_ge(logit, t + 1)
                V.tensor_copy(logits[:, bass.ds(t, 1), :].rearrange("p t e -> p (t e)"),
                              lo_banks[k % 2]).then_inc(l_ev, 1)

            def first_part(t, k, i):
                if live(t - 2):
                    residual(t - 2, (k - 2) % U)
                if live(t - 3):
                    inverse(t - 3, (k - 3) % U)
                if live(t - 5):
                    take_logits(t - 5, (k - 5) % U)
                if live(t - 2):
                    statistics(t - 2, (k - 2) % U)
                if live(t - 3):
                    normalise(t - 3, (k - 3) % U, body(k, i, 3))
                if live(t - 2):
                    variance(t - 2, (k - 2) % U)
            def low_part(i, k):
                if k % 2 == 0:
                    subtract_high(V, dve, i, k)
            pipeline(dve, first_part, 5, low_part, NE + 3)

            n = [0]

            def r(op):
                n[0] += 1
                op.then_inc(rt, 1)
                dve.wait_ge(rt, n[0])

            def wide_of(a):
                return a.broadcast_to(wide)

            dve.wait_ge(l_ev, TT)
            dve.wait_ge(const, 9)
            lg = logits[:, :, 0:NE]
            r(V.tensor_reduce(tops[:, 0, :, :], lg, AX.X, ALU.max))
            r(V.tensor_tensor(rest[:, :, :], lg, wide_of(tops[:, 0, :, :]), ALU.subtract))
            assert n[0] == R_SUB
            dve.wait_ge(rexp, 2)
            r(V.tensor_reduce(tops[:, 1, :, :], probs[:, :, :], AX.X, ALU.add))
            r(V.reciprocal(tops[:, 0, :, :], tops[:, 1, :, :]))
            r(V.tensor_tensor(probs[:, :, :], probs[:, :, :], wide_of(tops[:, 0, :, :]), ALU.mult))
            r(V.tensor_scalar(tops[:, 4, :, :], tops[:, 4, :, :], 1.0, None, ALU.add))
            r(V.reciprocal(weights[:, 2, :, :], tops[:, 4, :, :]))

            def choose(of, top, mask):
                r(V.tensor_reduce(top, of[:, :, :], AX.X, ALU.max))
                r(V.tensor_tensor(score[:, :, :], of[:, :, :], wide_of(top), ALU.is_equal))
                r(V.tensor_tensor(score[:, :, :], score[:, :, :], order[:, :, :], ALU.mult))
                r(V.tensor_reduce(tops[:, 3, :, :], score[:, :, :], AX.X, ALU.max))
                r(V.tensor_tensor(mask[:, :, :], score[:, :, :], wide_of(tops[:, 3, :, :]), ALU.is_equal))

            choose(probs, tops[:, 0, :, :], first)
            r(V.scalar_tensor_tensor(rest[:, :, :], first[:, :, :], -2.0, probs[:, :, :], ALU.mult, ALU.add))
            choose(rest, tops[:, 1, :, :], second)
            r(V.tensor_tensor(tops[:, 2, :, :], tops[:, 0, :, :], tops[:, 1, :, :], ALU.add))
            r(V.reciprocal(tops[:, 3, :, :], tops[:, 2, :, :]))
            for c in range(TOPK):
                r(V.tensor_tensor(weights[:, c, :, :], tops[:, c, :, :], tops[:, 3, :, :], ALU.mult))
            r(V.tensor_tensor(chosen[:, :, :], first[:, :, :], second[:, :, :], ALU.add))
            assert n[0] == R_CHOSEN
            dve.wait_ge(rcount, 2)
            totals = ps_u[:, 0:TT * NE].rearrange("p (t e) -> p t e", e=NE)
            inside = ps_g[:, 0:TT * NE].rearrange("p (t e) -> p t e", e=NE)
            r(V.tensor_copy(scan[0][:, :, :], totals))
            s, d = 0, 1
            while d < TT:
                r(V.tensor_copy(scan[1 - s][:, 0:d, :], scan[s][:, 0:d, :]))
                r(V.tensor_tensor(scan[1 - s][:, d:TT, :], scan[s][:, d:TT, :], scan[s][:, 0:TT - d, :], ALU.add))
                s, d = 1 - s, 2 * d
            r(V.tensor_tensor(place[:, :, :], scan[s][:, :, :], totals, ALU.subtract))
            r(V.tensor_tensor(place[:, :, :], place[:, :, :], inside, ALU.add))
            r(V.tensor_scalar(need[:, 0, :], scan[s][:, TT - 1, :], float(P - 1), None, ALU.add))
            r(V.tensor_copy(need_i[:, 0, :], need[:, 0, :]))
            r(V.tensor_scalar(need_i[:, 1, :], need_i[:, 0, :], P.bit_length() - 1, None, ALU.arith_shift_right))
            r(V.tensor_copy(need[:, 1, :], need_i[:, 1, :]))
            r(V.tensor_copy(need[:, 0, :], need_i[:, 1, :]))
            a, d = 1, 1
            while d < NE:
                b = 3 - a
                r(V.tensor_copy(need[:, b, 0:d], need[:, a, 0:d]))
                r(V.tensor_tensor(need[:, b, d:NE], need[:, a, d:NE], need[:, a, 0:NE - d], ALU.add))
                a, d = b, 2 * d
            r(V.tensor_tensor(need[:, 3, :], need[:, a, :], need[:, 0, :], ALU.subtract))
            r(V.tensor_scalar(need[:, 3, :], need[:, 3, :], float(P), None, ALU.mult))
            r(V.tensor_tensor(place[:, :, :], place[:, :, :],
                              need[:, 3:4, :].broadcast_to(wide), ALU.add))
            for c, mask in enumerate((first, second)):
                r(V.tensor_tensor(score[:, :, :], place[:, :, :], mask[:, :, :], ALU.mult))
                r(V.tensor_reduce(posf[:, c, :], score[:, :, :], AX.X, ALU.add))
            r(V.tensor_copy(pos[:, :, :], posf[:, :, :]))
            r(V.tensor_scalar(unit_ex[:, 0, :], unit_no[:, :], 0.0, float(NE), ALU.is_lt, ALU.mult))
            for e in range(NE):
                r(V.scalar_tensor_tensor(unit_ex[:, (e + 1) % 2, :], unit_no[:, :], need[0:1, a, e:e + 1],
                                         unit_ex[:, e % 2, :], ALU.is_ge, ALU.add))
            r(V.tensor_copy(unit_tab[:, :], unit_ex[:, NE % 2, :]))
            assert n[0] == R_ALL, n[0]

            def split_pos(a):
                return a.rearrange("p c (h t) -> p c h t", h=2)

            def slots(u, k, i, ph):
                t = u if ph == SEND else u - LAST
                if ph == SEND:
                    wait(dve, sent[k], 2 * TOPK * 16 * i)
                    wait(dve, y_ev, u - U + 1)
                else:
                    wait(dve, got[k], 2 * TOPK * 16 * (i - LAST // U))
                    wait(dve, f_step, F_STEPS * (t - U) + F_SUMS)
                V.tensor_copy(to[:, k, :, :, :], split_pos(pos[:, :, :])[:, :, :, bass.ds(t, 1)]).then_inc(slot_done, 1)
                V.tensor_copy(wsl[:, k, :, :, :],
                              split_pos(weights[:, :, :, :].rearrange("p c t o -> p c (t o)"))[:, :, :, bass.ds(t, 1)]
                              ).then_inc(slot_done, 1)

            def hidden(u, k):
                dve.wait_ge(silu_done, u + 1)
                dve.wait_ge(gu, u + 1)
                V.tensor_tensor(hid[:, k % 2, 0:FI], hid[:, k % 2, 0:FI], ps_u[:, 0:FI], ALU.mult).then_inc(h_done, 1)

            def unit_low(u, k):
                dve.wait_ge(ut_ev, u + 1)
                V.tensor_tensor(uT[1][:, k % 2, :, :], ps_t[:, :, :], uT[0][:, k % 2, :, :].bitcast(F32),
                                ALU.subtract).then_inc(ut_lo, 1)

            def hidden_low(u, k):
                dve.wait_ge(ht_ev, u + 1)
                V.tensor_tensor(hT[1][:, k % 2, :, :], ps_h[:, :, :], hT[0][:, k % 2, :, :].bitcast(F32),
                                ALU.subtract).then_inc(ht_lo, 1)

            def shared_result(u, k, i, ph):
                dve.wait_ge(down, u + 1)
                if ph == SEND:
                    dve.wait_ge(slot_done, 2 * u + 2)
                    dve.wait_ge(y_st[k], 16 * i + 16)
                    into, h = u_out[:, k, :], 0
                else:
                    q = u - LAST
                    dve.wait_ge(slot_done, 2 * (HALF + q) + 2)
                    wait(dve, f_norm, 2 * (q - U) + 2)
                    into, h = sums[:, k, 1, :], 1
                V.scalar_tensor_tensor(into, ps_y[:, 0:D], wsl[:, k, 2, h, :], u_in[:, k, :],
                                       ALU.mult, ALU.add).then_inc(y_ev, 1)

            def add_experts(q, k, i):
                dve.wait_ge(got[k], 2 * TOPK * 16 * (i + 1))
                dve.wait_ge(s_ld[k], 16 * (i + 1))
                dve.wait_ge(y_ev, q + LAST + 1)
                for c in range(TOPK):
                    for h in range(2):
                        if c:
                            dve.wait_ge(f_step, F_STEPS * q + 1 + h)
                        old = s_in[:, k, :] if (c, h) == (0, 0) else sums[:, k, h, :]
                        V.scalar_tensor_tensor(sums[:, k, h, :], y_in[:, k, h, c, :], wsl[:, k, c, h, :], old,
                                               ALU.mult, ALU.add).then_inc(f_step, 1)

            def statistics2(q, k):
                for h in range(2):
                    dve.wait_ge(f_step, F_STEPS * q + 3 + h)
                    V.bn_stats(stats2[:, k, h, :], sums[:, k, h, :]).then_inc(f_step, 1)
                for h in range(2):
                    hold(dve, passed, f_step, F_STEPS * q + 5 + h)
                    V.bn_aggr(mv2[:, k, h, :], stats2[:, k, h, :]).then_inc(f_step, 1)

            def mean_shift(q, k):
                dve.wait_ge(f_std, 2 * q + 2)
                V.scalar_tensor_tensor(shift[:, k, :, :], mv2[:, k, :, 0:1], -1.0, rstd2[:, k, :, :],
                                       ALU.mult, ALU.mult).then_inc(f_shift, 1)

            def unit(u, k, i, ph):
                p3 = phase(u - 3, ph)
                if p3 in (SEND, SUM):
                    shared_result(u - 3, (k - 3) % U, body(k, i, 3), p3)
                if phase(u - 4, ph) == SUM:
                    add_experts(u - 4 - LAST, k, i - 1 - LAST // U)
                if phase(u, ph) in (SEND, SUM):
                    slots(u, k, i, phase(u, ph))
                if phase(u - 5, ph) == SUM:
                    mean_shift(u - 5 - LAST, (k - 5) % U)
                if phase(u - 2, ph) is not None:
                    hidden_low(u - 2, (k - 2) % U)
                if phase(u - 1, ph) is not None:
                    hidden(u - 1, (k - 1) % U)
                if phase(u, ph) is not None:
                    unit_low(u, k)
                if phase(u - 4, ph) == SUM:
                    statistics2(u - 4 - LAST, k)
            units(dve, unit, 5, peel=2)

        @block.tensor
        def _(pe):
            pe.wait_ge(const, 7)
            pe.wait_ge(small_in, 48)

            def turn_ctx(t, k, i):
                pe.wait_ge(c_ld[k], 16 * (i + 1))
                wait(pe, c_ev, t - 1)
                for d in range(DK):
                    mm = pe.transpose(ct_banks[k % 2][:, d, :], c_in[:, k, d * P:(d + 1) * P], ident[:, :])
                mm.then_inc(cturn, 1)

            def project(t, k):
                pe.wait_ge(c_ev, t + 1)
                wait(pe, r_step, 3 * (t - 2) + 1)
                for d in range(DK):
                    mm = pe.matmul(pr_banks[k % 2], cT[:, k % 2, d, :], wo[:, d, :], start=(d == 0), stop=(d == DK - 1))
                mm.then_inc(proj, 1)

            def turn_x1(t, k):
                pe.wait_ge(n_step, 2 * t + 2)
                wait(pe, xt_ev, t - 1)
                for d in range(DK):
                    mm = pe.transpose(xt_banks[k % 2][:, d, :], x1[:, k, d * P:(d + 1) * P], ident[:, :])
                mm.then_inc(xturn, 1)

            def route(t, k):
                pe.wait_ge(xt_ev, t + 1)
                wait(pe, l_ev, t - 1)
                for d in range(DK):
                    mm = pe.matmul(lo_banks[k % 2], x1T[:, k % 2, d, :], gates[:, d, :],
                                   start=(d == 0), stop=(d == DK - 1))
                mm.then_inc(logit, 1)

            def first_part(t, k, i):
                if live(t - 4):
                    turn_x1(t - 4, (k - 4) % U)
                if live(t):
                    turn_ctx(t, k, i)
                if live(t - 1):
                    project(t - 1, (k - 1) % U)
                if live(t - 4):
                    route(t - 4, (k - 4) % U)
            pipeline(pe, first_part, 4)

            pe.wait_ge(rt, R_CHOSEN)
            flat = chosen[:, :, :].rearrange("p t e -> p (t e)")
            pe.matmul(ps_g[:, 0:TT * NE], before[:, :], flat, start=True, stop=True).then_inc(rcount, 1)
            pe.matmul(ps_u[:, 0:TT * NE], ones[:, :], flat, start=True, stop=True).then_inc(rcount, 1)

            def turn_unit(u, k, i):
                pe.wait_ge(u_ld[k], 16 * (i + 1))
                wait(pe, ut_lo, u)
                for d in range(DK):
                    mm = pe.transpose(ps_t[:, d, :], u_in[:, k, d * P:(d + 1) * P], ident[:, :])
                mm.then_inc(uturn, 1)

            def expert_of(u):
                return pe.value_load(unit_tab[0:1, bass.ds(u, 1)], min_val=0, max_val=NE)

            def gate_up(u, k, e):
                pe.wait_ge(ut_lo, u + 1)
                wait(pe, h_done, u)
                for w, bank, done in zip(w_gu, (ps_g, ps_u), (gate_done, gu)):
                    for n, (a, b) in enumerate(THREE):
                        for d in range(DK):
                            mm = pe.matmul(bank[:, 0:FI], uT[a][:, k % 2, d, :],
                                           w[b][:, d, bass.ds(e, 1), :].rearrange("p e n -> p (e n)"),
                                           start=(n == d == 0), stop=(n == 2 and d == DK - 1))
                    mm.then_inc(done, 1)

            def turn_hidden(u, k):
                pe.wait_ge(h_done, u + 1)
                wait(pe, ht_lo, u)
                for c in range(NC):
                    mm = pe.transpose(ps_h[:, c, :], hid[:, k % 2, c * P:(c + 1) * P], ident[:, :])
                mm.then_inc(hturn, 1)

            def project_down(u, k, e):
                pe.wait_ge(ht_lo, u + 1)
                wait(pe, y_ev, u)
                for n, (a, b) in enumerate(THREE):
                    for c, (_, rows) in enumerate(FCH):
                        mm = pe.matmul(ps_y[:, 0:D], hT[a][0:rows, k % 2, c, :],
                                       w_dn[b][0:rows, c, bass.ds(e, 1), :].rearrange("p e n -> p (e n)"),
                                       start=(n == c == 0), stop=(n == 2 and c == NC - 1))
                mm.then_inc(down, 1)

            def unit(u, k, i, head, tail):
                if head and live_unit(u - 2):
                    number[(k - 2) % U] = expert_of(u - 2)
                if head and live_unit(u - 1):
                    number[(k - 1) % U] = expert_of(u - 1)
                if live_unit(u - 2):
                    turn_hidden(u - 2, (k - 2) % U)
                if live_unit(u - 1):
                    gate_up(u - 1, (k - 1) % U, number[(k - 1) % U])
                if live_unit(u) and not tail:
                    number[k] = expert_of(u)
                if live_unit(u):
                    turn_unit(u, k, i)
                if live_unit(u - 2):
                    project_down(u - 2, (k - 2) % U, number[(k - 2) % U])

            def live_unit(u):
                return not isinstance(u, int) or 0 <= u < UNITS

            number = {}

            for s in w_lo_done:
                pe.wait_ge(s, NE + 2)
            pe.wait_ge(rt, R_ALL)
            pe.wait_ge(const, 10)
            def two_bodies(i):
                for k in range(2 * U):
                    unit(i * 2 * U + k, k % U, 2 * i + k // U, k == 0, k == 2 * U - 1)

            assert UNITS % (2 * U) == 0
            two_bodies(0)
            with pe.Fori(1, UNITS // (2 * U)) as i:
                two_bodies(i)
            for k in range(2):
                unit(UNITS + k, k, UNITS // U, k == 0, False)


_INS = ["x", "xT", "wqkT", "wvT", "qk_b", "v_b", "outT", "out_b", "gatesT", "w_gate", "w_up", "w_down"]


def build(nc, ins, out):
    B, D, S = ins["xT"].shape
    T = B * S
    NE = ins["w_gate"].shape[0] - 1
    TOPK = 2
    routed = T // P * TOPK + NE
    ctx_d = nc.dram_tensor("ctx_d", (B, S, D), F32).ap()
    qk_parts = nc.dram_tensor("qk_parts", (2, 3, D, S), BF16).ap()
    x1_rows = nc.dram_tensor("x1_rows", (T, D), F32).ap()
    shared_rows = nc.dram_tensor("shared_rows", (T // 2, D), F32).ap()
    rows_in = nc.dram_tensor("rows_in", (routed * P, D), F32).ap()
    rows_out = nc.dram_tensor("rows_out", (routed * P, D), F32).ap()

    for part in range(2):
        with ExitStack() as sems:
            def sem(name):
                return sems.enter_context(nc.semaphore(("at_", "ff_")[part] + name))

            if part == 0:
                attention(nc, ins["xT"], ins["wqkT"], ins["wvT"], ins["qk_b"], ins["v_b"], ctx_d, qk_parts,
                          rows_in, sem)
            else:
                feed_forward(nc, ins["x"], ctx_d.rearrange("b s d -> (b s) d"), ins["outT"], ins["out_b"],
                             ins["gatesT"], ins["w_gate"], ins["w_up"], ins["w_down"], x1_rows, shared_rows, rows_in,
                             rows_out,
                             out.rearrange("b s d -> (b s) d"), sem)


def kernel(L0_attn_x, L0_attn_qkv_w, L0_attn_qkv_b, L0_attn_out_w, L0_attn_out_b, L0_ffn_gate_w, L0_ffn_w_gate,
           L0_ffn_w_up, L0_ffn_w_down, L0_ffn_sw_gate, L0_ffn_sw_up, L0_ffn_sw_down, L0_ffn_shared_gate_w):
    import numpy as np
    import concourse.bacc as bacc
    from concourse.bass_utils import run_bass_kernel_spmd

    x = np.asarray(L0_attn_x)
    B, S, D = x.shape
    qkv_w, qkv_b = np.asarray(L0_attn_qkv_w), np.asarray(L0_attn_qkv_b)
    arrays = {
        "x": x.reshape(B * S, D),
        "xT": x.transpose(0, 2, 1),
        "wqkT": qkv_w[:2 * D].T,
        "wvT": qkv_w[2 * D:].T,
        "qk_b": qkv_b[:2 * D].reshape(-1, P).T,
        "v_b": qkv_b[2 * D:],
        "outT": np.asarray(L0_attn_out_w).T,
        "out_b": np.asarray(L0_attn_out_b),
        "gatesT": np.concatenate([np.asarray(L0_ffn_gate_w), np.asarray(L0_ffn_shared_gate_w)]).T,
        "w_gate": np.concatenate([np.asarray(L0_ffn_w_gate), np.asarray(L0_ffn_sw_gate)[None]]),
        "w_up": np.concatenate([np.asarray(L0_ffn_w_up), np.asarray(L0_ffn_sw_up)[None]]),
        "w_down": np.concatenate([np.asarray(L0_ffn_w_down), np.asarray(L0_ffn_sw_down)[None]]),
    }
    nc = bacc.Bacc("TRN2", target_bir_lowering=False, num_devices=1)
    ins = {}
    for name in _INS:
        arrays[name] = np.ascontiguousarray(arrays[name])
        ins[name] = nc.dram_tensor(f"in_{name}", arrays[name].shape, mybir.dt.from_np(arrays[name].dtype),
                                   kind="ExternalInput").ap()
    out = nc.dram_tensor("out", (B, S, D), F32, kind="ExternalOutput").ap()
    build(nc, ins, out)
    r = run_bass_kernel_spmd(nc, [{f"in_{name}": arrays[name] for name in _INS}], core_ids=[0])
    return r.results[0]["out"]
```
